# Optimizing a Trainium2 kernel written in Bass

```python
import numpy as np
import jax
import jax.numpy as jnp

def _softmax(x, axis=-1):
    return jax.nn.softmax(x, axis=axis)

def _gelu(x):
    return jax.nn.gelu(x, approximate=True)

def _silu(x):
    return jax.nn.silu(x)

def _sigmoid(x):
    return jax.nn.sigmoid(x)

def _layernorm(x, axis=-1, eps=1e-05):
    m = jnp.mean(x, axis=axis, keepdims=True)
    v = jnp.var(x, axis=axis, keepdims=True)
    return (x - m) / jnp.sqrt(v + eps)

def _scatter_add(tgt, idx, src, axis=0):
    return tgt.at[idx].add(src)

def _segment_sum(src, seg, n):
    return jax.ops.segment_sum(src, seg, n)
kernel_name = 'mk_decoder_postln_d1_seqx_r8_8415dc'

def setup_inputs(seed: int=0):
    np.random.seed(seed)
    _w = jnp.asarray

    def _rec_inputs():
        import jax
        import jax.numpy as jnp
        _rk = jax.random.key(seed)
        x = 7.22e-05 + 1 * jax.random.normal(jax.random.fold_in(_rk, 1), (8, 128, 512), jnp.float32)
        _lenS = 128 - jax.random.randint(jax.random.fold_in(_rk, 7), (8,), 0, max(1, 128 // 4) + 1, jnp.int32)
        _lenS2 = 128 - jax.random.randint(jax.random.fold_in(_rk, 8), (8,), 0, max(1, 128 // 4) + 1, jnp.int32)
        _ctx_4096P = jax.random.normal(jax.random.fold_in(_rk, 11), (8, 16, 512), jnp.float32)
        _ctx_4096c = jax.random.dirichlet(jax.random.fold_in(_rk, 511), 0.3 * jnp.ones((16,), jnp.float32), (8, 128))
        _ctx_4096t = jnp.einsum('bsk,bkd->bsd', _ctx_4096c, _ctx_4096P)
        _ctx_4096t = _ctx_4096t * jax.lax.rsqrt(jnp.mean(jnp.square(_ctx_4096t)) + 1e-12) * 0.953939
        ctx_4096 = 4.13588e-05 + 0.999923 * (_ctx_4096t + 0.3 * jax.random.normal(jax.random.fold_in(_rk, 611), (8, 128, 512), jnp.float32))
        _validS = jnp.arange(128)[None, :] < _lenS[:, None]
        _validS2 = jnp.arange(128)[None, :] < _lenS2[:, None]
        _causal = jnp.tril(jnp.ones((128, 128), dtype=bool))
        mask_BxSxS2_bk0 = jnp.logical_not(jnp.broadcast_to(_validS2[:, None, :], (8, 128, 128)))
        return (x, ctx_4096, mask_BxSxS2_bk0)
    x, ctx_4096, mask_BxSxS2_bk0 = _rec_inputs()

    def _L0_attn_setup():
        import jax, jax.numpy as jnp
        import numpy as np
        B, T, H, S, F, G = (2, 256, 512, 128, 1248, 6)
        GRAD_ORDER_MIN = 4
        THD = 2.5
        key = jax.random.key(seed)
        ks = jax.random.split(key, 9)
        sc = 0.02
        hidden_states = jax.random.normal(ks[0], (B, T, H), jnp.float32)
        up_w = jax.random.normal(ks[1], (S, H), jnp.float32) * sc
        gate_w = jax.random.normal(ks[2], (S, H), jnp.float32) / np.sqrt(H)
        local_point = jax.random.normal(ks[3], (S,), jnp.float32)
        local_approx_output = jax.random.normal(ks[4], (H, S), jnp.float32) * sc
        fuse_weight = jax.random.normal(ks[5], (H, S, G), jnp.float32) * sc
        discount_factor = jnp.asarray(np.cumsum(np.log(np.arange(1, G + 1, dtype=np.float64))), jnp.float32)
        ffn_gate_w = jax.random.normal(ks[6], (F, H), jnp.float32) * sc
        ffn_up_w = jax.random.normal(ks[7], (F, H), jnp.float32) * sc
        ffn_down_w = jax.random.normal(ks[8], (H, F), jnp.float32) * sc
        return {'hidden_states': hidden_states, 'up_w': up_w, 'gate_w': gate_w, 'local_point': local_point, 'local_approx_output': local_approx_output, 'fuse_weight': fuse_weight, 'discount_factor': discount_factor, 'ffn_gate_w': ffn_gate_w, 'ffn_up_w': ffn_up_w, 'ffn_down_w': ffn_down_w}
    _L0_attn_all = _L0_attn_setup()
    _L0_attn_in = {k: v for k, v in _L0_attn_all.items() if k in ('up_w', 'gate_w', 'local_point', 'local_approx_output', 'fuse_weight', 'discount_factor', 'ffn_gate_w', 'ffn_up_w', 'ffn_down_w')}
    del _L0_attn_all

    def _L0_xattn_setup():
        import jax, jax.numpy as jnp
        import numpy as np
        B, LQ, LK, D, H, DH = (2, 128, 128, 512, 32, 128)
        EPS = 1e-05

        def _rmsnorm(x, weight):
            var = jnp.mean(jnp.square(x), axis=-1, keepdims=True)
            return x * jax.lax.rsqrt(var + EPS) * weight
        key = jax.random.key(seed)
        ks = jax.random.split(key, 8)
        scale = 0.02
        return {'hidden_states': jax.random.normal(ks[0], (B, LQ, D), jnp.float32), 'key_value_states': jax.random.normal(ks[1], (B, LK, D), jnp.float32), 'attention_mask': jax.random.randint(ks[2], (B, LQ, LK), 0, 2) > 0, 'position_bias': jax.random.normal(ks[3], (H, LQ, LK), jnp.float32), 'ln_weight': jnp.ones((D,), jnp.float32), 'w_q': jax.random.normal(ks[4], (H * DH, D), jnp.float32) * scale, 'w_k': jax.random.normal(ks[5], (H * DH, D), jnp.float32) * scale, 'w_v': jax.random.normal(ks[6], (H * DH, D), jnp.float32) * scale, 'w_out': jax.random.normal(ks[7], (D, H * DH), jnp.float32) * scale}
    _L0_xattn_all = _L0_xattn_setup()
    _L0_xattn_in = {k: v for k, v in _L0_xattn_all.items() if k in ('position_bias', 'ln_weight', 'w_q', 'w_k', 'w_v', 'w_out')}
    del _L0_xattn_all

    def _L0_ffn_setup():
        import jax, jax.numpy as jnp
        import numpy as np
        HIDDEN = 512
        INTER = 1376
        SPARSITY = 0.5

        def _ternary_weight(key, out_dim, in_dim, sparsity):
            k_mask, k_sign = jax.random.split(key)
            nonzero = jax.random.bernoulli(k_mask, 1.0 - sparsity, (out_dim, in_dim))
            sign = jnp.where(jax.random.bernoulli(k_sign, 0.5, (out_dim, in_dim)), 1.0, -1.0)
            return (nonzero * sign).astype(jnp.float32)
        key = jax.random.key(seed)
        kx, kg, ku, kd, ksg, ksu, ksd = jax.random.split(key, 7)
        x = jax.random.normal(kx, (4, 256, HIDDEN), dtype=jnp.float32)
        Wg = _ternary_weight(kg, INTER, HIDDEN, SPARSITY)
        Wu = _ternary_weight(ku, INTER, HIDDEN, SPARSITY)
        Wd = _ternary_weight(kd, HIDDEN, INTER, SPARSITY)
        ag = jax.random.uniform(ksg, (INTER,), dtype=jnp.float32, minval=0.5, maxval=1.5) / np.sqrt(HIDDEN)
        au = jax.random.uniform(ksu, (INTER,), dtype=jnp.float32, minval=0.5, maxval=1.5) / np.sqrt(HIDDEN)
        ad = jax.random.uniform(ksd, (HIDDEN,), dtype=jnp.float32, minval=0.5, maxval=1.5) / np.sqrt(INTER)
        return {'x': x, 'Wg': Wg, 'Wu': Wu, 'Wd': Wd, 'ag': ag, 'au': au, 'ad': ad}
    _L0_ffn_all = _L0_ffn_setup()
    _L0_ffn_in = {k: v for k, v in _L0_ffn_all.items() if k in ('Wg', 'Wu', 'Wd', 'ag', 'au', 'ad')}
    del _L0_ffn_all
    return {'x': x, 'ctx_4096': ctx_4096, 'mask_BxSxS2_bk0': mask_BxSxS2_bk0, 'L0_attn_up_w': _L0_attn_in['up_w'], 'L0_attn_gate_w': _L0_attn_in['gate_w'], 'L0_attn_local_point': _L0_attn_in['local_point'], 'L0_attn_local_approx_output': _L0_attn_in['local_approx_output'], 'L0_attn_fuse_weight': _L0_attn_in['fuse_weight'], 'L0_attn_discount_factor': _L0_attn_in['discount_factor'], 'L0_attn_ffn_gate_w': _L0_attn_in['ffn_gate_w'], 'L0_attn_ffn_up_w': _L0_attn_in['ffn_up_w'], 'L0_attn_ffn_down_w': _L0_attn_in['ffn_down_w'], 'L0_xattn_position_bias': _L0_xattn_in['position_bias'], 'L0_xattn_ln_weight': _L0_xattn_in['ln_weight'], 'L0_xattn_w_q': _L0_xattn_in['w_q'], 'L0_xattn_w_k': _L0_xattn_in['w_k'], 'L0_xattn_w_v': _L0_xattn_in['w_v'], 'L0_xattn_w_out': _L0_xattn_in['w_out'], 'L0_ffn_Wg': _L0_ffn_in['Wg'], 'L0_ffn_Wu': _L0_ffn_in['Wu'], 'L0_ffn_Wd': _L0_ffn_in['Wd'], 'L0_ffn_ag': _L0_ffn_in['ag'], 'L0_ffn_au': _L0_ffn_in['au'], 'L0_ffn_ad': _L0_ffn_in['ad']}

def reference(x, ctx_4096, mask_BxSxS2_bk0, L0_attn_up_w, L0_attn_gate_w, L0_attn_local_point, L0_attn_local_approx_output, L0_attn_fuse_weight, L0_attn_discount_factor, L0_attn_ffn_gate_w, L0_attn_ffn_up_w, L0_attn_ffn_down_w, L0_xattn_position_bias, L0_xattn_ln_weight, L0_xattn_w_q, L0_xattn_w_k, L0_xattn_w_v, L0_xattn_w_out, L0_ffn_Wg, L0_ffn_Wu, L0_ffn_Wd, L0_ffn_ag, L0_ffn_au, L0_ffn_ad):
    import jax
    import jax.numpy as jnp

    def _L0_attn_ref(hidden_states, up_w, gate_w, local_point, local_approx_output, fuse_weight, discount_factor, ffn_gate_w, ffn_up_w, ffn_down_w):
        import jax, jax.numpy as jnp
        import numpy as np
        B, T, H, S, F, G = (2, 256, 512, 128, 1248, 6)
        GRAD_ORDER_MIN = 4
        THD = 2.5
        approx_up = hidden_states @ up_w.T
        gate_pre = hidden_states @ gate_w.T
        delta = gate_pre - local_point
        neg_factor = jnp.where(delta > 0, 1.0, -1.0).astype(hidden_states.dtype)
        delta_abs = jnp.abs(delta)
        log_delta = jnp.log(delta_abs)
        keep = (delta_abs <= THD).astype(hidden_states.dtype)
        approx_out = approx_up @ local_approx_output.T
        for idx in range(G):
            m = idx + 1
            dterm = jnp.exp(log_delta * m - discount_factor[idx])
            if m % 2 == 1:
                dterm = dterm * neg_factor
            tmp = dterm * approx_up
            if m > GRAD_ORDER_MIN:
                tmp = tmp * keep
            approx_out = approx_out + tmp @ fuse_weight[:, :, idx].T
        ffn_out = jax.nn.silu(hidden_states @ ffn_gate_w.T) * (hidden_states @ ffn_up_w.T) @ ffn_down_w.T
        return approx_out + ffn_out

    def _L0_xattn_ref(hidden_states, key_value_states, attention_mask, position_bias, ln_weight, w_q, w_k, w_v, w_out):
        import jax, jax.numpy as jnp
        import numpy as np
        B, LQ, LK, D, H, DH = (2, 128, 128, 512, 32, 128)
        EPS = 1e-05

        def _rmsnorm(x, weight):
            var = jnp.mean(jnp.square(x), axis=-1, keepdims=True)
            return x * jax.lax.rsqrt(var + EPS) * weight
        x = _rmsnorm(hidden_states, ln_weight)
        b, lq, _ = x.shape
        lk = key_value_states.shape[1]
        h_q = (x @ w_q.T).reshape(b, lq, H, DH)
        h_k = (key_value_states @ w_k.T).reshape(b, lk, H, DH)
        h_v = (key_value_states @ w_v.T).reshape(b, lk, H, DH)
        score = jnp.einsum('bqhd,bkhd->bhqk', h_q, h_k)
        score = score + position_bias[None]
        m = attention_mask[:, None]
        score = jnp.where(m, score, -jnp.inf)
        score = jax.nn.softmax(score, axis=-1)
        score = jnp.where(m, score, 0.0)
        attn = jnp.einsum('bhqk,bkhd->bqhd', score, h_v).reshape(b, lq, H * DH)
        out = attn @ w_out.T
        return hidden_states + out

    def _L0_ffn_ref(x, Wg, Wu, Wd, ag, au, ad):
        import jax, jax.numpy as jnp
        import numpy as np
        HIDDEN = 512
        INTER = 1376
        SPARSITY = 0.5

        def _ternary_weight(key, out_dim, in_dim, sparsity):
            k_mask, k_sign = jax.random.split(key)
            nonzero = jax.random.bernoulli(k_mask, 1.0 - sparsity, (out_dim, in_dim))
            sign = jnp.where(jax.random.bernoulli(k_sign, 0.5, (out_dim, in_dim)), 1.0, -1.0)
            return (nonzero * sign).astype(jnp.float32)
        gate = jnp.einsum('bsh,ih->bsi', x, Wg) * ag
        up = jnp.einsum('bsh,ih->bsi', x, Wu) * au
        h = jax.nn.silu(gate) * up
        out = jnp.einsum('bsi,hi->bsh', h, Wd) * ad
        return out
    x = _layernorm(x + _L0_attn_ref(x, L0_attn_up_w, L0_attn_gate_w, L0_attn_local_point, L0_attn_local_approx_output, L0_attn_fuse_weight, L0_attn_discount_factor, L0_attn_ffn_gate_w, L0_attn_ffn_up_w, L0_attn_ffn_down_w), axis=-1)
    x = _layernorm(x + _L0_xattn_ref(x, ctx_4096, mask_BxSxS2_bk0, L0_xattn_position_bias, L0_xattn_ln_weight, L0_xattn_w_q, L0_xattn_w_k, L0_xattn_w_v, L0_xattn_w_out), axis=-1)
    x = _layernorm(x + _L0_ffn_ref(x, L0_ffn_Wg, L0_ffn_Wu, L0_ffn_Wd, L0_ffn_ag, L0_ffn_au, L0_ffn_ad), axis=-1)
    return x

_drawn_inputs = setup_inputs


def setup_inputs(seed=0):
    import zlib

    import numpy as np

    out = dict(_drawn_inputs(seed))
    spreads = {'L0_xattn_ln_weight': (1.0, 0.2)}
    factors = {}
    for name, (base, spread) in spreads.items():
        noise = np.random.default_rng([zlib.crc32(name.encode()), seed]).standard_normal(out[name].shape)
        drawn = base * np.exp(spread * noise) if base else spread * noise
        out[name] = jnp.asarray(drawn.astype(out[name].dtype))
    for name, factor in factors.items():
        out[name] = (out[name] * factor).astype(out[name].dtype)
    return out
```

```python
from contextlib import ExitStack

import concourse.bass as bass
from concourse import mybir

P = 128
F32 = mybir.dt.float32
F32R = mybir.dt.float32r
U8 = mybir.dt.uint8
U32 = mybir.dt.uint32
ALU = mybir.AluOpType
ACT = mybir.ActivationFunctionType
AX_X = mybir.AxisListType.X

BATCH, SEQ, D = 8, 128, 512
HALVES = 2
HB = BATCH // HALVES
N = HB * SEQ
C = D // P
TT = N // P
HEADS = 32
GH = 4
GROUPS = HEADS // GH
ORDERS = 6
POLY = ORDERS + 1
KEEP_ORDER = 4
THD = 2.5
F1 = -(-1248 // P)
F3 = -(-1376 // P)
LN_EPS = 1e-5
RMS_EPS = 1e-5
MASKED = 1e30

A1, T1 = 1 + F1, POLY + F1
AX0, TX0 = HALVES * A1, HALVES * T1
A30, T30 = AX0 + HALVES * HEADS, TX0 + HALVES * HEADS
POLY_STEPS = 3 + ORDERS
STAGE_V = 4
LAST_A, LAST_T = A30 + HALVES * F3 - 1, T30 + HALVES * F3 - 1
HN = HALVES * HEADS
PART_END = [T1 - 1, TX0 - 1, TX0 + HEADS - 1, T30 - 1, T30 + F3 - 1, LAST_T]

COL_POINT, COL_LNW, COL_DISC = 0, 1, 1 + C
COL_AG = COL_DISC + ORDERS
COL_AU = COL_AG + F3
COLS = COL_AU + F3

PEEL1, PEEL3 = 3, 4
LOOP1, LOOP3 = (F1 - 1 - PEEL1) // 2, (F3 - 1 - PEEL3) // 2


def decoder_kernel(nc, xT, ctxT, x_tok, mask, consts, ad, a1, b1, ax, bx, wv, bias, a3, b3, out):
    with ExitStack() as ctx:
        def sb(name, shape, dt=F32):
            return ctx.enter_context(nc.sbuf_tensor(name, shape, dt))

        def two(name, shape, dt=F32):
            return [sb(f"{name}{i}", shape, dt) for i in range(2)]

        def sem(name):
            return ctx.enter_context(nc.semaphore(name))

        a_raw, a_hi, a_lo = two("a_raw", [P, 2 * C * P]), two("a_hi", [P, 2, C, P], F32R), two("a_lo", [P, 2, C, P], F32R)
        b_raw, b_hi, b_lo = two("b_raw", [P, D]), two("b_hi", [P, D], F32R), two("b_lo", [P, D], F32R)
        stage = sb("stage", [P, C * N])
        wv_hi, wv_lo = sb("wv_hi", [P, C, GH * P], F32R), sb("wv_lo", [P, C, GH * P], F32R)
        feat_hi, feat_lo = two("feat_hi", [P, C, N], F32R), two("feat_lo", [P, C, N], F32R)
        ctx_hi, ctx_lo = two("ctx_hi", [P, C, N], F32R), two("ctx_lo", [P, C, N], F32R)
        tile_hi, tile_lo = two("tile_hi", [P, N], F32R), two("tile_lo", [P, N], F32R)
        gated = sb("gated", [P, N])
        hidden = two("hidden", [P, N])
        delta, delta_kept = sb("delta", [P, N]), sb("delta_kept", [P, N])
        ratio_log, ratio = sb("ratio_log", [P, ORDERS]), sb("ratio", [P, ORDERS])
        q_sb, k_sb = sb("q_sb", [P, N]), sb("k_sb", [P, N])
        v_sb = two("v_sb", [P, HB, GH * P])
        score, prob = sb("score", [P, HB, P]), sb("prob", [P, HB, P])
        prob_t = sb("prob_t", [P, HB * P])
        bias_sb = two("bias_sb", [P, GH * P])
        mask_words = sb("mask_words", [P, BATCH, SEQ // 4], U32)
        mask_u8 = mask_words[:].bitcast(U8)
        mask_add = sb("mask_add", [P, BATCH, P])
        row_valid = sb("row_valid", [P, BATCH])
        row_max, neg_max = sb("row_max", [P, HB]), sb("neg_max", [P, HB])
        row_sum, row_inv = sb("row_sum", [P, HB]), sb("row_inv", [P, HB])
        resid = sb("resid", [P, HALVES * TT, D])
        normed = sb("normed", [P, TT, D])
        ad_sb = sb("ad_sb", [P, D])
        const = sb("const", [P, COLS])
        stats = sb("stats", [P, TT, 6])
        moments = sb("moments", [P, TT, 2])
        square = sb("square", [P, TT])
        deviation, scale = sb("deviation", [P, TT]), sb("scale", [P, TT])
        eps = sb("eps", [P, 1])
        ident = sb("ident", [P, P])

        bank = [ctx.enter_context(nc.psum_tensor(f"bank{i}", [P, 512], F32)) for i in range(4)]
        acc = [ctx.enter_context(nc.psum_tensor(f"acc{t}", [P, D], F32)) for t in range(TT)]

        a_dma, b_dma = [sem("a_dma0"), sem("a_dma1")], [sem("b_dma0"), sem("b_dma1")]
        gate_dma = sem("gate_dma")
        chunk_dma = [sem(f"chunk_dma{c}") for c in range(C)]
        stage_dma = sem("stage_dma")
        bias_dma = [sem("bias_dma0"), sem("bias_dma1")]
        const_dma, mask_dma, resid_dma, out_dma = sem("const_dma"), sem("mask_dma"), sem("resid_dma"), sem("out_dma")
        a_hi_ok, a_lo_ok, b_hi_ok, b_lo_ok = sem("a_hi_ok"), sem("a_lo_ok"), sem("b_hi_ok"), sem("b_lo_ok")
        stage_hi_ok, stage_lo_ok = sem("stage_hi_ok"), sem("stage_lo_ok")
        tile_hi_ok, tile_lo_ok = sem("tile_hi_ok"), sem("tile_lo_ok")
        feat_hi_ok, feat_lo_ok = sem("feat_hi_ok"), sem("feat_lo_ok")
        first_mm = sem("first_mm")
        a_used = sem("a_used")
        b_used = sem("b_used")
        score_mm, prob_t_mm, pv_mm, v_mm = sem("score_mm"), sem("prob_t_mm"), sem("pv_mm"), sem("v_mm")
        feat_mm = sem("feat_mm")
        acc_full = sem("acc_full")
        silu_ok, hidden_ok = sem("silu_ok"), sem("hidden_ok")
        poly_ok, ratio_in, ratio_ok = sem("poly_ok"), sem("ratio_in"), sem("ratio_ok")
        q_ok, k_ok, v_ok = sem("q_ok"), sem("k_ok"), sem("v_ok")
        biased_ok, masked_ok, neg_max_ok, exp_ok = sem("biased_ok"), sem("masked_ok"), sem("neg_max_ok"), sem("exp_ok")
        inv_ok, prob_ok, prob_t_ok = sem("inv_ok"), sem("prob_ok"), sem("prob_t_ok")
        mask_ok = sem("mask_ok")
        acc_read, acc_sum, moments_ok, dev_ok = sem("acc_read"), sem("acc_sum"), sem("moments_ok"), sem("dev_ok")
        ln_step, operand_ok, part_ok = sem("ln_step"), sem("operand_ok"), sem("part_ok")
        ident_set, ident_ok, eps_ok = sem("ident_set"), sem("ident_ok"), sem("eps_ok")

        block = ctx.enter_context(nc.Block())

        def staged(k):
            return C + k

        @block.sync
        def _(sp):
            def load_a(n, par, src):
                if not isinstance(n, int) or n >= 2:
                    sp.wait_ge(a_lo_ok, n)
                sp.dma_start(a_raw[par][:], src).then_inc(a_dma[par], 16)

            def load_b(m, par, src):
                if not isinstance(m, int) or m >= 2:
                    sp.wait_ge(b_lo_ok, m - 1)
                sp.dma_start(b_raw[par][:], src).then_inc(b_dma[par], 16)

            def load_bias(g, par, src):
                if not isinstance(g, int) or g >= 2:
                    sp.wait_ge(biased_ok, (g - 1) * GH)
                sp.dma_start(bias_sb[par][:], src).then_inc(bias_dma[par], 16)

            sp.dma_start(a_raw[0][:, 0:C * P], a1[0][:, 0:C * P]).then_inc(gate_dma, 16)
            for c in range(1, C):
                sp.dma_start(stage[:, c * N:(c + 1) * N], xT[0][:, c * N:(c + 1) * N]).then_inc(chunk_dma[c], 16)

            for h in range(HALVES):
                a0, t0 = h * A1, h * T1

                def load_step1(f, static_f):
                    load_a(f + (a0 + 1), (a0 + 1 + static_f) % 2, a1[f + 1])
                    load_b(f + (t0 + POLY), (t0 + POLY + static_f) % 2, b1[f + POLY])

                if h > 0:
                    load_a(a0, a0 % 2, a1[0])
                load_b(t0, t0 % 2, b1[0])
                load_a(a0 + 1, (a0 + 1) % 2, a1[1])
                load_b(t0 + 1, (t0 + 1) % 2, b1[1])
                load_a(a0 + 2, a0 % 2, a1[2])
                for m in range(2, POLY + 1):
                    load_b(t0 + m, (t0 + m) % 2, b1[m])
                load_b(t0 + POLY + 1, (t0 + POLY + 1) % 2, b1[POLY + 1])
                load_step1(2, 2)
                with sp.Fori(0, LOOP1) as i:
                    for j in range(2):
                        load_step1(i * 2 + (PEEL1 + j), PEEL1 + j)
                load_step1(F1 - 1, F1 - 1)

            load_bias(0, 0, bias[0])

            def load_group(g, gl, par, last=False):
                for j in range(GH):
                    load_a(g * GH + (AX0 + j), (AX0 + j) % 2, ax[gl * GH + j])
                    load_b(g * GH + (TX0 + j), (TX0 + j) % 2, bx[gl * GH + j])
                    if j == 1 and not last:
                        load_bias(g + 1, (par + 1) % 2, bias[0 if isinstance(gl, int) and gl == GROUPS - 1 else gl + 1])

            for h in range(HALVES):
                g0 = h * GROUPS
                load_group(g0, 0, 0)
                with sp.Fori(0, (GROUPS - 2) // 2) as i:
                    load_group(i * 2 + (g0 + 1), i * 2 + 1, 1)
                    load_group(i * 2 + (g0 + 2), i * 2 + 2, 0)
                load_group(g0 + GROUPS - 1, GROUPS - 1, 1, last=(h == HALVES - 1))

            for h in range(HALVES):
                a0, t0 = A30 + h * F3, T30 + h * F3

                def load_step3(f, static_f):
                    load_a(f + a0, (a0 + static_f) % 2, a3[f])
                    load_b(f + t0, (t0 + static_f) % 2, b3[f])

                for f in range(PEEL3):
                    load_step3(f, f)
                with sp.Fori(0, LOOP3) as i:
                    for j in range(2):
                        load_step3(i * 2 + (PEEL3 + j), PEEL3 + j)
                load_step3(F3 - 1, F3 - 1)

        @block.gpsimd
        def _(pool):
            pool.memset(ident[:], 0.0).then_inc(ident_set, 1)
            pool.wait_ge(ident_set, 1)
            pool.affine_select(out=ident[:], in_=ident[:], compare_op=ALU.not_equal, fill=1.0, base=0,
                               pattern=[[-1, P]], channel_multiplier=1).then_inc(ident_ok, 1)
            pool.dma_start(mask_words[:], mask).then_inc(mask_dma, 16)
            pool.dma_start(ad_sb[:], ad).then_inc(mask_dma, 16)

            def load_stage(k, src):
                pool.wait_ge(stage_lo_ok, k + staged(-1))
                pool.dma_start(stage[:], src).then_inc(stage_dma, 16)

            load_stage(1, xT[1])
            for h in range(HALVES):
                pool.dma_start(resid[:, h * TT:(h + 1) * TT, :], x_tok[h]).then_inc(resid_dma, 16)
            load_stage(2, ctxT[0])
            load_stage(3, ctxT[1])
            load_stage(STAGE_V, wv[0])
            for h in range(HALVES):
                with pool.Fori(0, GROUPS) as i:
                    load_stage(i + (h * GROUPS + STAGE_V + 1), wv[i + 1])
            for h in range(HALVES):
                for t in range(TT):
                    pool.wait_ge(part_ok, h * TT + t + 1)
                    pool.dma_start(out[h, t], resid[:, h * TT + t, :]).then_inc(out_dma, 16)
            pool.wait_ge(out_dma, HALVES * TT * 16)

        @block.tensor
        def _(pe):
            def passes(out_ap, w_hi, w_lo, x_hi, x_lo, start, stop):
                pe.matmul(out_ap, w_hi, x_hi, start=start, stop=False, skip_group_check=True)
                pe.matmul(out_ap, w_hi, x_lo, start=False, stop=False, skip_group_check=True)
                return pe.matmul(out_ap, w_lo, x_hi, start=False, stop=stop, skip_group_check=True)

            def project(bank_, par, which, half, x_hi=feat_hi, x_lo=feat_lo):
                for c in range(C):
                    mm = passes(bank_[:], a_hi[par][:, which, c, :], a_lo[par][:, which, c, :],
                                x_hi[half][:, c, :], x_lo[half][:, c, :], c == 0, c == C - 1)
                return mm

            def down(m, par, part, first=False, last=False):
                pe.wait_ge(b_lo_ok, m + 1)
                pe.wait_ge(tile_lo_ok, m + 1)
                for t in range(TT):
                    if first and part > 0:
                        pe.wait_ge(acc_read, (part - 1) * TT + t + 1)
                    rows = slice(t * P, (t + 1) * P)
                    mm = passes(acc[t][:], tile_hi[par][:, rows], tile_lo[par][:, rows], b_hi[par][:], b_lo[par][:],
                                first, last)
                    if last and t < TT - 1:
                        mm.then_inc(acc_full, 1)
                mm.then_inc(b_used, 1)

            def transposes(p, c, bank_, src):
                pe.wait_ge(operand_ok, (p + 1) * TT)
                for t in range(TT):
                    mm = pe.transpose(bank_[:, t * P:(t + 1) * P], src[:, t, c * P:(c + 1) * P], ident[:])
                mm.then_inc(feat_mm, 1)

            def values(bank_, b, half):
                cols = slice(b * P, (b + 1) * P)
                for c in range(C):
                    mm = passes(bank_[:], ctx_hi[half][:, c, cols], ctx_lo[half][:, c, cols],
                                wv_hi[:, c, :], wv_lo[:, c, :], c == 0, c == C - 1)
                mm.then_inc(v_mm, 1)

            def gate(a, par, half, done):
                pe.wait_ge(a_lo_ok, a + 2)
                pe.wait_ge(silu_ok, done)
                project(bank[0], par, 0, half).then_inc(first_mm, 1)

            def up(par, half, done):
                pe.wait_ge(hidden_ok, done)
                project(bank[1], par, 1, half).then_inc(a_used, 1)

            pe.wait_ge(ident_ok, 1)

            for h in range(HALVES):
                a0, t0, s0 = h * A1, h * T1, h * F1

                def step1(f, sf):
                    gate(f + (a0 + 1), (a0 + 1 + sf) % 2, h, f + s0)
                    up((a0 + 1 + sf) % 2, h, f + s0)
                    down(f + (t0 + POLY - 1), (t0 + POLY - 1 + sf) % 2, h)

                if h == 0:
                    pe.wait_ge(a_lo_ok, 1)
                    for c in range(C):
                        pe.wait_ge(stage_lo_ok, c + 1)
                        mm = passes(bank[0][:], a_hi[0][:, 0, c, :], a_lo[0][:, 0, c, :],
                                    feat_hi[0][:, c, :], feat_lo[0][:, c, :], c == 0, c == C - 1)
                    mm.then_inc(first_mm, 1)
                    pe.wait_ge(a_lo_ok, 2)
                else:
                    pe.wait_ge(a_lo_ok, a0 + 2)
                    pe.wait_ge(stage_lo_ok, staged(1))
                    pe.wait_ge(silu_ok, s0)
                    project(bank[0], a0 % 2, 0, h).then_inc(first_mm, 1)
                    pe.wait_ge(hidden_ok, s0)
                project(bank[1], a0 % 2, 1, h).then_inc(a_used, 1)
                if h > 0:
                    down(t0 - 1, (t0 - 1) % 2, h - 1, last=True)
                pe.wait_ge(a_lo_ok, a0 + 3)
                pe.wait_ge(poly_ok, h * POLY_STEPS + 1)
                project(bank[0], (a0 + 1) % 2, 0, h).then_inc(first_mm, 1)
                pe.wait_ge(poly_ok, h * POLY_STEPS + 4)
                pe.wait_ge(tile_lo_ok, t0 + 1)
                project(bank[1], (a0 + 1) % 2, 1, h).then_inc(a_used, 1)
                for m in range(POLY):
                    down(t0 + m, (t0 + m) % 2, h, first=(m == 0))
                for f in range(1, PEEL1):
                    step1(f, f)
                with pe.Fori(0, LOOP1) as i:
                    for j in range(2):
                        step1(i * 2 + (PEEL1 + j), PEEL1 + j)
                if h == 0:
                    step1(F1 - 1, F1 - 1)

            f, a, h = F1 - 1, 2 * A1 - 1, 1
            transposes(0, 0, bank[2], normed)
            gate(a, a % 2, h, s0 + f)
            transposes(0, 1, bank[3], normed)
            up(a % 2, h, s0 + f)
            pe.wait_ge(feat_lo_ok, 1)
            transposes(0, 2, bank[2], normed)
            down(TX0 - 2, (TX0 - 2) % 2, h)
            pe.wait_ge(feat_lo_ok, 2)
            transposes(0, 3, bank[3], normed)
            pe.wait_ge(stage_lo_ok, staged(STAGE_V))
            for b in range(HB):
                pe.wait_ge(feat_lo_ok, C - 1 + b % 2)
                if b >= 2:
                    pe.wait_ge(v_ok, b - 1)
                values(bank[2 + b % 2], b, 0)

            def head(g, j, gpar, half, next_half, behind=2, feature_part=None, features_done=0,
                     part=2, out_first=False, out_last=False):
                n, apar = g * GH + j, (AX0 + j) % 2
                pe.wait_ge(a_lo_ok, n + (AX0 + 2))
                if behind >= 1:
                    pe.wait_ge(biased_ok, n)
                else:
                    pe.wait_ge(silu_ok, HALVES * F1)
                project(bank[0], apar, 0, half).then_inc(first_mm, 1)
                if behind >= 2:
                    pe.wait_ge(tile_lo_ok, n + (TX0 - 1))
                elif behind == 1:
                    pe.wait_ge(k_ok, n)
                else:
                    pe.wait_ge(hidden_ok, HALVES * F1)
                project(bank[1], apar, 1, half, ctx_hi, ctx_lo).then_inc(a_used, 1)
                if behind == 0:
                    down(TX0 - 1, (TX0 - 1) % 2, 1, last=True)
                if behind >= 1:
                    if features_done:
                        pe.wait_ge(feat_lo_ok, features_done)
                    turn_probs(n, bank[2], behind)
                if next_half is not None:
                    pe.wait_ge(stage_lo_ok, g + staged(STAGE_V + 1))
                    pe.wait_ge(v_ok, n + HB)
                    values(bank[3], j, next_half)
                pe.wait_ge(q_ok, n + 1)
                pe.wait_ge(k_ok, n + 1)
                for b in range(HB):
                    cols = slice(b * SEQ, (b + 1) * SEQ)
                    mm = pe.matmul(bank[0][:, cols], q_sb[:, cols], k_sb[:, cols], start=True, stop=True)
                mm.then_inc(score_mm, 1)
                if behind >= 1:
                    weigh_values(n, j, gpar, bank[1])
                if feature_part is not None:
                    transposes(feature_part, j, bank[2], normed if feature_part < 2 else resid[:, 0:TT, :])
                if behind >= 2:
                    down(n + (TX0 - 2), (TX0 + j) % 2, part, first=out_first, last=out_last)

            def turn_probs(n, bank_, behind=2):
                pe.wait_ge(prob_ok, n)
                if behind >= 2:
                    pe.wait_ge(prob_t_ok, n - 1)
                else:
                    pe.wait_ge(v_ok, HB)
                for b in range(HB):
                    mm = pe.transpose(bank_[:, b * SEQ:(b + 1) * SEQ], prob[:, b, :], ident[:])
                mm.then_inc(prob_t_mm, 1)

            def weigh_values(n, j, gpar, bank_):
                pe.wait_ge(prob_t_ok, n)
                pe.wait_ge(v_ok, n + ((HB - j) if j else 0))
                vpar, hh = (gpar, j - 1) if j else (1 - gpar, GH - 1)
                for b in range(HB):
                    mm = pe.matmul(bank_[:, b * SEQ:(b + 1) * SEQ], v_sb[vpar][:, b, hh * P:(hh + 1) * P],
                                   prob_t[:, b * SEQ:(b + 1) * SEQ], start=True, stop=True)
                mm.then_inc(pv_mm, 1)

            pe.wait_ge(feat_lo_ok, C)
            for j in range(GH):
                head(0, j, 0, 0, 0, behind=min(j, 2), out_first=(j == 2))
            with pe.Fori(0, (GROUPS - 2) // 2) as i:
                for e in (1, 2):
                    for j in range(GH):
                        head(i * 2 + e, j, e % 2, 0, 0)
            for j in range(GH):
                head(GROUPS - 1, j, 1, 0, 1, feature_part=1, features_done=C + j)
            pe.wait_ge(feat_lo_ok, 2 * C)
            for j in range(GH):
                head(GROUPS, j, 0, 1, 1, part=2 + (j >= 2), out_first=(j == 2), out_last=(j == 1),
                     features_done=2 * C if j == 0 else 0)
            with pe.Fori(0, (GROUPS - 2) // 2) as i:
                for e in (1, 2):
                    for j in range(GH):
                        head(i * 2 + (GROUPS + e), j, e % 2, 1, 1, part=3)
            for j in range(GH):
                head(2 * GROUPS - 1, j, 1, 1, None, part=3, feature_part=2, features_done=2 * C + j)

            def step3(f, sf, h, first=False):
                a, t, done = f + (A30 + h * F3), f + (T30 + h * F3 - 1), f + (HALVES * F1 + h * F3)
                gate(a, (A30 + h * F3 + sf) % 2, h, done)
                up((A30 + h * F3 + sf) % 2, h, done)
                down(t, (T30 + h * F3 - 1 + sf) % 2, 4 + h, first=first)

            s0 = HALVES * F1
            pe.wait_ge(feat_lo_ok, 3 * C)
            pe.wait_ge(biased_ok, HN)
            gate(A30, A30 % 2, 0, s0)
            turn_probs(HN, bank[2])
            pe.wait_ge(tile_lo_ok, T30 - 1)
            up(A30 % 2, 0, s0)
            weigh_values(HN, 0, 0, bank[3])
            down(T30 - 2, T30 % 2, 3)
            gate(A30 + 1, (A30 + 1) % 2, 0, s0 + 1)
            down(T30 - 1, (T30 - 1) % 2, 3, last=True)
            up((A30 + 1) % 2, 0, s0 + 1)
            gate(A30 + 2, A30 % 2, 0, s0 + 2)
            down(T30, T30 % 2, 4, first=True)
            up(A30 % 2, 0, s0 + 2)
            down(T30 + 1, (T30 + 1) % 2, 4)
            for f in range(3, PEEL3):
                step3(f, f, 0)
            with pe.Fori(0, LOOP3) as i:
                for j in range(2):
                    step3(i * 2 + (PEEL3 + j), PEEL3 + j, 0)
            f, a = F3 - 1, A30 + F3 - 1
            x1 = resid[:, TT:2 * TT, :]
            transposes(3, 0, bank[2], x1)
            gate(a, a % 2, 0, s0 + f)
            transposes(3, 1, bank[3], x1)
            up(a % 2, 0, s0 + f)
            pe.wait_ge(feat_lo_ok, 3 * C + 1)
            transposes(3, 2, bank[2], x1)
            down(T30 + f - 1, (T30 + f - 1) % 2, 4)
            pe.wait_ge(feat_lo_ok, 3 * C + 2)
            transposes(3, 3, bank[3], x1)

            pe.wait_ge(feat_lo_ok, 4 * C)
            a, t = A30 + F3, T30 + F3
            gate(a, a % 2, 1, s0 + F3)
            up(a % 2, 1, s0 + F3)
            down(t - 1, (t - 1) % 2, 4, last=True)
            for f in range(1, PEEL3):
                step3(f, f, 1, first=(f == 1))
            with pe.Fori(0, LOOP3) as i:
                for j in range(2):
                    step3(i * 2 + (PEEL3 + j), PEEL3 + j, 1)
            step3(F3 - 1, F3 - 1, 1)
            down(LAST_T, LAST_T % 2, 5, last=True)

        @block.scalar
        def _(act):
            act.dma_start(stage[:, 0:N], xT[0][:, 0:N]).then_inc(chunk_dma[0], 16)
            act.dma_start(a_raw[0][:, C * P:], a1[0][:, C * P:]).then_inc(a_dma[0], 16)
            act.dma_start(const[:], consts).then_inc(const_dma, 16)

            def split_a(n, par):
                act.wait_ge(a_dma[par], n * 8 + (16 - 8 * par))
                if not isinstance(n, int) or n >= 2:
                    act.wait_ge(a_used, n - 1)
                act.activation(a_hi[par][:].rearrange("p w c k -> p (w c k)"), a_raw[par][:], ACT.Copy).then_inc(a_hi_ok, 1)

            def split_b(m, par):
                act.wait_ge(b_dma[par], m * 8 + (16 - 8 * par))
                if not isinstance(m, int) or m >= 2:
                    act.wait_ge(b_used, m - 1)
                act.activation(b_hi[par][:], b_raw[par][:], ACT.Copy).then_inc(b_hi_ok, 1)

            def split_stage(k, hi):
                act.wait_ge(stage_dma, k * 16)
                act.activation(hi[:].rearrange("p c n -> p (c n)"), stage[:], ACT.Copy).then_inc(stage_hi_ok, 1)

            def tile_from(m, par, src):
                if not isinstance(m, int) or m >= 2:
                    act.wait_ge(b_used, m - 1)
                act.activation(tile_hi[par][:], src, ACT.Copy).then_inc(tile_hi_ok, 1)

            def silu(a, done, last_block, f):
                act.wait_ge(first_mm, a + 1)
                act.wait_ge(hidden_ok, done)
                if last_block:
                    act.activation(gated[:], bank[0][:], ACT.Silu, scale=const[:, bass.ds(f + COL_AG, 1)]).then_inc(silu_ok, 1)
                else:
                    act.activation(gated[:], bank[0][:], ACT.Silu).then_inc(silu_ok, 1)

            def feed(a, apar, m, mpar, done, last_block=False, f=0, split_next=True):
                silu(a, done, last_block, f)
                if split_next:
                    split_a(a + 1, 1 - apar)
                split_b(m, mpar)
                act.wait_ge(hidden_ok, done + 1)
                tile_from(m, mpar, hidden[mpar][:])

            def chunk(p, c, bank_):
                act.wait_ge(feat_mm, p * C + c + 1)
                if p < 2:
                    act.activation(feat_hi[p % 2][:, c, :], bank_[:], ACT.Copy,
                                   scale=const[:, COL_LNW + c:COL_LNW + c + 1]).then_inc(feat_hi_ok, 1)
                else:
                    act.activation(feat_hi[p % 2][:, c, :], bank_[:], ACT.Copy).then_inc(feat_hi_ok, 1)

            def root(k, src):
                act.wait_ge(moments_ok, k + 1)
                act.activation(deviation[:], src, ACT.Sqrt, bias=eps[:, 0:1]).then_inc(dev_ok, 1)

            variance = moments[:, :, 1]

            def copy_values(count, bank_, vpar, b):
                act.wait_ge(v_mm, count)
                act.activation(v_sb[vpar][:, b, :], bank_[:], ACT.Copy).then_inc(v_ok, 1)

            def split_half_a(which):
                act.activation(a_hi[0][:, which].rearrange("p c k -> p (c k)"), a_raw[0][:, which * C * P:(which + 1) * C * P],
                               ACT.Copy).then_inc(a_hi_ok, 1)

            act.wait_ge(gate_dma, 16)
            split_half_a(0)
            for c in range(C):
                act.wait_ge(chunk_dma[c], 16)
                act.activation(feat_hi[0][:, c, :], stage[:, c * N:(c + 1) * N], ACT.Copy).then_inc(stage_hi_ok, 1)
            act.wait_ge(a_dma[0], 16)
            split_half_a(1)
            act.wait_ge(ratio_in, 1)
            act.activation(ratio[:], ratio_log[:], ACT.Exp).then_inc(ratio_ok, 1)

            for h in range(HALVES):
                a0, t0, s0 = h * A1, h * T1, h * F1

                def step1(f, sf, split_next=True):
                    feed(f + (a0 + 1), (a0 + 1 + sf) % 2, f + (t0 + POLY), (t0 + POLY + sf) % 2, f + s0)

                split_a(a0 + 1, (a0 + 1) % 2)
                act.wait_ge(a_used, a0 + 1)
                tile_from(t0, t0 % 2, bank[1][:])
                split_b(t0, t0 % 2)
                silu(a0 + 1, s0, False, 0)
                split_a(a0 + 2, a0 % 2)
                for m in range(1, POLY):
                    split_b(t0 + m, (t0 + m) % 2)
                    act.wait_ge(poly_ok, h * POLY_STEPS + 3 + m)
                    tile_from(t0 + m, (t0 + m) % 2, hidden[(t0 + m) % 2][:])
                split_b(t0 + POLY, (t0 + POLY) % 2)
                act.wait_ge(hidden_ok, s0 + 1)
                tile_from(t0 + POLY, (t0 + POLY) % 2, hidden[(t0 + POLY) % 2][:])
                step1(1, 1)
                if h == 0:
                    split_stage(1, feat_hi[1])
                else:
                    root(0, variance)
                step1(2, 2)
                if h > 0:
                    root(1, square[:])
                    split_stage(STAGE_V, wv_hi)
                with act.Fori(0, LOOP1) as i:
                    for j in range(2):
                        step1(i * 2 + (PEEL1 + j), PEEL1 + j)
                if h == 0:
                    split_stage(2, ctx_hi[0])
                    step1(F1 - 1, F1 - 1)
                    split_stage(3, ctx_hi[1])
            a, m, done = 2 * A1 - 1, TX0 - 1, HALVES * F1 - 1
            chunk(0, 0, bank[2])
            silu(a, done, False, 0)
            chunk(0, 1, bank[3])
            split_a(a + 1, (a + 1) % 2)
            chunk(0, 2, bank[2])
            split_b(m, m % 2)
            act.wait_ge(hidden_ok, done + 1)
            tile_from(m, m % 2, hidden[m % 2][:])
            chunk(0, 3, bank[3])
            for b in range(HB):
                copy_values(b + 1, bank[2 + b % 2], 0, b)

            def head(g, j, gpar, behind=2, feature_part=None, has_values=True, has_next=True, root_of=None):
                n = g * GH + j
                if behind == 0:
                    split_stage(STAGE_V + 1, wv_hi)
                act.wait_ge(first_mm, n + (AX0 + 1))
                if behind >= 1:
                    act.wait_ge(score_mm, n)
                act.activation(q_sb[:], bank[0][:], ACT.Copy).then_inc(q_ok, 1)
                split_a(n + (AX0 + 1), (AX0 + j + 1) % 2)
                if behind >= 1:
                    split_b(n + (TX0 - 1), (TX0 + j - 1) % 2)
                act.wait_ge(a_used, n + (AX0 + 1))
                act.activation(k_sb[:], bank[1][:], ACT.Copy).then_inc(k_ok, 1)
                if behind >= 1:
                    copy_probs(n, behind)
                    act.wait_ge(pv_mm, n)
                    tile_from(n + (TX0 - 1), (TX0 + j - 1) % 2, bank[1][:])
                if has_values:
                    copy_values(n + (HB + 1), bank[3], 1 - gpar, j)
                if feature_part is not None:
                    chunk(feature_part, j, bank[2])
                exponentials(n)
                if root_of is not None:
                    root(*root_of)
                if j == GH - 1 and has_next:
                    act.wait_ge(v_mm, n + (HB + 1))
                    act.wait_ge(stage_dma, g * 16 + 16 * (STAGE_V + 2))
                    act.activation(wv_hi[:].rearrange("p c n -> p (c n)"), stage[:], ACT.Copy).then_inc(stage_hi_ok, 1)

            def copy_probs(n, behind=2):
                act.wait_ge(prob_t_mm, n)
                if behind >= 2:
                    act.wait_ge(pv_mm, n - 1)
                act.activation(prob_t[:], bank[2][:], ACT.Copy).then_inc(prob_t_ok, 1)

            def exponentials(n):
                act.wait_ge(neg_max_ok, n + 1)
                if not isinstance(n, int) or n >= 1:
                    act.wait_ge(prob_t_mm, n)
                for b in range(HB):
                    e = act.activation(prob[:, b, :], score[:, b, :], ACT.Exp, bias=neg_max[:, b:b + 1],
                                       accum_out=row_sum[:, b:b + 1])
                e.then_inc(exp_ok, 1)

            for j in range(GH):
                head(0, j, 0, behind=min(j, 2), root_of={1: (2, variance), 2: (3, square[:])}.get(j))
            with act.Fori(0, (GROUPS - 2) // 2) as i:
                for e in (1, 2):
                    for j in range(GH):
                        head(i * 2 + e, j, e % 2)
            for j in range(GH):
                head(GROUPS - 1, j, 1, feature_part=1)
            for j in range(GH):
                head(GROUPS, j, 0, root_of=(4, variance) if j == 2 else None)
            with act.Fori(0, (GROUPS - 2) // 2) as i:
                for e in (1, 2):
                    for j in range(GH):
                        head(i * 2 + (GROUPS + e), j, e % 2)
            for j in range(GH):
                head(2 * GROUPS - 1, j, 1, feature_part=2, has_values=False, has_next=False)

            s0 = HALVES * F1

            def step3(f, sf, h, split_next=True):
                feed(f + (A30 + h * F3), (A30 + h * F3 + sf) % 2, f + (T30 + h * F3), (T30 + h * F3 + sf) % 2,
                     f + (s0 + h * F3), last_block=True, f=f, split_next=split_next)

            silu(A30, s0, True, 0)
            split_a(A30 + 1, (A30 + 1) % 2)
            copy_probs(HN)
            split_b(T30 - 1, (T30 - 1) % 2)
            act.wait_ge(pv_mm, HN)
            tile_from(T30 - 1, (T30 - 1) % 2, bank[3][:])
            split_b(T30, T30 % 2)
            act.wait_ge(hidden_ok, s0 + 1)
            tile_from(T30, T30 % 2, hidden[T30 % 2][:])
            step3(1, 1, 0)
            step3(2, 2, 0)
            root(5, variance)
            for f in range(3, PEEL3):
                step3(f, f, 0)
            with act.Fori(0, LOOP3) as i:
                for j in range(2):
                    step3(i * 2 + (PEEL3 + j), PEEL3 + j, 0)
            a, m, f = A30 + F3 - 1, T30 + F3 - 1, F3 - 1
            chunk(3, 0, bank[2])
            silu(a, s0 + f, True, f)
            chunk(3, 1, bank[3])
            split_a(a + 1, (a + 1) % 2)
            chunk(3, 2, bank[2])
            split_b(m, m % 2)
            act.wait_ge(hidden_ok, s0 + f + 1)
            tile_from(m, m % 2, hidden[m % 2][:])
            chunk(3, 3, bank[3])
            step3(0, 0, 1)
            step3(1, 1, 1)
            root(6, variance)
            for f in range(2, PEEL3):
                step3(f, f, 1)
            with act.Fori(0, LOOP3) as i:
                for j in range(2):
                    step3(i * 2 + (PEEL3 + j), PEEL3 + j, 1)
            step3(F3 - 1, F3 - 1, 1, split_next=False)
            root(7, variance)

        @block.vector
        def _(dve):
            def low(out_ap, whole, high):
                return dve.tensor_tensor(out_ap, whole, high, ALU.subtract)

            def split_a(n, par):
                dve.wait_ge(a_hi_ok, n + 2)
                low(a_lo[par][:].rearrange("p w c k -> p (w c k)"), a_raw[par][:],
                    a_hi[par][:].rearrange("p w c k -> p (w c k)").bitcast(F32)).then_inc(a_lo_ok, 1)

            def split_b(m, par):
                dve.wait_ge(b_hi_ok, m + 1)
                low(b_lo[par][:], b_raw[par][:], b_hi[par][:].bitcast(F32)).then_inc(b_lo_ok, 1)

            def split_stage(k, hi, lo):
                dve.wait_ge(stage_hi_ok, k + C)
                low(lo[:].rearrange("p c n -> p (c n)"), stage[:],
                    hi[:].rearrange("p c n -> p (c n)").bitcast(F32)).then_inc(stage_lo_ok, 1)

            def tile_rest(m, par, src):
                dve.wait_ge(tile_hi_ok, m + 1)
                low(tile_lo[par][:], src, tile_hi[par][:].bitcast(F32)).then_inc(tile_lo_ok, 1)

            def product(a, done, m, mpar, last_block, f):
                dve.wait_ge(silu_ok, done + 1)
                dve.wait_ge(a_used, a + 1)
                dve.wait_ge(tile_lo_ok, m - 1)
                if last_block:
                    dve.scalar_tensor_tensor(out=hidden[mpar][:], in0=bank[1][:], scalar=const[:, bass.ds(f + COL_AU, 1)],
                                             in1=gated[:], op0=ALU.mult, op1=ALU.mult).then_inc(hidden_ok, 1)
                else:
                    dve.tensor_tensor(hidden[mpar][:], bank[1][:], gated[:], ALU.mult).then_inc(hidden_ok, 1)

            def feed(a, apar, m, mpar, done, last_block=False, f=0, split_next=True, before=None):
                if split_next:
                    split_a(a + 1, 1 - apar)
                if before is not None:
                    before()
                product(a, done, m, mpar, last_block, f)
                split_b(m, mpar)
                dve.wait_ge(hidden_ok, done + 1)
                tile_rest(m, mpar, hidden[mpar][:])

            def chunk(p, c, bank_):
                dve.wait_ge(feat_hi_ok, p * C + c + 1)
                high = feat_hi[p % 2][:, c, :].bitcast(F32)
                if p < 2:
                    dve.scalar_tensor_tensor(out=feat_lo[p % 2][:, c, :], in0=bank_[:], scalar=const[:, COL_LNW + c:COL_LNW + c + 1],
                                             in1=high, op0=ALU.mult, op1=ALU.subtract).then_inc(feat_lo_ok, 1)
                else:
                    low(feat_lo[p % 2][:, c, :], bank_[:], high).then_inc(feat_lo_ok, 1)

            steps = [0]

            def step(ins):
                steps[0] += 1
                ins.then_inc(ln_step, 1)

            def after_steps():
                dve.wait_ge(ln_step, steps[0])

            def residual(p):
                for t in range(TT):
                    if t < TT - 1:
                        dve.wait_ge(acc_full, p * (TT - 1) + t + 1)
                    else:
                        dve.wait_ge(b_used, PART_END[p] + 1)
                    x = resid[:, (p % 2) * TT + t, :]
                    if p < 2:
                        dve.tensor_tensor(x, acc[t][:], x, ALU.add).then_inc(acc_read, 1)
                    elif p < 4:
                        dve.scalar_tensor_tensor(out=x, in0=x, scalar=2.0, in1=acc[t][:], op0=ALU.mult, op1=ALU.add).then_inc(acc_read, 1)
                    else:
                        dve.tensor_tensor(normed[:, t, :], acc[t][:], ad_sb[:], ALU.mult).then_inc(acc_read, 1)
                        dve.wait_ge(acc_read, p * TT + t + 1)
                        dve.tensor_tensor(x, normed[:, t, :], x, ALU.add).then_inc(acc_sum, 1)

            def take_moments(p):
                for t in range(TT):
                    step(dve.bn_stats(stats[:, t, :], resid[:, (p % 2) * TT + t, :]))
                after_steps()
                for t in range(TT):
                    step(dve.bn_aggr(moments[:, t, :], stats[:, t, :]))
                after_steps()

            def variances(p):
                dve.wait_ge(acc_read, (p + 1) * TT)
                if p >= 4:
                    dve.wait_ge(acc_sum, (p - 3) * TT)
                take_moments(p)
                dve.sem_inc(moments_ok, 1)

            def normalise(p, k, last=False):
                dve.wait_ge(dev_ok, k + 1)
                step(dve.reciprocal(scale[:], deviation[:]))
                after_steps()
                for t in range(TT):
                    x = resid[:, (p % 2) * TT + t, :]
                    ins = dve.tensor_scalar(x, x, moments[:, t, 0:1], scale[:, t:t + 1], ALU.subtract, ALU.mult)
                    if p < 2:
                        step(ins)
                    elif p < 4:
                        ins.then_inc(operand_ok, 1)
                    else:
                        ins.then_inc(part_ok, 1)
                if p < 2:
                    after_steps()
                    take_moments(p)
                    step(dve.tensor_tensor(square[:], moments[:, :, 0], moments[:, :, 0], ALU.mult))
                    after_steps()
                    dve.tensor_tensor(square[:], square[:], moments[:, :, 1], ALU.add).then_inc(moments_ok, 1)

            def rms_operand(p, k):
                dve.wait_ge(dev_ok, k + 1)
                step(dve.reciprocal(scale[:], deviation[:]))
                after_steps()
                for t in range(TT):
                    dve.tensor_scalar(normed[:, t, :], resid[:, (p % 2) * TT + t, :], scale[:, t:t + 1], None,
                                      ALU.mult).then_inc(operand_ok, 1)

            dve.memset(eps[:], LN_EPS).then_inc(eps_ok, 1)
            def split_half_a(which):
                dve.wait_ge(a_hi_ok, which + 1)
                low(a_lo[0][:, which].rearrange("p c k -> p (c k)"), a_raw[0][:, which * C * P:(which + 1) * C * P],
                    a_hi[0][:, which].rearrange("p c k -> p (c k)").bitcast(F32)).then_inc(a_lo_ok, 1)

            split_half_a(0)
            for c in range(C):
                dve.wait_ge(stage_hi_ok, c + 1)
                low(feat_lo[0][:, c, :], stage[:, c * N:(c + 1) * N], feat_hi[0][:, c, :].bitcast(F32)).then_inc(stage_lo_ok, 1)
            split_half_a(1)
            dve.wait_ge(const_dma, 16)
            dve.tensor_scalar(ratio_log[:, 0:1], const[:, COL_DISC:COL_DISC + 1], -1.0, None, ALU.mult)
            dve.tensor_tensor(ratio_log[:, 1:ORDERS], const[:, COL_DISC:COL_DISC + ORDERS - 1],
                              const[:, COL_DISC + 1:COL_DISC + ORDERS], ALU.subtract).then_inc(ratio_in, 1)

            for h in range(HALVES):
                a0, t0, s0, p0 = h * A1, h * T1, h * F1, h * POLY_STEPS

                def step1(f, sf, before=None):
                    feed(f + (a0 + 1), (a0 + 1 + sf) % 2, f + (t0 + POLY), (t0 + POLY + sf) % 2, f + s0, before=before)

                split_a(a0 + 1, (a0 + 1) % 2)
                dve.wait_ge(first_mm, a0 + 1)
                dve.tensor_scalar(delta[:], bank[0][:], const[:, COL_POINT:COL_POINT + 1], None, ALU.subtract).then_inc(poly_ok, 1)
                dve.wait_ge(poly_ok, p0 + 1)
                dve.tensor_tensor(delta_kept[:], delta[:], delta[:], ALU.mult).then_inc(poly_ok, 1)
                dve.wait_ge(poly_ok, p0 + 2)
                dve.scalar_tensor_tensor(out=delta_kept[:], in0=delta_kept[:], scalar=THD ** 2, in1=delta[:],
                                         op0=ALU.is_le, op1=ALU.mult).then_inc(poly_ok, 1)
                if h == 0:
                    dve.wait_ge(ratio_ok, 1)
                dve.wait_ge(a_used, a0 + 1)
                if h > 0:
                    dve.wait_ge(tile_lo_ok, t0)
                tile_rest(t0, t0 % 2, bank[1][:])
                dve.scalar_tensor_tensor(out=hidden[(t0 + 1) % 2][:], in0=bank[1][:], scalar=ratio[:, 0:1], in1=delta[:],
                                         op0=ALU.mult, op1=ALU.mult).then_inc(poly_ok, 1)
                split_b(t0, t0 % 2)
                split_a(a0 + 2, a0 % 2)
                if h > 0:
                    residual(0)
                for m in range(1, POLY):
                    if m + 1 < POLY:
                        dve.wait_ge(poly_ok, p0 + 3 + m)
                        dve.wait_ge(tile_lo_ok, t0 + m)
                        dve.scalar_tensor_tensor(out=hidden[(t0 + m + 1) % 2][:], in0=hidden[(t0 + m) % 2][:],
                                                 scalar=ratio[:, m:m + 1], in1=(delta if m < KEEP_ORDER else delta_kept)[:],
                                                 op0=ALU.mult, op1=ALU.mult).then_inc(poly_ok, 1)
                    split_b(t0 + m, (t0 + m) % 2)
                    tile_rest(t0 + m, (t0 + m) % 2, hidden[(t0 + m) % 2][:])
                product(a0 + 1, s0, t0 + POLY, (t0 + POLY) % 2, False, 0)
                split_b(t0 + POLY, (t0 + POLY) % 2)
                dve.wait_ge(hidden_ok, s0 + 1)
                tile_rest(t0 + POLY, (t0 + POLY) % 2, hidden[(t0 + POLY) % 2][:])
                step1(1, 1, before=(lambda: variances(0)) if h > 0 else None)
                if h == 0:
                    split_stage(1, feat_hi[1], feat_lo[1])
                step1(2, 2, before=(lambda: normalise(0, 0)) if h > 0 else None)
                if h == 0:
                    dve.wait_ge(mask_dma, 32)
                    dve.tensor_scalar(mask_add[:], mask_u8, 1.0, MASKED, ALU.subtract, ALU.mult).then_inc(mask_ok, 1)
                    dve.tensor_reduce(row_valid[:], mask_u8, AX_X, ALU.max).then_inc(mask_ok, 1)
                    dve.wait_ge(resid_dma, 32)
                else:
                    rms_operand(0, 1)
                    split_stage(STAGE_V, wv_hi, wv_lo)
                with dve.Fori(0, LOOP1) as i:
                    for j in range(2):
                        step1(i * 2 + (PEEL1 + j), PEEL1 + j)
                if h == 0:
                    split_stage(2, ctx_hi[0], ctx_lo[0])
                    step1(F1 - 1, F1 - 1)
                    split_stage(3, ctx_hi[1], ctx_lo[1])
            a, m, done = 2 * A1 - 1, TX0 - 1, HALVES * F1 - 1
            chunk(0, 0, bank[2])
            chunk(0, 1, bank[3])
            split_a(a + 1, (a + 1) % 2)
            product(a, done, m, m % 2, False, 0)
            chunk(0, 2, bank[2])
            split_b(m, m % 2)
            dve.wait_ge(hidden_ok, done + 1)
            tile_rest(m, m % 2, hidden[m % 2][:])
            chunk(0, 3, bank[3])

            def head(g, j, gpar, half, behind=2, feature_part=None, has_next=True, past_half=None, before=None):
                n = g * GH + j
                if behind == 0:
                    split_stage(STAGE_V + 1, wv_hi, wv_lo)
                if behind >= 1:
                    divide(n, half if past_half is None else past_half)
                split_a(n + (AX0 + 1), (AX0 + j + 1) % 2)
                if behind >= 1:
                    split_b(n + (TX0 - 1), (TX0 + j - 1) % 2)
                if before is not None:
                    before()
                dve.wait_ge(score_mm, n + 1)
                dve.wait_ge(bias_dma[gpar], g * 8 + (16 - 8 * gpar))
                dve.tensor_tensor(score[:], bank[0][:].rearrange("p (b k) -> p b k", b=HB),
                                  bias_sb[gpar][:, j * SEQ:(j + 1) * SEQ].unsqueeze(1).broadcast_to([P, HB, SEQ]),
                                  ALU.add).then_inc(biased_ok, 1)
                dve.wait_ge(mask_ok, 2)
                dve.wait_ge(biased_ok, n + 1)
                for b in range(HB):
                    ins = dve.tensor_tensor_reduce(score[:, b, :], score[:, b, :], mask_add[:, half * HB + b, :], 1.0, -3e38,
                                                   ALU.add, ALU.max, row_max[:, b:b + 1])
                ins.then_inc(masked_ok, 1)
                dve.wait_ge(masked_ok, n + 1)
                dve.tensor_scalar(neg_max[:], row_max[:], -1.0, None, ALU.mult).then_inc(neg_max_ok, 1)
                if behind >= 1:
                    tile_rest(n + (TX0 - 1), (TX0 + j - 1) % 2, bank[1][:])
                if feature_part is not None:
                    chunk(feature_part, j, bank[2])
                if j == GH - 1 and has_next:
                    split_stage(g + (STAGE_V + 2), wv_hi, wv_lo)

            def divide(n, half):
                dve.wait_ge(exp_ok, n)
                dve.reciprocal(row_inv[:], row_sum[:]).then_inc(inv_ok, 1)
                dve.wait_ge(inv_ok, n * 2 - 1)
                dve.tensor_tensor(row_inv[:], row_inv[:], row_valid[:, half * HB:(half + 1) * HB], ALU.mult).then_inc(inv_ok, 1)
                dve.wait_ge(inv_ok, n * 2)
                dve.tensor_tensor(prob[:], prob[:], row_inv[:].unsqueeze(2).broadcast_to([P, HB, SEQ]), ALU.mult).then_inc(prob_ok, 1)

            def add_and_measure(p):
                residual(p)
                variances(p)

            ends = {1: lambda: add_and_measure(1), 2: lambda: normalise(1, 2), 3: lambda: rms_operand(1, 3)}
            for j in range(GH):
                head(0, j, 0, 0, behind=min(j, 2), before=ends.get(j))
            with dve.Fori(0, (GROUPS - 2) // 2) as i:
                for e in (1, 2):
                    for j in range(GH):
                        head(i * 2 + e, j, e % 2, 0)
            for j in range(GH):
                head(GROUPS - 1, j, 1, 0, feature_part=1)
            ends = {2: lambda: add_and_measure(2), 3: lambda: normalise(2, 4)}
            for j in range(GH):
                head(GROUPS, j, 0, 1, past_half=(0 if j == 0 else 1), before=ends.get(j))
            with dve.Fori(0, (GROUPS - 2) // 2) as i:
                for e in (1, 2):
                    for j in range(GH):
                        head(i * 2 + (GROUPS + e), j, e % 2, 1)
            for j in range(GH):
                head(2 * GROUPS - 1, j, 1, 1, feature_part=2, has_next=False)

            s0 = HALVES * F1

            def step3(f, sf, h, split_next=True, before=None):
                feed(f + (A30 + h * F3), (A30 + h * F3 + sf) % 2, f + (T30 + h * F3), (T30 + h * F3 + sf) % 2,
                     f + (s0 + h * F3), last_block=True, f=f, split_next=split_next, before=before)

            divide(HN, 1)
            split_a(A30 + 1, (A30 + 1) % 2)
            product(A30, s0, T30, T30 % 2, True, 0)
            split_b(T30 - 1, (T30 - 1) % 2)
            tile_rest(T30 - 1, (T30 - 1) % 2, bank[3][:])
            split_b(T30, T30 % 2)
            dve.wait_ge(hidden_ok, s0 + 1)
            tile_rest(T30, T30 % 2, hidden[T30 % 2][:])
            step3(1, 1, 0)
            residual(3)
            step3(2, 2, 0, before=lambda: variances(3))
            step3(3, 3, 0, before=lambda: normalise(3, 5))
            with dve.Fori(0, LOOP3) as i:
                for j in range(2):
                    step3(i * 2 + (PEEL3 + j), PEEL3 + j, 0)
            a, m, f = A30 + F3 - 1, T30 + F3 - 1, F3 - 1
            chunk(3, 0, bank[2])
            chunk(3, 1, bank[3])
            split_a(a + 1, (a + 1) % 2)
            product(a, s0 + f, m, m % 2, True, f)
            chunk(3, 2, bank[2])
            split_b(m, m % 2)
            dve.wait_ge(hidden_ok, s0 + f + 1)
            tile_rest(m, m % 2, hidden[m % 2][:])
            chunk(3, 3, bank[3])
            step3(0, 0, 1)
            residual(4)
            step3(1, 1, 1, before=lambda: variances(4))
            step3(2, 2, 1, before=lambda: normalise(4, 6))
            step3(3, 3, 1)
            with dve.Fori(0, LOOP3) as i:
                for j in range(2):
                    step3(i * 2 + (PEEL3 + j), PEEL3 + j, 1)
            step3(F3 - 1, F3 - 1, 1, split_next=False)
            residual(5)
            variances(5)
            normalise(5, 7)


def build(nc, arrays):
    aps = {name: nc.dram_tensor(name, a.shape, mybir.dt.from_np(a.dtype), kind="ExternalInput").ap()
           for name, a in arrays.items()}
    out = nc.dram_tensor("out", (HALVES, TT, P, D), F32, kind="ExternalOutput").ap()
    decoder_kernel(nc, out=out, **aps)


def kernel(**inputs):
    import numpy as np
    import concourse.bacc as bacc
    from concourse.bass_utils import run_bass_kernel_spmd

    g = {k: np.asarray(v) for k, v in inputs.items()}

    def feature_major(x):
        return x.reshape(HALVES, N, C, P).transpose(0, 3, 2, 1).reshape(HALVES, P, C * N)

    def in_maps(w, tiles):
        w = np.concatenate([w, np.zeros((tiles * P - w.shape[0], D), w.dtype)])
        return w.reshape(tiles, P, C, P).transpose(0, 3, 2, 1).reshape(tiles, P, C * P)

    def out_maps(w, tiles):
        w = np.concatenate([w.T, np.zeros((tiles * P - w.shape[1], D), w.dtype)])
        return w.reshape(tiles, P, D)

    def columns(v, tiles):
        v = np.concatenate([v, np.zeros(tiles * P - v.shape[0], v.dtype)])
        return v.reshape(tiles, P).T

    def pair(w0, w1, tiles):
        return np.concatenate([in_maps(w0, tiles), in_maps(w1, tiles)], axis=2)

    wv = g["L0_xattn_w_v"].reshape(GROUPS, GH * P, C, P).transpose(0, 3, 2, 1).reshape(GROUPS, P, C * GH * P)
    arrays = {
        "xT": feature_major(g["x"]),
        "ctxT": feature_major(g["ctx_4096"]),
        "x_tok": g["x"].reshape(HALVES, TT, P, D).transpose(0, 2, 1, 3),
        "mask": np.ascontiguousarray(g["mask_BxSxS2_bk0"].transpose(1, 0, 2)).view(np.uint32),
        "consts": np.concatenate([
            columns(g["L0_attn_local_point"], 1), columns(g["L0_xattn_ln_weight"], C),
            np.broadcast_to(g["L0_attn_discount_factor"], (P, ORDERS)),
            columns(g["L0_ffn_ag"], F3), columns(g["L0_ffn_au"], F3)], axis=1),
        "ad": np.broadcast_to(g["L0_ffn_ad"], (P, D)),
        "a1": np.concatenate([pair(g["L0_attn_gate_w"], g["L0_attn_up_w"], 1),
                              pair(g["L0_attn_ffn_gate_w"], g["L0_attn_ffn_up_w"], F1)]),
        "b1": np.concatenate([out_maps(g["L0_attn_local_approx_output"], 1)]
                             + [out_maps(g["L0_attn_fuse_weight"][:, :, m], 1) for m in range(ORDERS)]
                             + [out_maps(g["L0_attn_ffn_down_w"], F1)]),
        "ax": pair(g["L0_xattn_w_q"], g["L0_xattn_w_k"], HEADS),
        "bx": out_maps(g["L0_xattn_w_out"], HEADS),
        "wv": np.concatenate([wv, wv[:1]]),
        "bias": g["L0_xattn_position_bias"].reshape(GROUPS, GH, SEQ, SEQ).transpose(0, 2, 1, 3).reshape(GROUPS, P, GH * SEQ),
        "a3": pair(g["L0_ffn_Wg"], g["L0_ffn_Wu"], F3),
        "b3": out_maps(g["L0_ffn_Wd"], F3),
    }
    arrays = {k: np.ascontiguousarray(v) for k, v in arrays.items()}
    nc = bacc.Bacc("TRN2", target_bir_lowering=False, num_devices=1)
    build(nc, arrays)
    r = run_bass_kernel_spmd(nc, [arrays], core_ids=[0])
    return r.results[0]["out"].reshape(BATCH, SEQ, D)
```

```python
from contextlib import ExitStack

import concourse.bass as bass
from concourse import mybir

P = 128
F32 = mybir.dt.float32
F32R = mybir.dt.float32r
U8 = mybir.dt.uint8
U32 = mybir.dt.uint32
I32 = mybir.dt.int32
ALU = mybir.AluOpType
ACT = mybir.ActivationFunctionType
AX_X = mybir.AxisListType.X

BATCH, SEQ, D = 8, 128, 512
HALVES = 2
HB = BATCH // HALVES
N = HB * SEQ
C = D // P
TT = N // P
HEADS = 32
GH = 4
GROUPS = HEADS // GH
ORDERS = 6
POLY = ORDERS + 1
KEEP_ORDER = 4
THD = 2.5
F1 = -(-1248 // P)
F3 = -(-1376 // P)
LN_EPS = 1e-5
RMS_EPS = 1e-5
MASKED = 1e30

A1, T1 = 1 + F1, POLY + F1
AX0, TX0 = HALVES * A1, HALVES * T1
A30, T30 = AX0 + HALVES * HEADS, TX0 + HALVES * HEADS
POLY_STEPS = 3 + ORDERS
STAGE_V = 4
LAST_A, LAST_T = A30 + HALVES * F3 - 1, T30 + HALVES * F3 - 1
HN = HALVES * HEADS
PART_END = [T1 - 1, TX0 - 1, TX0 + HEADS - 1, T30 - 1, T30 + F3 - 1, LAST_T]

COL_POINT, COL_LNW, COL_DISC = 0, 1, 1 + C
COL_AG = COL_DISC + ORDERS
COL_AU = COL_AG + F3
COLS = COL_AU + F3

PEEL1, PEEL3 = 3, 4
SCANS = (GROUPS - 2) * GH
SCAN = F3 * 3 * D // SCANS
assert SCAN * SCANS == F3 * 3 * D and SCAN <= 2 * N
LOW_BITS = 0xFFF
LOOP1, LOOP3 = (F1 - 1 - PEEL1) // 2, (F3 - 1 - PEEL3) // 2


def decoder_kernel(nc, xT, ctxT, x_tok, mask, consts, ad, a1, b1, ax, bx, wv, bias, w3, out):
    with ExitStack() as ctx:
        def sb(name, shape, dt=F32):
            return ctx.enter_context(nc.sbuf_tensor(name, shape, dt))

        def two(name, shape, dt=F32):
            return [sb(f"{name}{i}", shape, dt) for i in range(2)]

        def sem(name):
            return ctx.enter_context(nc.semaphore(name))

        a_raw, a_hi, a_lo = two("a_raw", [P, 2 * C * P]), two("a_hi", [P, 2, C, P], F32R), two("a_lo", [P, 2, C, P], F32R)
        b_raw, b_hi, b_lo = two("b_raw", [P, D]), two("b_hi", [P, D], F32R), two("b_lo", [P, D], F32R)
        stage = sb("stage", [P, C * N])
        wv_hi, wv_lo = sb("wv_hi", [P, C, GH * P], F32R), sb("wv_lo", [P, C, GH * P], F32R)
        feat_hi, feat_lo = two("feat_hi", [P, C, N], F32R), two("feat_lo", [P, C, N], F32R)
        ctx_hi, ctx_lo = two("ctx_hi", [P, C, N], F32R), two("ctx_lo", [P, C, N], F32R)
        tile_hi, tile_lo = two("tile_hi", [P, N], F32R), two("tile_lo", [P, N], F32R)
        gated = sb("gated", [P, N])
        pair0, pair1 = sb("pair0", [P, 2 * N]), sb("pair1", [P, 2 * N])
        hidden = [pair0[:, 0:N], pair0[:, N:]]
        delta, delta_kept = pair1[:, 0:N], pair1[:, N:]
        piece = [pair0[:, 0:SCAN].bitcast(I32), pair1[:, 0:SCAN].bitcast(I32)]
        piece_top, piece_all = sb("piece_top", [P, SCANS]), sb("piece_all", [P, 2])
        low_flag = sb("low_flag", [P, 1], I32)
        ratio_log, ratio = sb("ratio_log", [P, ORDERS]), sb("ratio", [P, ORDERS])
        q_sb, k_sb = sb("q_sb", [P, N]), sb("k_sb", [P, N])
        v_sb = two("v_sb", [P, HB, GH * P])
        score, prob = sb("score", [P, HB, P]), sb("prob", [P, HB, P])
        prob_t = sb("prob_t", [P, HB * P])
        bias_sb = two("bias_sb", [P, GH * P])
        mask_words = sb("mask_words", [P, BATCH, SEQ // 4], U32)
        mask_u8 = mask_words[:].bitcast(U8)
        mask_add = sb("mask_add", [P, BATCH, P])
        row_valid = sb("row_valid", [P, BATCH])
        row_max, neg_max = sb("row_max", [P, HB]), sb("neg_max", [P, HB])
        row_sum, row_inv = sb("row_sum", [P, HB]), sb("row_inv", [P, HB])
        resid = sb("resid", [P, HALVES * TT, D])
        normed = sb("normed", [P, TT, D])
        ad_sb = sb("ad_sb", [P, D])
        const = sb("const", [P, COLS])
        stats = sb("stats", [P, TT, 6])
        moments = sb("moments", [P, TT, 2])
        square = sb("square", [P, TT])
        deviation, scale = sb("deviation", [P, TT]), sb("scale", [P, TT])
        eps = sb("eps", [P, 1])
        ident = sb("ident", [P, P])

        bank = [ctx.enter_context(nc.psum_tensor(f"bank{i}", [P, 512], F32)) for i in range(4)]
        acc = [ctx.enter_context(nc.psum_tensor(f"acc{t}", [P, D], F32)) for t in range(TT)]

        a_dma, b_dma = [sem("a_dma0"), sem("a_dma1")], [sem("b_dma0"), sem("b_dma1")]
        gate_dma = sem("gate_dma")
        chunk_dma = [sem(f"chunk_dma{c}") for c in range(C)]
        stage_dma = sem("stage_dma")
        bias_dma = [sem("bias_dma0"), sem("bias_dma1")]
        const_dma, mask_dma, resid_dma, out_dma = sem("const_dma"), sem("mask_dma"), sem("resid_dma"), sem("out_dma")
        a_hi_ok, a_lo_ok, b_hi_ok, b_lo_ok = sem("a_hi_ok"), sem("a_lo_ok"), sem("b_hi_ok"), sem("b_lo_ok")
        stage_hi_ok, stage_lo_ok = sem("stage_hi_ok"), sem("stage_lo_ok")
        tile_hi_ok, tile_lo_ok = sem("tile_hi_ok"), sem("tile_lo_ok")
        feat_hi_ok, feat_lo_ok = sem("feat_hi_ok"), sem("feat_lo_ok")
        first_mm = sem("first_mm")
        a_used = sem("a_used")
        b_used = sem("b_used")
        score_mm, prob_t_mm, pv_mm, v_mm = sem("score_mm"), sem("prob_t_mm"), sem("pv_mm"), sem("v_mm")
        feat_mm = sem("feat_mm")
        acc_full = sem("acc_full")
        silu_ok, hidden_ok = sem("silu_ok"), sem("hidden_ok")
        poly_ok, ratio_in, ratio_ok = sem("poly_ok"), sem("ratio_in"), sem("ratio_ok")
        q_ok, k_ok, v_ok = sem("q_ok"), sem("k_ok"), sem("v_ok")
        biased_ok, masked_ok, neg_max_ok, exp_ok = sem("biased_ok"), sem("masked_ok"), sem("neg_max_ok"), sem("exp_ok")
        inv_ok, prob_ok, prob_t_ok = sem("inv_ok"), sem("prob_ok"), sem("prob_t_ok")
        mask_ok = sem("mask_ok")
        acc_read, acc_sum, moments_ok, dev_ok = sem("acc_read"), sem("acc_sum"), sem("moments_ok"), sem("dev_ok")
        ln_step, operand_ok, part_ok = sem("ln_step"), sem("operand_ok"), sem("part_ok")
        piece_dma = [sem("piece_dma0"), sem("piece_dma1")]
        piece_free, piece_bits, top_ok, all_ok, flag_ok = sem("piece_free"), sem("piece_bits"), sem("top_ok"), sem("all_ok"), sem("flag_ok")
        last_scaled, last_sum, last_stats = sem("last_scaled"), sem("last_sum"), sem("last_stats")
        last_moments, last_dev, last_scale = sem("last_moments"), sem("last_dev"), sem("last_scale")
        last_ok, last_out_dma = sem("last_ok"), sem("last_out_dma")
        ident_set, ident_ok, eps_ok = sem("ident_set"), sem("ident_ok"), sem("eps_ok")

        block = ctx.enter_context(nc.Block())

        def staged(k):
            return C + k

        @block.sync
        def _(sp):
            def load_a(n, par, src):
                if not isinstance(n, int) or n >= 2:
                    sp.wait_ge(a_lo_ok, n)
                sp.dma_start(a_raw[par][:], src).then_inc(a_dma[par], 16)

            def load_b(m, par, src):
                if not isinstance(m, int) or m >= 2:
                    sp.wait_ge(b_lo_ok, m - 1)
                sp.dma_start(b_raw[par][:], src).then_inc(b_dma[par], 16)

            def load_bias(g, par, src):
                if not isinstance(g, int) or g >= 2:
                    sp.wait_ge(biased_ok, (g - 1) * GH)
                sp.dma_start(bias_sb[par][:], src).then_inc(bias_dma[par], 16)

            sp.dma_start(a_raw[0][:, 0:C * P], a1[0][:, 0:C * P]).then_inc(gate_dma, 16)
            for c in range(1, C):
                sp.dma_start(stage[:, c * N:(c + 1) * N], xT[0][:, c * N:(c + 1) * N]).then_inc(chunk_dma[c], 16)

            for h in range(HALVES):
                a0, t0 = h * A1, h * T1

                def load_step1(f, static_f):
                    load_a(f + (a0 + 1), (a0 + 1 + static_f) % 2, a1[f + 1])
                    load_b(f + (t0 + POLY), (t0 + POLY + static_f) % 2, b1[f + POLY])

                if h > 0:
                    load_a(a0, a0 % 2, a1[0])
                load_b(t0, t0 % 2, b1[0])
                load_a(a0 + 1, (a0 + 1) % 2, a1[1])
                load_b(t0 + 1, (t0 + 1) % 2, b1[1])
                load_a(a0 + 2, a0 % 2, a1[2])
                for m in range(2, POLY + 1):
                    load_b(t0 + m, (t0 + m) % 2, b1[m])
                load_b(t0 + POLY + 1, (t0 + POLY + 1) % 2, b1[POLY + 1])
                load_step1(2, 2)
                with sp.Fori(0, LOOP1) as i:
                    for j in range(2):
                        load_step1(i * 2 + (PEEL1 + j), PEEL1 + j)
                load_step1(F1 - 1, F1 - 1)

            load_bias(0, 0, bias[0])

            pieces = w3.rearrange("f p k -> (f p k)").rearrange("(p k) -> p k", p=P)

            def load_piece(k, par):
                sp.wait_ge(piece_free, k + 1)
                sp.dma_start(pair0[:, 0:SCAN] if par == 0 else pair1[:, 0:SCAN],
                             pieces[:, bass.ds(k * SCAN, SCAN)]).then_inc(piece_dma[par], 16)

            def load_group(g, gl, par, last=False, piece0=None):
                for j in range(GH):
                    load_a(g * GH + (AX0 + j), (AX0 + j) % 2, ax[gl * GH + j])
                    load_b(g * GH + (TX0 + j), (TX0 + j) % 2, bx[gl * GH + j])
                    if piece0 is not None:
                        load_piece(piece0 + j, j % 2)
                    if j == 1 and not last:
                        load_bias(g + 1, (par + 1) % 2, bias[0 if isinstance(gl, int) and gl == GROUPS - 1 else gl + 1])

            for h in range(HALVES):
                g0 = h * GROUPS
                load_group(g0, 0, 0)
                with sp.Fori(0, (GROUPS - 2) // 2) as i:
                    for e in (1, 2):
                        load_group(i * 2 + (g0 + e), i * 2 + e, e % 2,
                                   piece0=(i * (2 * GH) + (e - 1) * GH) if h == 0 else None)
                load_group(g0 + GROUPS - 1, GROUPS - 1, 1, last=(h == HALVES - 1))

            for h in range(HALVES):
                a0, t0 = A30 + h * F3, T30 + h * F3

                def load_step3(f, static_f):
                    load_a(f + a0, (a0 + static_f) % 2, w3[f][:, 0:2 * D])
                    load_b(f + t0, (t0 + static_f) % 2, w3[f][:, 2 * D:])

                for f in range(PEEL3):
                    load_step3(f, f)
                with sp.Fori(0, LOOP3) as i:
                    for j in range(2):
                        load_step3(i * 2 + (PEEL3 + j), PEEL3 + j)
                load_step3(F3 - 1, F3 - 1)

            for t in range(TT):
                sp.wait_ge(last_ok, t + 1)
                sp.dma_start(out[1, t], resid[:, TT + t, :]).then_inc(last_out_dma, 16)
            sp.wait_ge(last_out_dma, TT * 16)

        @block.gpsimd
        def _(pool):
            pool.memset(ident[:], 0.0).then_inc(ident_set, 1)
            pool.wait_ge(ident_set, 1)
            pool.affine_select(out=ident[:], in_=ident[:], compare_op=ALU.not_equal, fill=1.0, base=0,
                               pattern=[[-1, P]], channel_multiplier=1).then_inc(ident_ok, 1)
            pool.dma_start(mask_words[:], mask).then_inc(mask_dma, 16)
            pool.dma_start(ad_sb[:], ad).then_inc(mask_dma, 16)

            def load_stage(k, src):
                pool.wait_ge(stage_lo_ok, k + staged(-1))
                pool.dma_start(stage[:], src).then_inc(stage_dma, 16)

            load_stage(1, xT[1])
            for h in range(HALVES):
                pool.dma_start(resid[:, h * TT:(h + 1) * TT, :], x_tok[h]).then_inc(resid_dma, 16)
            load_stage(2, ctxT[0])
            load_stage(3, ctxT[1])
            load_stage(STAGE_V, wv[0])
            for h in range(HALVES):
                with pool.Fori(0, GROUPS) as i:
                    load_stage(i + (h * GROUPS + STAGE_V + 1), wv[i + 1])
                if h == 0:
                    pool.wait_ge(top_ok, 1)
                    pool.partition_all_reduce(piece_all[:, 1:2], piece_all[:, 0:1], P, bass.bass_isa.ReduceOp.max).then_inc(all_ok, 1)
                    pool.wait_ge(all_ok, 1)
                    pool.tensor_copy(low_flag[:], piece_all[:, 1:2]).then_inc(flag_ok, 1)
            for t in range(TT):
                pool.wait_ge(part_ok, t + 1)
                pool.dma_start(out[0, t], resid[:, t, :]).then_inc(out_dma, 16)
            for t in range(TT):
                pool.wait_ge(last_scaled, t + 1)
                x = resid[:, TT + t, :]
                pool.tensor_tensor(x, normed[:, t, :], x, ALU.add).then_inc(last_sum, 1)
            pool.wait_ge(out_dma, TT * 16)

        @block.tensor
        def _(pe):
            def passes(out_ap, w_hi, w_lo, x_hi, x_lo, start, stop):
                products = [(w_hi, x_hi)] + [(w_hi, x_lo)] * (x_lo is not None) + [(w_lo, x_hi)] * (w_lo is not None)
                for k, (w, x) in enumerate(products):
                    mm = pe.matmul(out_ap, w, x, start=start and k == 0, stop=stop and k == len(products) - 1,
                                   skip_group_check=True)
                return mm

            def project(bank_, par, which, half, x_hi=feat_hi, x_lo=feat_lo, low=True):
                for c in range(C):
                    mm = passes(bank_[:], a_hi[par][:, which, c, :], a_lo[par][:, which, c, :] if low else None,
                                x_hi[half][:, c, :], x_lo[half][:, c, :], c == 0, c == C - 1)
                return mm

            def down(m, par, part, first=False, last=False, low=True):
                pe.wait_ge(b_lo_ok, m + 1)
                pe.wait_ge(tile_lo_ok, m + 1)
                for t in range(TT):
                    if first and part > 0:
                        pe.wait_ge(acc_read, (part - 1) * TT + t + 1)
                    rows = slice(t * P, (t + 1) * P)
                    mm = passes(acc[t][:], tile_hi[par][:, rows], tile_lo[par][:, rows], b_hi[par][:],
                                b_lo[par][:] if low else None,
                                first, last)
                    if last and t < TT - 1:
                        mm.then_inc(acc_full, 1)
                mm.then_inc(b_used, 1)

            def transposes(p, c, bank_, src):
                pe.wait_ge(operand_ok, (p + 1) * TT)
                for t in range(TT):
                    mm = pe.transpose(bank_[:, t * P:(t + 1) * P], src[:, t, c * P:(c + 1) * P], ident[:])
                mm.then_inc(feat_mm, 1)

            def values(bank_, b, half):
                cols = slice(b * P, (b + 1) * P)
                for c in range(C):
                    mm = passes(bank_[:], ctx_hi[half][:, c, cols], ctx_lo[half][:, c, cols],
                                wv_hi[:, c, :], wv_lo[:, c, :], c == 0, c == C - 1)
                mm.then_inc(v_mm, 1)

            def gate(a, par, half, done, low=True):
                pe.wait_ge(a_lo_ok, a + 2)
                pe.wait_ge(silu_ok, done)
                project(bank[0], par, 0, half, low=low).then_inc(first_mm, 1)

            def up(par, half, done, low=True):
                pe.wait_ge(hidden_ok, done)
                project(bank[1], par, 1, half, low=low).then_inc(a_used, 1)

            pe.wait_ge(ident_ok, 1)

            for h in range(HALVES):
                a0, t0, s0 = h * A1, h * T1, h * F1

                def step1(f, sf):
                    gate(f + (a0 + 1), (a0 + 1 + sf) % 2, h, f + s0)
                    up((a0 + 1 + sf) % 2, h, f + s0)
                    down(f + (t0 + POLY - 1), (t0 + POLY - 1 + sf) % 2, h)

                if h == 0:
                    pe.wait_ge(a_lo_ok, 1)
                    for c in range(C):
                        pe.wait_ge(stage_lo_ok, c + 1)
                        mm = passes(bank[0][:], a_hi[0][:, 0, c, :], a_lo[0][:, 0, c, :],
                                    feat_hi[0][:, c, :], feat_lo[0][:, c, :], c == 0, c == C - 1)
                    mm.then_inc(first_mm, 1)
                    pe.wait_ge(a_lo_ok, 2)
                else:
                    pe.wait_ge(a_lo_ok, a0 + 2)
                    pe.wait_ge(stage_lo_ok, staged(1))
                    pe.wait_ge(silu_ok, s0)
                    project(bank[0], a0 % 2, 0, h).then_inc(first_mm, 1)
                    pe.wait_ge(hidden_ok, s0)
                project(bank[1], a0 % 2, 1, h).then_inc(a_used, 1)
                if h > 0:
                    down(t0 - 1, (t0 - 1) % 2, h - 1, last=True)
                pe.wait_ge(a_lo_ok, a0 + 3)
                pe.wait_ge(poly_ok, h * POLY_STEPS + 1)
                project(bank[0], (a0 + 1) % 2, 0, h).then_inc(first_mm, 1)
                pe.wait_ge(poly_ok, h * POLY_STEPS + 4)
                pe.wait_ge(tile_lo_ok, t0 + 1)
                project(bank[1], (a0 + 1) % 2, 1, h).then_inc(a_used, 1)
                for m in range(POLY):
                    down(t0 + m, (t0 + m) % 2, h, first=(m == 0))
                for f in range(1, PEEL1):
                    step1(f, f)
                with pe.Fori(0, LOOP1) as i:
                    for j in range(2):
                        step1(i * 2 + (PEEL1 + j), PEEL1 + j)
                if h == 0:
                    step1(F1 - 1, F1 - 1)

            f, a, h = F1 - 1, 2 * A1 - 1, 1
            transposes(0, 0, bank[2], normed)
            gate(a, a % 2, h, s0 + f)
            transposes(0, 1, bank[3], normed)
            up(a % 2, h, s0 + f)
            pe.wait_ge(feat_lo_ok, 1)
            transposes(0, 2, bank[2], normed)
            down(TX0 - 2, (TX0 - 2) % 2, h)
            pe.wait_ge(feat_lo_ok, 2)
            transposes(0, 3, bank[3], normed)
            pe.wait_ge(stage_lo_ok, staged(STAGE_V))
            for b in range(HB):
                pe.wait_ge(feat_lo_ok, C - 1 + b % 2)
                if b >= 2:
                    pe.wait_ge(v_ok, b - 1)
                values(bank[2 + b % 2], b, 0)

            def head(g, j, gpar, half, next_half, behind=2, feature_part=None, features_done=0,
                     part=2, out_first=False, out_last=False):
                n, apar = g * GH + j, (AX0 + j) % 2
                pe.wait_ge(a_lo_ok, n + (AX0 + 2))
                if behind >= 1:
                    pe.wait_ge(biased_ok, n)
                else:
                    pe.wait_ge(silu_ok, HALVES * F1)
                project(bank[0], apar, 0, half).then_inc(first_mm, 1)
                if behind >= 2:
                    pe.wait_ge(tile_lo_ok, n + (TX0 - 1))
                elif behind == 1:
                    pe.wait_ge(k_ok, n)
                else:
                    pe.wait_ge(hidden_ok, HALVES * F1)
                project(bank[1], apar, 1, half, ctx_hi, ctx_lo).then_inc(a_used, 1)
                if behind == 0:
                    down(TX0 - 1, (TX0 - 1) % 2, 1, last=True)
                if behind >= 1:
                    if features_done:
                        pe.wait_ge(feat_lo_ok, features_done)
                    turn_probs(n, bank[2], behind)
                if next_half is not None:
                    pe.wait_ge(stage_lo_ok, g + staged(STAGE_V + 1))
                    pe.wait_ge(v_ok, n + HB)
                    values(bank[3], j, next_half)
                pe.wait_ge(q_ok, n + 1)
                pe.wait_ge(k_ok, n + 1)
                for b in range(HB):
                    cols = slice(b * SEQ, (b + 1) * SEQ)
                    mm = pe.matmul(bank[0][:, cols], q_sb[:, cols], k_sb[:, cols], start=True, stop=True)
                mm.then_inc(score_mm, 1)
                if behind >= 1:
                    weigh_values(n, j, gpar, bank[1])
                if feature_part is not None:
                    transposes(feature_part, j, bank[2], normed if feature_part < 2 else resid[:, 0:TT, :])
                if behind >= 2:
                    down(n + (TX0 - 2), (TX0 + j) % 2, part, first=out_first, last=out_last)

            def turn_probs(n, bank_, behind=2):
                pe.wait_ge(prob_ok, n)
                if behind >= 2:
                    pe.wait_ge(prob_t_ok, n - 1)
                else:
                    pe.wait_ge(v_ok, HB)
                for b in range(HB):
                    mm = pe.transpose(bank_[:, b * SEQ:(b + 1) * SEQ], prob[:, b, :], ident[:])
                mm.then_inc(prob_t_mm, 1)

            def weigh_values(n, j, gpar, bank_):
                pe.wait_ge(prob_t_ok, n)
                pe.wait_ge(v_ok, n + ((HB - j) if j else 0))
                vpar, hh = (gpar, j - 1) if j else (1 - gpar, GH - 1)
                for b in range(HB):
                    mm = pe.matmul(bank_[:, b * SEQ:(b + 1) * SEQ], v_sb[vpar][:, b, hh * P:(hh + 1) * P],
                                   prob_t[:, b * SEQ:(b + 1) * SEQ], start=True, stop=True)
                mm.then_inc(pv_mm, 1)

            pe.wait_ge(feat_lo_ok, C)
            for j in range(GH):
                head(0, j, 0, 0, 0, behind=min(j, 2), out_first=(j == 2))
            with pe.Fori(0, (GROUPS - 2) // 2) as i:
                for e in (1, 2):
                    for j in range(GH):
                        head(i * 2 + e, j, e % 2, 0, 0)
            for j in range(GH):
                head(GROUPS - 1, j, 1, 0, 1, feature_part=1, features_done=C + j)
            pe.wait_ge(feat_lo_ok, 2 * C)
            for j in range(GH):
                head(GROUPS, j, 0, 1, 1, part=2 + (j >= 2), out_first=(j == 2), out_last=(j == 1),
                     features_done=2 * C if j == 0 else 0)
            with pe.Fori(0, (GROUPS - 2) // 2) as i:
                for e in (1, 2):
                    for j in range(GH):
                        head(i * 2 + (GROUPS + e), j, e % 2, 1, 1, part=3)
            for j in range(GH):
                head(2 * GROUPS - 1, j, 1, 1, None, part=3, feature_part=2, features_done=2 * C + j)

            def last_block(low):
                def step3(f, sf, h, first=False):
                    a, t, done = f + (A30 + h * F3), f + (T30 + h * F3 - 1), f + (HALVES * F1 + h * F3)
                    gate(a, (A30 + h * F3 + sf) % 2, h, done, low=low)
                    up((A30 + h * F3 + sf) % 2, h, done, low=low)
                    down(t, (T30 + h * F3 - 1 + sf) % 2, 4 + h, first=first, low=low)

                s0 = HALVES * F1
                pe.wait_ge(feat_lo_ok, 3 * C)
                pe.wait_ge(biased_ok, HN)
                gate(A30, A30 % 2, 0, s0, low=low)
                turn_probs(HN, bank[2])
                pe.wait_ge(tile_lo_ok, T30 - 1)
                up(A30 % 2, 0, s0, low=low)
                weigh_values(HN, 0, 0, bank[3])
                down(T30 - 2, T30 % 2, 3)
                gate(A30 + 1, (A30 + 1) % 2, 0, s0 + 1, low=low)
                down(T30 - 1, (T30 - 1) % 2, 3, last=True)
                up((A30 + 1) % 2, 0, s0 + 1, low=low)
                gate(A30 + 2, A30 % 2, 0, s0 + 2, low=low)
                down(T30, T30 % 2, 4, first=True, low=low)
                up(A30 % 2, 0, s0 + 2, low=low)
                down(T30 + 1, (T30 + 1) % 2, 4, low=low)
                for f in range(3, PEEL3):
                    step3(f, f, 0)
                with pe.Fori(0, LOOP3) as i:
                    for j in range(2):
                        step3(i * 2 + (PEEL3 + j), PEEL3 + j, 0)
                f, a = F3 - 1, A30 + F3 - 1
                x1 = resid[:, TT:2 * TT, :]
                transposes(3, 0, bank[2], x1)
                gate(a, a % 2, 0, s0 + f, low=low)
                transposes(3, 1, bank[3], x1)
                up(a % 2, 0, s0 + f, low=low)
                pe.wait_ge(feat_lo_ok, 3 * C + 1)
                transposes(3, 2, bank[2], x1)
                down(T30 + f - 1, (T30 + f - 1) % 2, 4, low=low)
                pe.wait_ge(feat_lo_ok, 3 * C + 2)
                transposes(3, 3, bank[3], x1)

                pe.wait_ge(feat_lo_ok, 4 * C)
                a, t = A30 + F3, T30 + F3
                gate(a, a % 2, 1, s0 + F3, low=low)
                up(a % 2, 1, s0 + F3, low=low)
                down(t - 1, (t - 1) % 2, 4, last=True, low=low)
                for f in range(1, PEEL3):
                    step3(f, f, 1, first=(f == 1))
                with pe.Fori(0, LOOP3) as i:
                    for j in range(2):
                        step3(i * 2 + (PEEL3 + j), PEEL3 + j, 1)
                step3(F3 - 1, F3 - 1, 1)
                down(LAST_T, LAST_T % 2, 5, last=True, low=low)

            pe.wait_ge(flag_ok, 1)
            has_low = pe.value_load(low_flag[0:1, 0:1], min_val=0, max_val=LOW_BITS)
            with pe.If(has_low > 0):
                last_block(True)
            with pe.Else():
                last_block(False)

        @block.scalar
        def _(act):
            act.dma_start(stage[:, 0:N], xT[0][:, 0:N]).then_inc(chunk_dma[0], 16)
            act.dma_start(a_raw[0][:, C * P:], a1[0][:, C * P:]).then_inc(a_dma[0], 16)
            act.dma_start(const[:], consts).then_inc(const_dma, 16)

            def split_a(n, par):
                act.wait_ge(a_dma[par], n * 8 + (16 - 8 * par))
                if not isinstance(n, int) or n >= 2:
                    act.wait_ge(a_used, n - 1)
                act.activation(a_hi[par][:].rearrange("p w c k -> p (w c k)"), a_raw[par][:], ACT.Copy).then_inc(a_hi_ok, 1)

            def split_b(m, par):
                act.wait_ge(b_dma[par], m * 8 + (16 - 8 * par))
                if not isinstance(m, int) or m >= 2:
                    act.wait_ge(b_used, m - 1)
                act.activation(b_hi[par][:], b_raw[par][:], ACT.Copy).then_inc(b_hi_ok, 1)

            def split_stage(k, hi):
                act.wait_ge(stage_dma, k * 16)
                act.activation(hi[:].rearrange("p c n -> p (c n)"), stage[:], ACT.Copy).then_inc(stage_hi_ok, 1)

            def tile_from(m, par, src):
                if not isinstance(m, int) or m >= 2:
                    act.wait_ge(b_used, m - 1)
                act.activation(tile_hi[par][:], src, ACT.Copy).then_inc(tile_hi_ok, 1)

            def silu(a, done, last_block, f):
                act.wait_ge(first_mm, a + 1)
                act.wait_ge(hidden_ok, done)
                if last_block:
                    act.activation(gated[:], bank[0][:], ACT.Silu, scale=const[:, bass.ds(f + COL_AG, 1)]).then_inc(silu_ok, 1)
                else:
                    act.activation(gated[:], bank[0][:], ACT.Silu).then_inc(silu_ok, 1)

            def feed(a, apar, m, mpar, done, last_block=False, f=0, split_next=True):
                silu(a, done, last_block, f)
                if split_next:
                    split_a(a + 1, 1 - apar)
                split_b(m, mpar)
                act.wait_ge(hidden_ok, done + 1)
                tile_from(m, mpar, hidden[mpar])

            def chunk(p, c, bank_):
                act.wait_ge(feat_mm, p * C + c + 1)
                if p < 2:
                    act.activation(feat_hi[p % 2][:, c, :], bank_[:], ACT.Copy,
                                   scale=const[:, COL_LNW + c:COL_LNW + c + 1]).then_inc(feat_hi_ok, 1)
                else:
                    act.activation(feat_hi[p % 2][:, c, :], bank_[:], ACT.Copy).then_inc(feat_hi_ok, 1)

            def root(k, src):
                act.wait_ge(moments_ok, k + 1)
                act.activation(deviation[:], src, ACT.Sqrt, bias=eps[:, 0:1]).then_inc(dev_ok, 1)

            variance = moments[:, :, 1]

            def copy_values(count, bank_, vpar, b):
                act.wait_ge(v_mm, count)
                act.activation(v_sb[vpar][:, b, :], bank_[:], ACT.Copy).then_inc(v_ok, 1)

            def split_half_a(which):
                act.activation(a_hi[0][:, which].rearrange("p c k -> p (c k)"), a_raw[0][:, which * C * P:(which + 1) * C * P],
                               ACT.Copy).then_inc(a_hi_ok, 1)

            act.wait_ge(gate_dma, 16)
            split_half_a(0)
            for c in range(C):
                act.wait_ge(chunk_dma[c], 16)
                act.activation(feat_hi[0][:, c, :], stage[:, c * N:(c + 1) * N], ACT.Copy).then_inc(stage_hi_ok, 1)
            act.wait_ge(a_dma[0], 16)
            split_half_a(1)
            act.wait_ge(ratio_in, 1)
            act.activation(ratio[:], ratio_log[:], ACT.Exp).then_inc(ratio_ok, 1)

            for h in range(HALVES):
                a0, t0, s0 = h * A1, h * T1, h * F1

                def step1(f, sf, split_next=True):
                    feed(f + (a0 + 1), (a0 + 1 + sf) % 2, f + (t0 + POLY), (t0 + POLY + sf) % 2, f + s0)

                split_a(a0 + 1, (a0 + 1) % 2)
                act.wait_ge(a_used, a0 + 1)
                tile_from(t0, t0 % 2, bank[1][:])
                split_b(t0, t0 % 2)
                silu(a0 + 1, s0, False, 0)
                split_a(a0 + 2, a0 % 2)
                for m in range(1, POLY):
                    split_b(t0 + m, (t0 + m) % 2)
                    act.wait_ge(poly_ok, h * POLY_STEPS + 3 + m)
                    tile_from(t0 + m, (t0 + m) % 2, hidden[(t0 + m) % 2])
                split_b(t0 + POLY, (t0 + POLY) % 2)
                act.wait_ge(hidden_ok, s0 + 1)
                tile_from(t0 + POLY, (t0 + POLY) % 2, hidden[(t0 + POLY) % 2])
                step1(1, 1)
                if h == 0:
                    split_stage(1, feat_hi[1])
                else:
                    root(0, variance)
                step1(2, 2)
                if h > 0:
                    root(1, square[:])
                    split_stage(STAGE_V, wv_hi)
                with act.Fori(0, LOOP1) as i:
                    for j in range(2):
                        step1(i * 2 + (PEEL1 + j), PEEL1 + j)
                if h == 0:
                    split_stage(2, ctx_hi[0])
                    step1(F1 - 1, F1 - 1)
                    split_stage(3, ctx_hi[1])
            a, m, done = 2 * A1 - 1, TX0 - 1, HALVES * F1 - 1
            chunk(0, 0, bank[2])
            silu(a, done, False, 0)
            chunk(0, 1, bank[3])
            split_a(a + 1, (a + 1) % 2)
            chunk(0, 2, bank[2])
            split_b(m, m % 2)
            act.wait_ge(hidden_ok, done + 1)
            tile_from(m, m % 2, hidden[m % 2])
            chunk(0, 3, bank[3])
            for b in range(HB):
                copy_values(b + 1, bank[2 + b % 2], 0, b)

            def head(g, j, gpar, behind=2, feature_part=None, has_values=True, has_next=True, root_of=None):
                n = g * GH + j
                if behind == 0:
                    split_stage(STAGE_V + 1, wv_hi)
                act.wait_ge(first_mm, n + (AX0 + 1))
                if behind >= 1:
                    act.wait_ge(score_mm, n)
                act.activation(q_sb[:], bank[0][:], ACT.Copy).then_inc(q_ok, 1)
                split_a(n + (AX0 + 1), (AX0 + j + 1) % 2)
                if behind >= 1:
                    split_b(n + (TX0 - 1), (TX0 + j - 1) % 2)
                act.wait_ge(a_used, n + (AX0 + 1))
                act.activation(k_sb[:], bank[1][:], ACT.Copy).then_inc(k_ok, 1)
                if behind >= 1:
                    copy_probs(n, behind)
                    act.wait_ge(pv_mm, n)
                    tile_from(n + (TX0 - 1), (TX0 + j - 1) % 2, bank[1][:])
                if has_values:
                    copy_values(n + (HB + 1), bank[3], 1 - gpar, j)
                if feature_part is not None:
                    chunk(feature_part, j, bank[2])
                exponentials(n)
                if root_of is not None:
                    root(*root_of)
                if j == GH - 1 and has_next:
                    act.wait_ge(v_mm, n + (HB + 1))
                    act.wait_ge(stage_dma, g * 16 + 16 * (STAGE_V + 2))
                    act.activation(wv_hi[:].rearrange("p c n -> p (c n)"), stage[:], ACT.Copy).then_inc(stage_hi_ok, 1)

            def copy_probs(n, behind=2):
                act.wait_ge(prob_t_mm, n)
                if behind >= 2:
                    act.wait_ge(pv_mm, n - 1)
                act.activation(prob_t[:], bank[2][:], ACT.Copy).then_inc(prob_t_ok, 1)

            def exponentials(n):
                act.wait_ge(neg_max_ok, n + 1)
                if not isinstance(n, int) or n >= 1:
                    act.wait_ge(prob_t_mm, n)
                for b in range(HB):
                    e = act.activation(prob[:, b, :], score[:, b, :], ACT.Exp, bias=neg_max[:, b:b + 1],
                                       accum_out=row_sum[:, b:b + 1])
                e.then_inc(exp_ok, 1)

            for j in range(GH):
                head(0, j, 0, behind=min(j, 2), root_of={1: (2, variance), 2: (3, square[:])}.get(j))
            with act.Fori(0, (GROUPS - 2) // 2) as i:
                for e in (1, 2):
                    for j in range(GH):
                        head(i * 2 + e, j, e % 2)
            for j in range(GH):
                head(GROUPS - 1, j, 1, feature_part=1)
            for j in range(GH):
                head(GROUPS, j, 0, root_of=(4, variance) if j == 2 else None)
            with act.Fori(0, (GROUPS - 2) // 2) as i:
                for e in (1, 2):
                    for j in range(GH):
                        head(i * 2 + (GROUPS + e), j, e % 2)
            for j in range(GH):
                head(2 * GROUPS - 1, j, 1, feature_part=2, has_values=False, has_next=False)

            s0 = HALVES * F1

            def step3(f, sf, h, split_next=True):
                feed(f + (A30 + h * F3), (A30 + h * F3 + sf) % 2, f + (T30 + h * F3), (T30 + h * F3 + sf) % 2,
                     f + (s0 + h * F3), last_block=True, f=f, split_next=split_next)

            silu(A30, s0, True, 0)
            split_a(A30 + 1, (A30 + 1) % 2)
            copy_probs(HN)
            split_b(T30 - 1, (T30 - 1) % 2)
            act.wait_ge(pv_mm, HN)
            tile_from(T30 - 1, (T30 - 1) % 2, bank[3][:])
            split_b(T30, T30 % 2)
            act.wait_ge(hidden_ok, s0 + 1)
            tile_from(T30, T30 % 2, hidden[T30 % 2])
            step3(1, 1, 0)
            step3(2, 2, 0)
            root(5, variance)
            for f in range(3, PEEL3):
                step3(f, f, 0)
            with act.Fori(0, LOOP3) as i:
                for j in range(2):
                    step3(i * 2 + (PEEL3 + j), PEEL3 + j, 0)
            a, m, f = A30 + F3 - 1, T30 + F3 - 1, F3 - 1
            chunk(3, 0, bank[2])
            silu(a, s0 + f, True, f)
            chunk(3, 1, bank[3])
            split_a(a + 1, (a + 1) % 2)
            chunk(3, 2, bank[2])
            split_b(m, m % 2)
            act.wait_ge(hidden_ok, s0 + f + 1)
            tile_from(m, m % 2, hidden[m % 2])
            chunk(3, 3, bank[3])
            step3(0, 0, 1)
            step3(1, 1, 1)
            root(6, variance)
            for f in range(2, PEEL3):
                step3(f, f, 1)
            with act.Fori(0, LOOP3) as i:
                for j in range(2):
                    step3(i * 2 + (PEEL3 + j), PEEL3 + j, 1)
            step3(F3 - 1, F3 - 1, 1, split_next=False)
            for t in range(TT):
                act.wait_ge(last_moments, t + 1)
                act.activation(deviation[:, t:t + 1], moments[:, t, 1:2], ACT.Sqrt, bias=eps[:, 0:1]).then_inc(last_dev, 1)

        @block.vector
        def _(dve):
            def low(out_ap, whole, high):
                return dve.tensor_tensor(out_ap, whole, high, ALU.subtract)

            def split_a(n, par):
                dve.wait_ge(a_hi_ok, n + 2)
                low(a_lo[par][:].rearrange("p w c k -> p (w c k)"), a_raw[par][:],
                    a_hi[par][:].rearrange("p w c k -> p (w c k)").bitcast(F32)).then_inc(a_lo_ok, 1)

            def split_b(m, par):
                dve.wait_ge(b_hi_ok, m + 1)
                low(b_lo[par][:], b_raw[par][:], b_hi[par][:].bitcast(F32)).then_inc(b_lo_ok, 1)

            def split_stage(k, hi, lo):
                dve.wait_ge(stage_hi_ok, k + C)
                low(lo[:].rearrange("p c n -> p (c n)"), stage[:],
                    hi[:].rearrange("p c n -> p (c n)").bitcast(F32)).then_inc(stage_lo_ok, 1)

            def tile_rest(m, par, src):
                dve.wait_ge(tile_hi_ok, m + 1)
                low(tile_lo[par][:], src, tile_hi[par][:].bitcast(F32)).then_inc(tile_lo_ok, 1)

            def product(a, done, m, mpar, last_block, f):
                dve.wait_ge(silu_ok, done + 1)
                dve.wait_ge(a_used, a + 1)
                dve.wait_ge(tile_lo_ok, m - 1)
                if last_block:
                    dve.scalar_tensor_tensor(out=hidden[mpar], in0=bank[1][:], scalar=const[:, bass.ds(f + COL_AU, 1)],
                                             in1=gated[:], op0=ALU.mult, op1=ALU.mult).then_inc(hidden_ok, 1)
                else:
                    dve.tensor_tensor(hidden[mpar], bank[1][:], gated[:], ALU.mult).then_inc(hidden_ok, 1)

            def feed(a, apar, m, mpar, done, last_block=False, f=0, split_next=True, before=None):
                if split_next:
                    split_a(a + 1, 1 - apar)
                if before is not None:
                    before()
                product(a, done, m, mpar, last_block, f)
                split_b(m, mpar)
                dve.wait_ge(hidden_ok, done + 1)
                tile_rest(m, mpar, hidden[mpar])

            def chunk(p, c, bank_):
                dve.wait_ge(feat_hi_ok, p * C + c + 1)
                high = feat_hi[p % 2][:, c, :].bitcast(F32)
                if p < 2:
                    dve.scalar_tensor_tensor(out=feat_lo[p % 2][:, c, :], in0=bank_[:], scalar=const[:, COL_LNW + c:COL_LNW + c + 1],
                                             in1=high, op0=ALU.mult, op1=ALU.subtract).then_inc(feat_lo_ok, 1)
                else:
                    low(feat_lo[p % 2][:, c, :], bank_[:], high).then_inc(feat_lo_ok, 1)

            steps = [0]

            def step(ins):
                steps[0] += 1
                ins.then_inc(ln_step, 1)

            def after_steps():
                dve.wait_ge(ln_step, steps[0])

            def residual(p):
                for t in range(TT):
                    if t < TT - 1:
                        dve.wait_ge(acc_full, p * (TT - 1) + t + 1)
                    else:
                        dve.wait_ge(b_used, PART_END[p] + 1)
                    x = resid[:, (p % 2) * TT + t, :]
                    if p < 2:
                        dve.tensor_tensor(x, acc[t][:], x, ALU.add).then_inc(acc_read, 1)
                    elif p < 4:
                        dve.scalar_tensor_tensor(out=x, in0=x, scalar=2.0, in1=acc[t][:], op0=ALU.mult, op1=ALU.add).then_inc(acc_read, 1)
                    else:
                        dve.tensor_tensor(normed[:, t, :], acc[t][:], ad_sb[:], ALU.mult).then_inc(acc_read, 1)
                        dve.wait_ge(acc_read, p * TT + t + 1)
                        dve.tensor_tensor(x, normed[:, t, :], x, ALU.add).then_inc(acc_sum, 1)

            def take_moments(p):
                for t in range(TT):
                    step(dve.bn_stats(stats[:, t, :], resid[:, (p % 2) * TT + t, :]))
                after_steps()
                for t in range(TT):
                    step(dve.bn_aggr(moments[:, t, :], stats[:, t, :]))
                after_steps()

            def variances(p):
                dve.wait_ge(acc_read, (p + 1) * TT)
                if p >= 4:
                    dve.wait_ge(acc_sum, (p - 3) * TT)
                take_moments(p)
                dve.sem_inc(moments_ok, 1)

            def normalise(p, k, last=False):
                dve.wait_ge(dev_ok, k + 1)
                step(dve.reciprocal(scale[:], deviation[:]))
                after_steps()
                for t in range(TT):
                    x = resid[:, (p % 2) * TT + t, :]
                    ins = dve.tensor_scalar(x, x, moments[:, t, 0:1], scale[:, t:t + 1], ALU.subtract, ALU.mult)
                    if p < 2:
                        step(ins)
                    elif p < 4:
                        ins.then_inc(operand_ok, 1)
                    else:
                        ins.then_inc(part_ok, 1)
                if p < 2:
                    after_steps()
                    take_moments(p)
                    step(dve.tensor_tensor(square[:], moments[:, :, 0], moments[:, :, 0], ALU.mult))
                    after_steps()
                    dve.tensor_tensor(square[:], square[:], moments[:, :, 1], ALU.add).then_inc(moments_ok, 1)

            def rms_operand(p, k):
                dve.wait_ge(dev_ok, k + 1)
                step(dve.reciprocal(scale[:], deviation[:]))
                after_steps()
                for t in range(TT):
                    dve.tensor_scalar(normed[:, t, :], resid[:, (p % 2) * TT + t, :], scale[:, t:t + 1], None,
                                      ALU.mult).then_inc(operand_ok, 1)

            dve.memset(eps[:], LN_EPS).then_inc(eps_ok, 1)
            def split_half_a(which):
                dve.wait_ge(a_hi_ok, which + 1)
                low(a_lo[0][:, which].rearrange("p c k -> p (c k)"), a_raw[0][:, which * C * P:(which + 1) * C * P],
                    a_hi[0][:, which].rearrange("p c k -> p (c k)").bitcast(F32)).then_inc(a_lo_ok, 1)

            split_half_a(0)
            for c in range(C):
                dve.wait_ge(stage_hi_ok, c + 1)
                low(feat_lo[0][:, c, :], stage[:, c * N:(c + 1) * N], feat_hi[0][:, c, :].bitcast(F32)).then_inc(stage_lo_ok, 1)
            split_half_a(1)
            dve.wait_ge(const_dma, 16)
            dve.tensor_scalar(ratio_log[:, 0:1], const[:, COL_DISC:COL_DISC + 1], -1.0, None, ALU.mult)
            dve.tensor_tensor(ratio_log[:, 1:ORDERS], const[:, COL_DISC:COL_DISC + ORDERS - 1],
                              const[:, COL_DISC + 1:COL_DISC + ORDERS], ALU.subtract).then_inc(ratio_in, 1)

            for h in range(HALVES):
                a0, t0, s0, p0 = h * A1, h * T1, h * F1, h * POLY_STEPS

                def step1(f, sf, before=None):
                    feed(f + (a0 + 1), (a0 + 1 + sf) % 2, f + (t0 + POLY), (t0 + POLY + sf) % 2, f + s0, before=before)

                split_a(a0 + 1, (a0 + 1) % 2)
                dve.wait_ge(first_mm, a0 + 1)
                dve.tensor_scalar(delta, bank[0][:], const[:, COL_POINT:COL_POINT + 1], None, ALU.subtract).then_inc(poly_ok, 1)
                dve.wait_ge(poly_ok, p0 + 1)
                dve.tensor_tensor(delta_kept, delta, delta, ALU.mult).then_inc(poly_ok, 1)
                dve.wait_ge(poly_ok, p0 + 2)
                dve.scalar_tensor_tensor(out=delta_kept, in0=delta_kept, scalar=THD ** 2, in1=delta,
                                         op0=ALU.is_le, op1=ALU.mult).then_inc(poly_ok, 1)
                if h == 0:
                    dve.wait_ge(ratio_ok, 1)
                dve.wait_ge(a_used, a0 + 1)
                if h > 0:
                    dve.wait_ge(tile_lo_ok, t0)
                tile_rest(t0, t0 % 2, bank[1][:])
                dve.scalar_tensor_tensor(out=hidden[(t0 + 1) % 2], in0=bank[1][:], scalar=ratio[:, 0:1], in1=delta,
                                         op0=ALU.mult, op1=ALU.mult).then_inc(poly_ok, 1)
                split_b(t0, t0 % 2)
                split_a(a0 + 2, a0 % 2)
                if h > 0:
                    residual(0)
                for m in range(1, POLY):
                    if m + 1 < POLY:
                        dve.wait_ge(poly_ok, p0 + 3 + m)
                        dve.wait_ge(tile_lo_ok, t0 + m)
                        dve.scalar_tensor_tensor(out=hidden[(t0 + m + 1) % 2], in0=hidden[(t0 + m) % 2],
                                                 scalar=ratio[:, m:m + 1], in1=(delta if m < KEEP_ORDER else delta_kept),
                                                 op0=ALU.mult, op1=ALU.mult).then_inc(poly_ok, 1)
                    split_b(t0 + m, (t0 + m) % 2)
                    tile_rest(t0 + m, (t0 + m) % 2, hidden[(t0 + m) % 2])
                product(a0 + 1, s0, t0 + POLY, (t0 + POLY) % 2, False, 0)
                split_b(t0 + POLY, (t0 + POLY) % 2)
                dve.wait_ge(hidden_ok, s0 + 1)
                tile_rest(t0 + POLY, (t0 + POLY) % 2, hidden[(t0 + POLY) % 2])
                step1(1, 1, before=(lambda: variances(0)) if h > 0 else None)
                if h == 0:
                    split_stage(1, feat_hi[1], feat_lo[1])
                step1(2, 2, before=(lambda: normalise(0, 0)) if h > 0 else None)
                if h == 0:
                    dve.wait_ge(mask_dma, 32)
                    dve.tensor_scalar(mask_add[:], mask_u8, 1.0, MASKED, ALU.subtract, ALU.mult).then_inc(mask_ok, 1)
                    dve.tensor_reduce(row_valid[:], mask_u8, AX_X, ALU.max).then_inc(mask_ok, 1)
                    dve.wait_ge(resid_dma, 32)
                else:
                    rms_operand(0, 1)
                    split_stage(STAGE_V, wv_hi, wv_lo)
                with dve.Fori(0, LOOP1) as i:
                    for j in range(2):
                        step1(i * 2 + (PEEL1 + j), PEEL1 + j)
                if h == 0:
                    split_stage(2, ctx_hi[0], ctx_lo[0])
                    step1(F1 - 1, F1 - 1)
                    split_stage(3, ctx_hi[1], ctx_lo[1])
            a, m, done = 2 * A1 - 1, TX0 - 1, HALVES * F1 - 1
            chunk(0, 0, bank[2])
            chunk(0, 1, bank[3])
            split_a(a + 1, (a + 1) % 2)
            product(a, done, m, m % 2, False, 0)
            chunk(0, 2, bank[2])
            split_b(m, m % 2)
            dve.wait_ge(hidden_ok, done + 1)
            tile_rest(m, m % 2, hidden[m % 2])
            chunk(0, 3, bank[3])

            def head(g, j, gpar, half, behind=2, feature_part=None, has_next=True, past_half=None, before=None):
                n = g * GH + j
                if behind == 0:
                    split_stage(STAGE_V + 1, wv_hi, wv_lo)
                if behind >= 1:
                    divide(n, half if past_half is None else past_half)
                split_a(n + (AX0 + 1), (AX0 + j + 1) % 2)
                if behind >= 1:
                    split_b(n + (TX0 - 1), (TX0 + j - 1) % 2)
                if before is not None:
                    before()
                dve.wait_ge(score_mm, n + 1)
                dve.wait_ge(bias_dma[gpar], g * 8 + (16 - 8 * gpar))
                dve.tensor_tensor(score[:], bank[0][:].rearrange("p (b k) -> p b k", b=HB),
                                  bias_sb[gpar][:, j * SEQ:(j + 1) * SEQ].unsqueeze(1).broadcast_to([P, HB, SEQ]),
                                  ALU.add).then_inc(biased_ok, 1)
                dve.wait_ge(mask_ok, 2)
                dve.wait_ge(biased_ok, n + 1)
                for b in range(HB):
                    ins = dve.tensor_tensor_reduce(score[:, b, :], score[:, b, :], mask_add[:, half * HB + b, :], 1.0, -3e38,
                                                   ALU.add, ALU.max, row_max[:, b:b + 1])
                ins.then_inc(masked_ok, 1)
                dve.wait_ge(masked_ok, n + 1)
                dve.tensor_scalar(neg_max[:], row_max[:], -1.0, None, ALU.mult).then_inc(neg_max_ok, 1)
                if behind >= 1:
                    tile_rest(n + (TX0 - 1), (TX0 + j - 1) % 2, bank[1][:])
                if feature_part is not None:
                    chunk(feature_part, j, bank[2])
                if j == GH - 1 and has_next:
                    split_stage(g + (STAGE_V + 2), wv_hi, wv_lo)

            def look_at(k, par):
                dve.wait_ge(piece_dma[par], k * 8 + (16 - 8 * par))
                dve.tensor_scalar(piece[par], piece[par], LOW_BITS, None, ALU.bitwise_and).then_inc(piece_bits, 1)
                dve.wait_ge(piece_bits, k + 1)
                dve.tensor_reduce(piece_top[:, bass.ds(k, 1)], piece[par], AX_X, ALU.max).then_inc(piece_free, 1)

            def divide(n, half):
                dve.wait_ge(exp_ok, n)
                dve.reciprocal(row_inv[:], row_sum[:]).then_inc(inv_ok, 1)
                dve.wait_ge(inv_ok, n * 2 - 1)
                dve.tensor_tensor(row_inv[:], row_inv[:], row_valid[:, half * HB:(half + 1) * HB], ALU.mult).then_inc(inv_ok, 1)
                dve.wait_ge(inv_ok, n * 2)
                dve.tensor_tensor(prob[:], prob[:], row_inv[:].unsqueeze(2).broadcast_to([P, HB, SEQ]), ALU.mult).then_inc(prob_ok, 1)

            def add_and_measure(p):
                residual(p)
                variances(p)

            dve.wait_ge(tile_lo_ok, TX0)
            dve.sem_inc(piece_free, 2)
            ends = {1: lambda: add_and_measure(1), 2: lambda: normalise(1, 2), 3: lambda: rms_operand(1, 3)}
            for j in range(GH):
                head(0, j, 0, 0, behind=min(j, 2), before=ends.get(j))
            with dve.Fori(0, (GROUPS - 2) // 2) as i:
                for e in (1, 2):
                    for j in range(GH):
                        head(i * 2 + e, j, e % 2, 0,
                             before=lambda: look_at(i * (2 * GH) + ((e - 1) * GH + j), j % 2))
            dve.wait_ge(piece_free, SCANS + 2)
            dve.tensor_reduce(piece_all[:, 0:1], piece_top[:], AX_X, ALU.max).then_inc(top_ok, 1)
            for j in range(GH):
                head(GROUPS - 1, j, 1, 0, feature_part=1)
            ends = {2: lambda: add_and_measure(2), 3: lambda: normalise(2, 4)}
            for j in range(GH):
                head(GROUPS, j, 0, 1, past_half=(0 if j == 0 else 1), before=ends.get(j))
            with dve.Fori(0, (GROUPS - 2) // 2) as i:
                for e in (1, 2):
                    for j in range(GH):
                        head(i * 2 + (GROUPS + e), j, e % 2, 1)
            for j in range(GH):
                head(2 * GROUPS - 1, j, 1, 1, feature_part=2, has_next=False)

            s0 = HALVES * F1

            def step3(f, sf, h, split_next=True, before=None):
                feed(f + (A30 + h * F3), (A30 + h * F3 + sf) % 2, f + (T30 + h * F3), (T30 + h * F3 + sf) % 2,
                     f + (s0 + h * F3), last_block=True, f=f, split_next=split_next, before=before)

            divide(HN, 1)
            split_a(A30 + 1, (A30 + 1) % 2)
            product(A30, s0, T30, T30 % 2, True, 0)
            split_b(T30 - 1, (T30 - 1) % 2)
            tile_rest(T30 - 1, (T30 - 1) % 2, bank[3][:])
            split_b(T30, T30 % 2)
            dve.wait_ge(hidden_ok, s0 + 1)
            tile_rest(T30, T30 % 2, hidden[T30 % 2])
            step3(1, 1, 0)
            residual(3)
            step3(2, 2, 0, before=lambda: variances(3))
            step3(3, 3, 0, before=lambda: normalise(3, 5))
            with dve.Fori(0, LOOP3) as i:
                for j in range(2):
                    step3(i * 2 + (PEEL3 + j), PEEL3 + j, 0)
            a, m, f = A30 + F3 - 1, T30 + F3 - 1, F3 - 1
            chunk(3, 0, bank[2])
            chunk(3, 1, bank[3])
            split_a(a + 1, (a + 1) % 2)
            product(a, s0 + f, m, m % 2, True, f)
            chunk(3, 2, bank[2])
            split_b(m, m % 2)
            dve.wait_ge(hidden_ok, s0 + f + 1)
            tile_rest(m, m % 2, hidden[m % 2])
            chunk(3, 3, bank[3])
            step3(0, 0, 1)
            residual(4)
            step3(1, 1, 1, before=lambda: variances(4))
            step3(2, 2, 1, before=lambda: normalise(4, 6))
            step3(3, 3, 1)
            with dve.Fori(0, LOOP3) as i:
                for j in range(2):
                    step3(i * 2 + (PEEL3 + j), PEEL3 + j, 1)
            step3(F3 - 1, F3 - 1, 1, split_next=False)

            def scaled(t):
                if t < TT - 1:
                    dve.wait_ge(acc_full, 5 * (TT - 1) + t + 1)
                else:
                    dve.wait_ge(b_used, LAST_T + 1)
                dve.tensor_tensor(normed[:, t, :], acc[t][:], ad_sb[:], ALU.mult).then_inc(last_scaled, 1)

            def measured(t):
                dve.wait_ge(last_sum, t + 1)
                dve.bn_stats(stats[:, t, :], resid[:, TT + t, :]).then_inc(last_stats, 1)
                dve.wait_ge(last_stats, t + 1)
                dve.bn_aggr(moments[:, t, :], stats[:, t, :]).then_inc(last_moments, 1)

            def normed_tile(t):
                dve.wait_ge(last_dev, t + 1)
                dve.reciprocal(scale[:, t:t + 1], deviation[:, t:t + 1]).then_inc(last_scale, 1)
                dve.wait_ge(last_scale, t + 1)
                x = resid[:, TT + t, :]
                dve.tensor_scalar(x, x, moments[:, t, 0:1], scale[:, t:t + 1], ALU.subtract, ALU.mult).then_inc(last_ok, 1)

            for t in range(TT + 2):
                if t < TT:
                    scaled(t)
                if 1 <= t <= TT:
                    measured(t - 1)
                if t >= 2:
                    normed_tile(t - 2)


def build(nc, arrays):
    aps = {name: nc.dram_tensor(name, a.shape, mybir.dt.from_np(a.dtype), kind="ExternalInput").ap()
           for name, a in arrays.items()}
    out = nc.dram_tensor("out", (HALVES, TT, P, D), F32, kind="ExternalOutput").ap()
    decoder_kernel(nc, out=out, **aps)


def kernel(**inputs):
    import numpy as np
    import concourse.bacc as bacc
    from concourse.bass_utils import run_bass_kernel_spmd

    g = {k: np.asarray(v) for k, v in inputs.items()}

    def feature_major(x):
        return x.reshape(HALVES, N, C, P).transpose(0, 3, 2, 1).reshape(HALVES, P, C * N)

    def in_maps(w, tiles):
        w = np.concatenate([w, np.zeros((tiles * P - w.shape[0], D), w.dtype)])
        return w.reshape(tiles, P, C, P).transpose(0, 3, 2, 1).reshape(tiles, P, C * P)

    def out_maps(w, tiles):
        w = np.concatenate([w.T, np.zeros((tiles * P - w.shape[1], D), w.dtype)])
        return w.reshape(tiles, P, D)

    def columns(v, tiles):
        v = np.concatenate([v, np.zeros(tiles * P - v.shape[0], v.dtype)])
        return v.reshape(tiles, P).T

    def pair(w0, w1, tiles):
        return np.concatenate([in_maps(w0, tiles), in_maps(w1, tiles)], axis=2)

    wv = g["L0_xattn_w_v"].reshape(GROUPS, GH * P, C, P).transpose(0, 3, 2, 1).reshape(GROUPS, P, C * GH * P)
    arrays = {
        "xT": feature_major(g["x"]),
        "ctxT": feature_major(g["ctx_4096"]),
        "x_tok": g["x"].reshape(HALVES, TT, P, D).transpose(0, 2, 1, 3),
        "mask": np.ascontiguousarray(g["mask_BxSxS2_bk0"].transpose(1, 0, 2)).view(np.uint32),
        "consts": np.concatenate([
            columns(g["L0_attn_local_point"], 1), columns(g["L0_xattn_ln_weight"], C),
            np.broadcast_to(g["L0_attn_discount_factor"], (P, ORDERS)),
            columns(g["L0_ffn_ag"], F3), columns(g["L0_ffn_au"], F3)], axis=1),
        "ad": np.broadcast_to(g["L0_ffn_ad"], (P, D)),
        "a1": np.concatenate([pair(g["L0_attn_gate_w"], g["L0_attn_up_w"], 1),
                              pair(g["L0_attn_ffn_gate_w"], g["L0_attn_ffn_up_w"], F1)]),
        "b1": np.concatenate([out_maps(g["L0_attn_local_approx_output"], 1)]
                             + [out_maps(g["L0_attn_fuse_weight"][:, :, m], 1) for m in range(ORDERS)]
                             + [out_maps(g["L0_attn_ffn_down_w"], F1)]),
        "ax": pair(g["L0_xattn_w_q"], g["L0_xattn_w_k"], HEADS),
        "bx": out_maps(g["L0_xattn_w_out"], HEADS),
        "wv": np.concatenate([wv, wv[:1]]),
        "bias": g["L0_xattn_position_bias"].reshape(GROUPS, GH, SEQ, SEQ).transpose(0, 2, 1, 3).reshape(GROUPS, P, GH * SEQ),
        "w3": np.concatenate([pair(g["L0_ffn_Wg"], g["L0_ffn_Wu"], F3), out_maps(g["L0_ffn_Wd"], F3)], axis=2),
    }
    arrays = {k: np.ascontiguousarray(v) for k, v in arrays.items()}
    nc = bacc.Bacc("TRN2", target_bir_lowering=False, num_devices=1)
    build(nc, arrays)
    r = run_bass_kernel_spmd(nc, [arrays], core_ids=[0])
    return r.results[0]["out"].reshape(BATCH, SEQ, D)
```

```python
from contextlib import ExitStack

import concourse.bass as bass
from concourse import mybir

P = 128
F32 = mybir.dt.float32
F32R = mybir.dt.float32r
U8 = mybir.dt.uint8
U32 = mybir.dt.uint32
I32 = mybir.dt.int32
ALU = mybir.AluOpType
ACT = mybir.ActivationFunctionType
AX_X = mybir.AxisListType.X

BATCH, SEQ, D = 8, 128, 512
HALVES = 2
HB = BATCH // HALVES
N = HB * SEQ
C = D // P
TT = N // P
HEADS = 32
GH = 4
GROUPS = HEADS // GH
ORDERS = 6
POLY = ORDERS + 1
KEEP_ORDER = 4
THD = 2.5
F1 = -(-1248 // P)
F3 = -(-1376 // P)
LN_EPS = 1e-5
RMS_EPS = 1e-5
MASKED = 1e30

A1, T1 = 1 + F1, POLY + F1
AX0, TX0 = HALVES * A1, HALVES * T1
A30, T30 = AX0 + HALVES * HEADS, TX0 + HALVES * HEADS
POLY_STEPS = 3 + ORDERS
STAGE_V = 4
LAST_T = T30 + HALVES * F3 - 1
HN = HALVES * HEADS
PART_END = [T1 - 1, TX0 - 1, TX0 + HEADS - 1, T30 - 1, T30 + F3 - 1, LAST_T]
FEW = P // HB
WV_CUT = 3 * C * GH * P // 4

COL_POINT, COL_LNW, COL_DISC = 0, 1, 1 + C
COL_AG = COL_DISC + ORDERS
COL_AU = COL_AG + F3
COLS = COL_AU + F3

PEEL1, PEEL3 = 3, 4
LOOP1, LOOP3 = (F1 - 1 - PEEL1) // 2, (F3 - 1 - PEEL3) // 2
SCANS = (GROUPS - 2) * GH
SCAN = F3 * 3 * D // SCANS
assert SCAN * SCANS == F3 * 3 * D and SCAN <= 2 * N
LOW_BITS = 0xFFF


def decoder_kernel(nc, xT, ctxT, x_tok, mask, consts, ad, a1, b1, ax, bx, wv, bias, w3, out):
    with ExitStack() as ctx:
        def sb(name, shape, dt=F32):
            return ctx.enter_context(nc.sbuf_tensor(name, shape, dt))

        def two(name, shape, dt=F32):
            return [sb(f"{name}{i}", shape, dt) for i in range(2)]

        def sem(name):
            return ctx.enter_context(nc.semaphore(name))

        a_raw, a_hi, a_lo = two("a_raw", [P, 2 * C * P]), two("a_hi", [P, 2, C, P], F32R), two("a_lo", [P, 2, C, P], F32R)
        b_raw, b_hi, b_lo = two("b_raw", [P, D]), two("b_hi", [P, D], F32R), two("b_lo", [P, D], F32R)
        stage = sb("stage", [P, C * N])
        wv_hi, wv_lo = sb("wv_hi", [P, C, GH * P], F32R), sb("wv_lo", [P, C, GH * P], F32R)
        feat_hi, feat_lo = two("feat_hi", [P, C, N], F32R), two("feat_lo", [P, C, N], F32R)
        ctx_hi, ctx_lo = two("ctx_hi", [P, C, N], F32R), two("ctx_lo", [P, C, N], F32R)
        tile_hi, tile_lo = two("tile_hi", [P, N], F32R), two("tile_lo", [P, N], F32R)
        gated = sb("gated", [P, N])
        pair0, pair1 = sb("pair0", [P, 2 * N]), sb("pair1", [P, 2 * N])
        hidden = [pair0[:, 0:N], pair0[:, N:]]
        delta, delta_kept = pair1[:, 0:N], pair1[:, N:]
        piece = [pair0[:, 0:SCAN].bitcast(I32), pair1[:, 0:SCAN].bitcast(I32)]
        piece_top, piece_all = sb("piece_top", [P, SCANS]), sb("piece_all", [P, 2])
        low_flag = sb("low_flag", [P, 1], I32)
        ratio_log, ratio = sb("ratio_log", [P, ORDERS]), sb("ratio", [P, ORDERS])
        q_sb, k_sb = sb("q_sb", [P, N]), sb("k_sb", [P, N])
        v_sb = two("v_sb", [P, HB, GH * P])
        score, prob = sb("score", [P, HB, P]), sb("prob", [P, N])
        prob_t = sb("prob_t", [P, HB * P])
        bias_sb = two("bias_sb", [P, GH * P])
        mask_words = sb("mask_words", [P, BATCH, SEQ // 4], U32)
        mask_u8 = mask_words[:].bitcast(U8)
        mask_add = sb("mask_add", [P, BATCH, P])
        row_valid = sb("row_valid", [P, BATCH])
        row_max, neg_max = sb("row_max", [P, HB]), sb("neg_max", [P, HB])
        row_sum, row_inv = sb("row_sum", [P, HB]), sb("row_inv", [P, HB])
        few_ctx = [sb("few_ctx", [P, C * P]), gated]
        value_rows = sb("value_rows", [P, HB])
        many, keys_flag = sb("many", [P, BATCH + 2]), sb("keys_flag", [P, 1], I32)
        resid = sb("resid", [P, HALVES * TT, D])
        normed = sb("normed", [P, TT, D])
        ad_sb = sb("ad_sb", [P, D])
        const = sb("const", [P, COLS])
        stats = sb("stats", [P, TT, 6])
        moments = sb("moments", [P, TT, 2])
        scale, rms_scale = sb("scale", [P, TT]), sb("rms_scale", [P, TT])
        neg_mean = sb("neg_mean", [P, TT])
        exponent = sb("exponent", [P, TT])
        ident = sb("ident", [P, P])
        table_in, table_out = sb("table_in", [P, 1]), sb("table_out", [P, 1])

        bank = [ctx.enter_context(nc.psum_tensor(f"bank{i}", [P, 512], F32)) for i in range(4)]
        acc = [ctx.enter_context(nc.psum_tensor(f"acc{t}", [P, D], F32)) for t in range(TT)]

        a_dma, b_dma = [sem("a_dma0"), sem("a_dma1")], [sem("b_dma0"), sem("b_dma1")]
        gate_dma = sem("gate_dma")
        chunk_dma = [sem(f"chunk_dma{c}") for c in range(C)]
        stage_dma = sem("stage_dma")
        bias_dma = [sem("bias_dma0"), sem("bias_dma1")]
        const_dma, mask_dma, resid_dma, out_dma = sem("const_dma"), sem("mask_dma"), sem("resid_dma"), sem("out_dma")
        a_hi_ok, a_lo_ok, b_hi_ok, b_lo_ok = sem("a_hi_ok"), sem("a_lo_ok"), sem("b_hi_ok"), sem("b_lo_ok")
        stage_hi_ok, stage_lo_ok = sem("stage_hi_ok"), sem("stage_lo_ok")
        tile_hi_ok, tile_lo_ok = sem("tile_hi_ok"), sem("tile_lo_ok")
        feat_hi_ok, feat_lo_ok = sem("feat_hi_ok"), sem("feat_lo_ok")
        first_mm = sem("first_mm")
        a_used = sem("a_used")
        b_used = sem("b_used")
        score_mm, prob_t_mm, pv_mm, v_mm = sem("score_mm"), sem("prob_t_mm"), sem("pv_mm"), sem("v_mm")
        feat_mm = sem("feat_mm")
        acc_full = sem("acc_full")
        silu_ok, hidden_ok = sem("silu_ok"), sem("hidden_ok")
        poly_ok, ratio_in, ratio_ok = sem("poly_ok"), sem("ratio_in"), sem("ratio_ok")
        q_ok, k_ok, v_ok = sem("q_ok"), sem("k_ok"), sem("v_ok")
        biased_ok, masked_ok, neg_max_ok, exp_ok = sem("biased_ok"), sem("masked_ok"), sem("neg_max_ok"), sem("exp_ok")
        inv_ok, prob_ok, prob_t_ok = sem("inv_ok"), sem("prob_ok"), sem("prob_t_ok")
        mask_ok = sem("mask_ok")
        wv_cut_ok = sem("wv_cut_ok")
        few_dma = sem("few_dma")
        rows_in, value_rows_ok = sem("rows_in"), sem("value_rows_ok")
        many_ok, keys_flag_ok = sem("many_ok"), sem("keys_flag_ok")
        normed_ok, root_step = sem("normed_ok"), sem("root_step")
        acc_read, acc_sum, moments_ok, scale_ok = sem("acc_read"), sem("acc_sum"), sem("moments_ok"), sem("scale_ok")
        ln_step, operand_ok, part_ok = sem("ln_step"), sem("operand_ok"), sem("part_ok")
        piece_dma = [sem("piece_dma0"), sem("piece_dma1")]
        piece_free, piece_bits, top_ok, all_ok, flag_ok = sem("piece_free"), sem("piece_bits"), sem("top_ok"), sem("all_ok"), sem("flag_ok")
        last_stats = sem("last_stats")
        last_moments, last_scale = sem("last_moments"), sem("last_scale")
        last_sum, last_offset, last_act_ok = sem("last_sum"), sem("last_offset"), sem("last_act_ok")
        last_ok, last_out_dma = sem("last_ok"), sem("last_out_dma")
        table_in_ok = sem("table_in_ok")
        ident_set, ident_ok = sem("ident_set"), sem("ident_ok")

        block = ctx.enter_context(nc.Block())

        def staged(k):
            return C + k

        @block.sync
        def _(sp):
            def load_a(n, par, src, after_products=False):
                if after_products:
                    sp.wait_ge(a_used, n - 1)
                elif not isinstance(n, int) or n >= 2:
                    sp.wait_ge(a_lo_ok, n)
                sp.dma_start(a_raw[par][:], src).then_inc(a_dma[par], 16)

            def load_b(m, par, src):
                if not isinstance(m, int) or m >= 2:
                    sp.wait_ge(b_lo_ok, m - 1)
                sp.dma_start(b_raw[par][:], src).then_inc(b_dma[par], 16)

            def load_bias(g, par, src):
                if not isinstance(g, int) or g >= 2:
                    sp.wait_ge(biased_ok, (g - 1) * GH)
                sp.dma_start(bias_sb[par][:], src).then_inc(bias_dma[par], 16)

            sp.dma_start(a_raw[0][:, 0:C * P], a1[0][:, 0:C * P]).then_inc(gate_dma, 16)
            for c in range(1, C):
                sp.dma_start(stage[:, c * N:(c + 1) * N], xT[0][:, c * N:(c + 1) * N]).then_inc(chunk_dma[c], 16)
            sp.dma_start(a_raw[0][:, C * P:], a1[0][:, C * P:]).then_inc(a_dma[0], 16)

            for h in range(HALVES):
                a0, t0 = h * A1, h * T1

                def load_step1(f, static_f):
                    load_a(f + (a0 + 1), (a0 + 1 + static_f) % 2, a1[f + 1])
                    load_b(f + (t0 + POLY), (t0 + POLY + static_f) % 2, b1[f + POLY])

                if h > 0:
                    load_a(a0, a0 % 2, a1[0])
                load_b(t0, t0 % 2, b1[0])
                load_a(a0 + 1, (a0 + 1) % 2, a1[1])
                load_b(t0 + 1, (t0 + 1) % 2, b1[1])
                load_a(a0 + 2, a0 % 2, a1[2])
                for m in range(2, POLY + 1):
                    load_b(t0 + m, (t0 + m) % 2, b1[m])
                load_b(t0 + POLY + 1, (t0 + POLY + 1) % 2, b1[POLY + 1])
                load_step1(2, 2)
                with sp.Fori(0, LOOP1) as i:
                    for j in range(2):
                        load_step1(i * 2 + (PEEL1 + j), PEEL1 + j)
                load_step1(F1 - 1, F1 - 1)

            load_bias(0, 0, bias[0])

            pieces = w3.rearrange("f p k -> (f p k)").rearrange("(p k) -> p k", p=P)

            def load_piece(k, par):
                sp.wait_ge(piece_free, k + 1)
                sp.dma_start(pair0[:, 0:SCAN] if par == 0 else pair1[:, 0:SCAN],
                             pieces[:, bass.ds(k * SCAN, SCAN)]).then_inc(piece_dma[par], 16)

            def load_group(g, gl, par, last=False, piece0=None):
                for j in range(GH):
                    if j == GH - 1 and isinstance(gl, int) and gl == GROUPS - 1:
                        following = w3[0][:, 0:2 * D] if last else ax[0]
                    else:
                        following = ax[gl * GH + (j + 1)]
                    load_a(g * GH + (AX0 + j + 1), (AX0 + j + 1) % 2, following, after_products=True)
                    load_b(g * GH + (TX0 + j), (TX0 + j) % 2, bx[gl * GH + j])
                    if piece0 is not None:
                        load_piece(piece0 + j, j % 2)
                    if j == GH - 1 and not last:
                        load_bias(g + 1, (par + 1) % 2, bias[0 if isinstance(gl, int) and gl == GROUPS - 1 else gl + 1])

            load_a(AX0, AX0 % 2, ax[0], after_products=True)
            for h in range(HALVES):
                g0 = h * GROUPS
                load_group(g0, 0, 0)
                with sp.Fori(0, (GROUPS - 2) // 2) as i:
                    for e in (1, 2):
                        load_group(i * 2 + (g0 + e), i * 2 + e, e % 2,
                                   piece0=(i * (2 * GH) + (e - 1) * GH) if h == 0 else None)
                load_group(g0 + GROUPS - 1, GROUPS - 1, 1, last=(h == HALVES - 1))

            for h in range(HALVES):
                a0, t0 = A30 + h * F3, T30 + h * F3

                def load_step3(f, static_f):
                    if h > 0 or static_f > 0:
                        load_a(f + a0, (a0 + static_f) % 2, w3[f][:, 0:2 * D], after_products=(h == 0 and static_f < 2))
                    load_b(f + t0, (t0 + static_f) % 2, w3[f][:, 2 * D:])

                for f in range(PEEL3):
                    load_step3(f, f)
                with sp.Fori(0, LOOP3) as i:
                    for j in range(2):
                        load_step3(i * 2 + (PEEL3 + j), PEEL3 + j)
                load_step3(F3 - 1, F3 - 1)

            for t in range(TT - 1):
                sp.wait_ge(last_act_ok, t + 1)
                sp.dma_start(out[1, t], resid[:, TT + t, :]).then_inc(last_out_dma, 16)
            sp.wait_ge(last_ok, 1)
            sp.dma_start(out[1, TT - 1][:P // 2], resid[:P // 2, 2 * TT - 1, :]).then_inc(last_out_dma, 16)
            sp.wait_ge(last_out_dma, (TT + 1) * 16)

        @block.gpsimd
        def _(pool):
            pool.memset(ident[:], 0.0).then_inc(ident_set, 1)
            pool.wait_ge(ident_set, 1)
            pool.memset(exponent[:], -0.5)
            pool.affine_select(out=ident[:], in_=ident[:], compare_op=ALU.not_equal, fill=1.0, base=0,
                               pattern=[[-1, P]], channel_multiplier=1).then_inc(ident_ok, 1)
            pool.dma_start(const[:], consts).then_inc(const_dma, 16)
            pool.dma_start(mask_words[:], mask).then_inc(mask_dma, 16)
            pool.dma_start(ad_sb[:], ad).then_inc(mask_dma, 16)

            def load_stage(k, src):
                pool.wait_ge(stage_lo_ok, k + staged(-1))
                pool.dma_start(stage[:], src).then_inc(stage_dma, 16)

            variance = moments[:, :, 1]

            roots = [0]

            def inverse_root(out_ap, src, epsilon):
                pool.tensor_scalar(out_ap, src, epsilon, None, ALU.add).then_inc(root_step, 1)
                roots[0] += 1
                pool.wait_ge(root_step, roots[0])
                return pool.tensor_tensor(out_ap, out_ap, exponent[:, 0:out_ap.shape[1]], ALU.pow)

            def scales(p):
                pool.wait_ge(moments_ok, p + 1)
                ins = inverse_root(scale[:], variance, LN_EPS)
                if p < 2:
                    for factor in (variance, rms_scale[:]):
                        ins.then_inc(root_step, 1)
                        roots[0] += 1
                        pool.wait_ge(root_step, roots[0])
                        ins = pool.tensor_tensor(rms_scale[:], factor, scale[:], ALU.mult)
                    ins.then_inc(root_step, 1)
                    roots[0] += 1
                    pool.wait_ge(root_step, roots[0])
                    ins = inverse_root(rms_scale[:], rms_scale[:], RMS_EPS)
                ins.then_inc(scale_ok, 1)

            def normalise(p):
                scales(p)
                pool.wait_ge(scale_ok, p + 1)
                for t in range(TT):
                    x = resid[:, (p % 2) * TT + t, :]
                    ins = pool.tensor_scalar(x, x, moments[:, t, 0:1], scale[:, t:t + 1], ALU.subtract, ALU.mult)
                    ins.then_inc(normed_ok if p < 2 else operand_ok if p < 4 else part_ok, 1)
                if p < 2:
                    for t in range(TT):
                        pool.wait_ge(normed_ok, p * TT + t + 1)
                        pool.tensor_scalar(normed[:, t, :], resid[:, (p % 2) * TT + t, :], rms_scale[:, t:t + 1], None,
                                           ALU.mult).then_inc(operand_ok, 1)

            load_stage(1, xT[1])
            for h in range(HALVES):
                pool.dma_start(resid[:, h * TT:(h + 1) * TT, :], x_tok[h]).then_inc(resid_dma, 16)
            load_stage(2, ctxT[0])
            pool.dma_start(few_ctx[0][:].rearrange("p (c n) -> p c n", c=C),
                           ctxT[0].rearrange("p (c n) -> p c n", c=C)[:, :, N - P:]).then_inc(few_dma, 16)
            pool.wait_ge(many_ok, 2)
            pool.partition_all_reduce(many[:, BATCH + 1:BATCH + 2], many[:, BATCH:BATCH + 1], P,
                                      bass.bass_isa.ReduceOp.max).then_inc(many_ok, 1)
            pool.wait_ge(many_ok, 3)
            pool.tensor_copy(keys_flag[:], many[:, BATCH + 1:BATCH + 2]).then_inc(keys_flag_ok, 1)
            load_stage(3, ctxT[1])
            load_stage(STAGE_V, wv[0])
            normalise(0)
            pool.wait_ge(hidden_ok, HALVES * F1)
            pool.dma_start(few_ctx[1][:].rearrange("p (c n) -> p c n", c=C),
                           ctxT[1].rearrange("p (c n) -> p c n", c=C)[:, :, N - P:]).then_inc(few_dma, 16)
            for h in range(HALVES):
                load_stage(h * GROUPS + (STAGE_V + 1), wv[1])
                load_stage(h * GROUPS + (STAGE_V + 2), wv[2])
                normalise(1 + h)
                with pool.Fori(2, GROUPS) as i:
                    load_stage(i + (h * GROUPS + STAGE_V + 1), wv[i + 1])
                if h == 0:
                    pool.wait_ge(top_ok, 1)
                    pool.partition_all_reduce(piece_all[:, 1:2], piece_all[:, 0:1], P, bass.bass_isa.ReduceOp.max).then_inc(all_ok, 1)
                    pool.wait_ge(all_ok, 1)
                    pool.tensor_copy(low_flag[:], piece_all[:, 1:2]).then_inc(flag_ok, 1)
            def add_scaled(p, t):
                pool.wait_ge(acc_read, p * TT + t + 1)
                x = resid[:, (p % 2) * TT + t, :]
                pool.tensor_tensor(x, normed[:, t, :], x, ALU.add).then_inc(acc_sum, 1)

            normalise(3)
            for t in range(TT):
                add_scaled(4, t)
            normalise(4)
            for t in range(TT):
                pool.wait_ge(part_ok, t + 1)
                pool.dma_start(out[0, t], resid[:, t, :]).then_inc(out_dma, 16)
            for t in range(TT - 1):
                add_scaled(5, t)
            for t in range(TT):
                pool.wait_ge(last_moments, t + 1)
                inverse_root(scale[:, t:t + 1], moments[:, t, 1:2], LN_EPS).then_inc(last_scale, 1)
            pool.wait_ge(out_dma, TT * 16)

        @block.tensor
        def _(pe):
            def passes(out_ap, w_hi, w_lo, x_hi, x_lo, start, stop):
                products = [(w_hi, x_hi)] + [(w_hi, x_lo)] * (x_lo is not None) + [(w_lo, x_hi)] * (w_lo is not None)
                for k, (w, x) in enumerate(products):
                    mm = pe.matmul(out_ap, w, x, start=start and k == 0, stop=stop and k == len(products) - 1,
                                   skip_group_check=True)
                return mm

            def project(bank_, par, which, half, x_hi=feat_hi, x_lo=feat_lo, low=True):
                for c in range(C):
                    mm = passes(bank_[:], a_hi[par][:, which, c, :], a_lo[par][:, which, c, :] if low else None,
                                x_hi[half][:, c, :], x_lo[half][:, c, :], c == 0, c == C - 1)
                return mm

            def down(m, par, part, first=False, last=False, low=True, tiles=range(TT)):
                pe.wait_ge(b_lo_ok, m + 1)
                pe.wait_ge(tile_lo_ok, m + 1)
                for t in tiles:
                    if first and part > 0:
                        pe.wait_ge(acc_read, (part - 1) * TT + t + 1)
                    rows = slice(t * P, (t + 1) * P)
                    mm = passes(acc[t][:], tile_hi[par][:, rows], tile_lo[par][:, rows], b_hi[par][:],
                                b_lo[par][:] if low else None,
                                first, last)
                    if last and t < TT - 1:
                        mm.then_inc(acc_full, 1)
                if tiles[-1] == TT - 1:
                    mm.then_inc(b_used, 1)

            def transposes(p, c, bank_, src):
                pe.wait_ge(operand_ok, (p + 1) * TT)
                for t in range(TT):
                    mm = pe.transpose(bank_[:, t * P:(t + 1) * P], src[:, t, c * P:(c + 1) * P], ident[:])
                mm.then_inc(feat_mm, 1)

            def values(bank_, b, half, few):
                cols = slice(N - P, N) if few else slice(b, N, HB)
                for c in range(C):
                    mm = passes(bank_[:], ctx_hi[half][:, c, cols], ctx_lo[half][:, c, cols],
                                wv_hi[:, c, :], wv_lo[:, c, :], c == 0, c == C - 1)
                mm.then_inc(v_mm, 1)

            def gate(a, par, half, done, low=True):
                pe.wait_ge(a_lo_ok, a + 2)
                pe.wait_ge(silu_ok, done)
                project(bank[0], par, 0, half, low=low).then_inc(first_mm, 1)

            def up(par, half, done, low=True):
                pe.wait_ge(hidden_ok, done)
                project(bank[1], par, 1, half, low=low).then_inc(a_used, 1)

            pe.wait_ge(ident_ok, 1)

            for h in range(HALVES):
                a0, t0, s0 = h * A1, h * T1, h * F1

                def step1(f, sf):
                    gate(f + (a0 + 1), (a0 + 1 + sf) % 2, h, f + s0)
                    up((a0 + 1 + sf) % 2, h, f + s0)
                    down(f + (t0 + POLY - 1), (t0 + POLY - 1 + sf) % 2, h)

                if h == 0:
                    pe.wait_ge(a_lo_ok, 1)
                    for c in range(C):
                        pe.wait_ge(stage_lo_ok, c + 1)
                        mm = passes(bank[0][:], a_hi[0][:, 0, c, :], a_lo[0][:, 0, c, :],
                                    feat_hi[0][:, c, :], feat_lo[0][:, c, :], c == 0, c == C - 1)
                    mm.then_inc(first_mm, 1)
                    pe.wait_ge(a_lo_ok, 2)
                else:
                    pe.wait_ge(a_lo_ok, a0 + 2)
                    pe.wait_ge(stage_lo_ok, staged(1))
                    pe.wait_ge(silu_ok, s0)
                    project(bank[0], a0 % 2, 0, h).then_inc(first_mm, 1)
                    pe.wait_ge(hidden_ok, s0)
                project(bank[1], a0 % 2, 1, h).then_inc(a_used, 1)
                if h > 0:
                    down(t0 - 1, (t0 - 1) % 2, h - 1, last=True)
                pe.wait_ge(a_lo_ok, a0 + 3)
                pe.wait_ge(poly_ok, h * POLY_STEPS + 1)
                project(bank[0], (a0 + 1) % 2, 0, h).then_inc(first_mm, 1)
                pe.wait_ge(poly_ok, h * POLY_STEPS + 4)
                pe.wait_ge(tile_lo_ok, t0 + 1)
                project(bank[1], (a0 + 1) % 2, 1, h).then_inc(a_used, 1)
                for m in range(POLY):
                    down(t0 + m, (t0 + m) % 2, h, first=(m == 0))
                for f in range(1, PEEL1):
                    step1(f, f)
                with pe.Fori(0, LOOP1) as i:
                    for j in range(2):
                        step1(i * 2 + (PEEL1 + j), PEEL1 + j)
                if h == 0:
                    step1(F1 - 1, F1 - 1)

            f, a, h = F1 - 1, 2 * A1 - 1, 1
            transposes(0, 0, bank[2], normed)
            gate(a, a % 2, h, s0 + f)
            transposes(0, 1, bank[3], normed)
            up(a % 2, h, s0 + f)
            pe.wait_ge(feat_lo_ok, 1)
            transposes(0, 2, bank[2], normed)
            down(TX0 - 2, (TX0 - 2) % 2, h)
            pe.wait_ge(feat_lo_ok, 2)
            transposes(0, 3, bank[3], normed)

            def attention(few):
                if few:
                    pe.wait_ge(few_dma, HALVES * 16)
                pe.wait_ge(stage_lo_ok, staged(STAGE_V))
                for b in range(HB):
                    pe.wait_ge(feat_lo_ok, C - 1 + b % 2)
                    if few and b >= 2:
                        pe.wait_ge(v_mm, b)
                        pe.sem_inc(v_mm, 1)
                        continue
                    if b >= 2:
                        pe.wait_ge(v_ok, b - 1)
                    values(bank[2 + b % 2], b, 0, few)

                def head(g, j, gpar, half, next_half, behind=2, feature_part=None, features_done=0,
                         part=2, out_first=False, out_last=False):
                    n, apar = g * GH + j, (AX0 + j) % 2
                    pe.wait_ge(a_lo_ok, n + (AX0 + 2))
                    if behind >= 1:
                        pe.wait_ge(biased_ok, n)
                    else:
                        pe.wait_ge(silu_ok, HALVES * F1)
                    project(bank[0], apar, 0, half).then_inc(first_mm, 1)
                    if behind >= 2:
                        pe.wait_ge(tile_lo_ok, n + (TX0 - 1))
                    elif behind == 1:
                        pe.wait_ge(k_ok, n)
                    else:
                        pe.wait_ge(hidden_ok, HALVES * F1)
                    if few:
                        for c in range(C):
                            mm = pe.matmul(bank[1][:, N - P:], a_raw[apar][:, (C + c) * P:(C + c + 1) * P],
                                           few_ctx[half][:, c * P:(c + 1) * P], start=(c == 0), stop=(c == C - 1))
                        mm.then_inc(a_used, 1)
                    else:
                        project(bank[1], apar, 1, half, ctx_hi, ctx_lo).then_inc(a_used, 1)
                    if behind == 0:
                        down(TX0 - 1, (TX0 - 1) % 2, 1, last=True)
                    if behind >= 1:
                        if features_done:
                            pe.wait_ge(feat_lo_ok, features_done)
                        turn_probs(n, bank[2], behind)
                    if next_half is not None:
                        if not few:
                            pe.wait_ge(stage_lo_ok, g + staged(STAGE_V + 1))
                        pe.wait_ge(v_ok, n + HB)
                        if few and j > 0:
                            pe.wait_ge(v_mm, n + HB)
                            pe.sem_inc(v_mm, 1)
                        elif not few:
                            values(bank[3], j, next_half, few)
                    if behind >= 2:
                        down(n + (TX0 - 2), (TX0 + j) % 2, part, first=out_first, last=out_last, tiles=range(TT // 2))
                    pe.wait_ge(q_ok, n + 1)
                    pe.wait_ge(k_ok, n + 1)
                    for b in range(HB):
                        keys = slice((b + 1) * SEQ - (FEW if few else SEQ), (b + 1) * SEQ)
                        mm = pe.matmul(bank[0][:, keys], q_sb[:, b * SEQ:(b + 1) * SEQ], k_sb[:, keys], start=True, stop=True)
                    mm.then_inc(score_mm, 1)
                    if behind >= 1:
                        weigh_values(n, j, gpar, bank[1])
                    if feature_part is not None:
                        transposes(feature_part, j, bank[2], normed if feature_part < 2 else resid[:, 0:TT, :])
                    if behind >= 2:
                        down(n + (TX0 - 2), (TX0 + j) % 2, part, first=out_first, last=out_last, tiles=range(TT // 2, TT))
                    if few and j == 0 and next_half is not None:
                        pe.wait_ge(stage_lo_ok, g + staged(STAGE_V + 1))
                        values(bank[3], j, next_half, few)

                def turn_probs(n, bank_, behind=2):
                    pe.wait_ge(prob_ok, n)
                    if behind >= 2:
                        pe.wait_ge(prob_t_ok, n - 1)
                    else:
                        pe.wait_ge(v_ok, HB)
                    if few:
                        mm = pe.transpose(bank_[:, 0:P], prob[:, N - P:], ident[:])
                    else:
                        for b in range(HB):
                            mm = pe.transpose(bank_[:, b * SEQ:(b + 1) * SEQ], prob[:, b:N:HB], ident[:])
                    mm.then_inc(prob_t_mm, 1)

                def weigh_values(n, j, gpar, bank_):
                    pe.wait_ge(prob_t_ok, n)
                    pe.wait_ge(v_ok, n + ((HB - j) if j else 0))
                    vpar, hh = (gpar, j - 1) if j else (1 - gpar, GH - 1)
                    for b in range(HB):
                        turned = prob_t[:, 0:SEQ] if few else prob_t[:, b * SEQ:(b + 1) * SEQ]
                        mm = pe.matmul(bank_[:, b * SEQ:(b + 1) * SEQ], v_sb[vpar][:, b, hh * P:(hh + 1) * P], turned,
                                       start=True, stop=True)
                    mm.then_inc(pv_mm, 1)

                pe.wait_ge(feat_lo_ok, C)
                for j in range(GH):
                    head(0, j, 0, 0, 0, behind=min(j, 2), out_first=(j == 2))
                with pe.Fori(0, (GROUPS - 2) // 2) as i:
                    for e in (1, 2):
                        for j in range(GH):
                            head(i * 2 + e, j, e % 2, 0, 0)
                for j in range(GH):
                    head(GROUPS - 1, j, 1, 0, 1, feature_part=1, features_done=C + j)
                pe.wait_ge(feat_lo_ok, 2 * C)
                for j in range(GH):
                    head(GROUPS, j, 0, 1, 1, part=2 + (j >= 2), out_first=(j == 2), out_last=(j == 1),
                         features_done=2 * C if j == 0 else 0)
                with pe.Fori(0, (GROUPS - 2) // 2) as i:
                    for e in (1, 2):
                        for j in range(GH):
                            head(i * 2 + (GROUPS + e), j, e % 2, 1, 1, part=3)
                for j in range(GH):
                    head(2 * GROUPS - 1, j, 1, 1, None, part=3, feature_part=2, features_done=2 * C + j)

                pe.wait_ge(feat_lo_ok, 3 * C)
                pe.wait_ge(biased_ok, HN)
                gate(A30, A30 % 2, 0, HALVES * F1)
                turn_probs(HN, bank[2])
                pe.wait_ge(tile_lo_ok, T30 - 1)
                up(A30 % 2, 0, HALVES * F1)
                weigh_values(HN, 0, 0, bank[3])
                down(T30 - 2, T30 % 2, 3)

            pe.wait_ge(keys_flag_ok, 1)
            many_keys = pe.value_load(keys_flag[0:1, 0:1], min_val=0, max_val=1)
            with pe.If(many_keys > 0):
                attention(False)
            with pe.Else():
                attention(True)

            def last_block(low):
                def step3(f, sf, h, first=False):
                    a, t, done = f + (A30 + h * F3), f + (T30 + h * F3 - 1), f + (HALVES * F1 + h * F3)
                    gate(a, (A30 + h * F3 + sf) % 2, h, done, low=low)
                    up((A30 + h * F3 + sf) % 2, h, done, low=low)
                    down(t, (T30 + h * F3 - 1 + sf) % 2, 4 + h, first=first, low=low)

                s0 = HALVES * F1
                gate(A30 + 1, (A30 + 1) % 2, 0, s0 + 1, low=low)
                down(T30 - 1, (T30 - 1) % 2, 3, last=True)
                up((A30 + 1) % 2, 0, s0 + 1, low=low)
                gate(A30 + 2, A30 % 2, 0, s0 + 2, low=low)
                down(T30, T30 % 2, 4, first=True, low=low)
                up(A30 % 2, 0, s0 + 2, low=low)
                down(T30 + 1, (T30 + 1) % 2, 4, low=low)
                for f in range(3, PEEL3):
                    step3(f, f, 0)
                with pe.Fori(0, LOOP3) as i:
                    for j in range(2):
                        step3(i * 2 + (PEEL3 + j), PEEL3 + j, 0)
                f, a = F3 - 1, A30 + F3 - 1
                x1 = resid[:, TT:2 * TT, :]
                transposes(3, 0, bank[2], x1)
                transposes(3, 1, bank[3], x1)
                gate(a, a % 2, 0, s0 + f, low=low)
                pe.wait_ge(feat_lo_ok, 3 * C + 1)
                transposes(3, 2, bank[2], x1)
                pe.wait_ge(feat_lo_ok, 3 * C + 2)
                transposes(3, 3, bank[3], x1)
                up(a % 2, 0, s0 + f, low=low)
                down(T30 + f - 1, (T30 + f - 1) % 2, 4, low=low)

                pe.wait_ge(feat_lo_ok, 4 * C)
                a, t = A30 + F3, T30 + F3
                gate(a, a % 2, 1, s0 + F3, low=low)
                up(a % 2, 1, s0 + F3, low=low)
                down(t - 1, (t - 1) % 2, 4, last=True, low=low)
                for f in range(1, PEEL3):
                    step3(f, f, 1, first=(f == 1))
                with pe.Fori(0, LOOP3) as i:
                    for j in range(2):
                        step3(i * 2 + (PEEL3 + j), PEEL3 + j, 1)
                step3(F3 - 1, F3 - 1, 1)
                down(LAST_T, LAST_T % 2, 5, last=True, low=low)

            pe.wait_ge(flag_ok, 1)
            has_low = pe.value_load(low_flag[0:1, 0:1], min_val=0, max_val=LOW_BITS)
            with pe.If(has_low > 0):
                last_block(True)
            with pe.Else():
                last_block(False)

        @block.scalar
        def _(act):
            act.dma_start(stage[:, 0:N], xT[0][:, 0:N]).then_inc(chunk_dma[0], 16)

            act.wait_ge(table_in_ok, 1)
            act.activation(table_out[:], table_in[:], ACT.Exp)

            def split_a(n, par):
                act.wait_ge(a_dma[par], n * 8 + (16 - 8 * par))
                if not isinstance(n, int) or n >= 2:
                    act.wait_ge(a_used, n - 1)
                act.activation(a_hi[par][:].rearrange("p w c k -> p (w c k)"), a_raw[par][:], ACT.Copy).then_inc(a_hi_ok, 1)

            def split_b(m, par):
                act.wait_ge(b_dma[par], m * 8 + (16 - 8 * par))
                if not isinstance(m, int) or m >= 2:
                    act.wait_ge(b_used, m - 1)
                act.activation(b_hi[par][:], b_raw[par][:], ACT.Copy).then_inc(b_hi_ok, 1)

            def split_stage(k, hi):
                act.wait_ge(stage_dma, k * 16)
                act.activation(hi[:].rearrange("p c n -> p (c n)"), stage[:], ACT.Copy).then_inc(stage_hi_ok, 1)

            def tile_from(m, par, src):
                if not isinstance(m, int) or m >= 2:
                    act.wait_ge(b_used, m - 1)
                act.activation(tile_hi[par][:], src, ACT.Copy).then_inc(tile_hi_ok, 1)

            def silu(a, done, last_block, f):
                act.wait_ge(first_mm, a + 1)
                act.wait_ge(hidden_ok, done)
                if last_block:
                    act.activation(gated[:], bank[0][:], ACT.Silu, scale=const[:, bass.ds(f + COL_AG, 1)]).then_inc(silu_ok, 1)
                else:
                    act.activation(gated[:], bank[0][:], ACT.Silu).then_inc(silu_ok, 1)

            def feed(a, apar, m, mpar, done, last_block=False, f=0, split_next=True, between=None):
                silu(a, done, last_block, f)
                if split_next:
                    split_a(a + 1, 1 - apar)
                if between is not None:
                    between()
                split_b(m, mpar)
                act.wait_ge(hidden_ok, done + 1)
                tile_from(m, mpar, hidden[mpar])

            def chunk(p, c, bank_):
                act.wait_ge(feat_mm, p * C + c + 1)
                if p < 2:
                    act.activation(feat_hi[p % 2][:, c, :], bank_[:], ACT.Copy,
                                   scale=const[:, COL_LNW + c:COL_LNW + c + 1]).then_inc(feat_hi_ok, 1)
                else:
                    act.activation(feat_hi[p % 2][:, c, :], bank_[:], ACT.Copy).then_inc(feat_hi_ok, 1)

            def copy_values(count, bank_, vpar, b):
                act.wait_ge(v_mm, count)
                act.activation(v_sb[vpar][:, b, :], bank_[:], ACT.Copy, scale=value_rows[:, b:b + 1]).then_inc(v_ok, 1)

            def split_half_a(which):
                act.activation(a_hi[0][:, which].rearrange("p c k -> p (c k)"), a_raw[0][:, which * C * P:(which + 1) * C * P],
                               ACT.Copy).then_inc(a_hi_ok, 1)

            act.wait_ge(gate_dma, 16)
            split_half_a(0)
            for c in range(C):
                act.wait_ge(chunk_dma[c], 16)
                act.activation(feat_hi[0][:, c, :], stage[:, c * N:(c + 1) * N], ACT.Copy).then_inc(stage_hi_ok, 1)
            act.wait_ge(a_dma[0], 16)
            split_half_a(1)
            act.wait_ge(const_dma, 16)
            act.wait_ge(ratio_in, 1)
            act.activation(ratio[:], ratio_log[:], ACT.Exp).then_inc(ratio_ok, 1)

            for h in range(HALVES):
                a0, t0, s0 = h * A1, h * T1, h * F1

                def step1(f, sf, between=None):
                    feed(f + (a0 + 1), (a0 + 1 + sf) % 2, f + (t0 + POLY), (t0 + POLY + sf) % 2, f + s0, between=between)

                split_a(a0 + 1, (a0 + 1) % 2)
                if h == 0:
                    act.activation(table_out[:], table_in[:], ACT.Silu)
                act.wait_ge(a_used, a0 + 1)
                tile_from(t0, t0 % 2, bank[1][:])
                split_b(t0, t0 % 2)
                for m in range(1, POLY):
                    split_b(t0 + m, (t0 + m) % 2)
                    act.wait_ge(poly_ok, h * POLY_STEPS + 3 + m)
                    tile_from(t0 + m, (t0 + m) % 2, hidden[(t0 + m) % 2])
                    if m == 1:
                        silu(a0 + 1, s0, False, 0)
                        split_a(a0 + 2, a0 % 2)
                split_b(t0 + POLY, (t0 + POLY) % 2)
                act.wait_ge(hidden_ok, s0 + 1)
                tile_from(t0 + POLY, (t0 + POLY) % 2, hidden[(t0 + POLY) % 2])
                step1(1, 1, between=lambda: split_stage(1 if h == 0 else STAGE_V, feat_hi[1] if h == 0 else wv_hi))
                step1(2, 2, between=(lambda: split_stage(2, ctx_hi[0])) if h == 0 else None)
                with act.Fori(0, LOOP1) as i:
                    for j in range(2):
                        step1(i * 2 + (PEEL1 + j), PEEL1 + j)
                if h == 0:
                    step1(F1 - 1, F1 - 1, between=lambda: split_stage(3, ctx_hi[1]))
            a, m, done = 2 * A1 - 1, TX0 - 1, HALVES * F1 - 1
            chunk(0, 0, bank[2])
            silu(a, done, False, 0)
            chunk(0, 1, bank[3])
            split_a(a + 1, (a + 1) % 2)
            chunk(0, 2, bank[2])
            split_b(m, m % 2)
            act.wait_ge(hidden_ok, done + 1)
            tile_from(m, m % 2, hidden[m % 2])
            chunk(0, 3, bank[3])
            act.wait_ge(value_rows_ok, 1)
            for b in range(HB):
                copy_values(b + 1, bank[2 + b % 2], 0, b)

            def head(g, j, gpar, behind=2, feature_part=None, has_values=True):
                n = g * GH + j
                wv_flat = wv_hi[:].rearrange("p c n -> p (c n)")
                if j == 0 and has_values:
                    act.wait_ge(v_mm, n + HB)
                    act.wait_ge(stage_dma, g * 16 + 16 * (STAGE_V + 1))
                    act.activation(wv_flat[:, 0:WV_CUT], stage[:, 0:WV_CUT], ACT.Copy).then_inc(wv_cut_ok, 1)
                else:
                    split_a(n + (AX0 + 1), (AX0 + j + 1) % 2)
                act.wait_ge(first_mm, n + (AX0 + 1))
                if behind >= 1:
                    act.wait_ge(score_mm, n)
                act.activation(q_sb[:], bank[0][:], ACT.Copy).then_inc(q_ok, 1)
                act.wait_ge(a_used, n + (AX0 + 1))
                act.activation(k_sb[:].rearrange("p (b k) -> p b k", b=HB),
                               bank[1][:].rearrange("p (k b) -> p b k", b=HB), ACT.Copy).then_inc(k_ok, 1)
                if behind >= 1:
                    split_b(n + (TX0 - 1), (TX0 + j - 1) % 2)
                if behind >= 1:
                    copy_probs(n, behind)
                if j == 0 and has_values:
                    act.activation(wv_flat[:, WV_CUT:], stage[:, WV_CUT:], ACT.Copy).then_inc(stage_hi_ok, 1)
                    split_a(n + (AX0 + 1), (AX0 + j + 1) % 2)
                if behind >= 1:
                    act.wait_ge(pv_mm, n)
                    tile_from(n + (TX0 - 1), (TX0 + j - 1) % 2, bank[1][:])
                if feature_part is not None:
                    chunk(feature_part, j, bank[2])
                exponentials(n)
                if has_values:
                    copy_values(n + (HB + 1), bank[3], 1 - gpar, j)

            def copy_probs(n, behind=2):
                act.wait_ge(prob_t_mm, n)
                if behind >= 2:
                    act.wait_ge(pv_mm, n - 1)
                act.activation(prob_t[:], bank[2][:], ACT.Copy).then_inc(prob_t_ok, 1)

            def exponentials(n):
                act.wait_ge(neg_max_ok, n + 1)
                if not isinstance(n, int) or n >= 1:
                    act.wait_ge(prob_t_mm, n)
                for b in range(HB):
                    e = act.activation(prob[:, b:N:HB], score[:, b, :], ACT.Exp, bias=neg_max[:, b:b + 1],
                                       accum_out=row_sum[:, b:b + 1])
                e.then_inc(exp_ok, 1)

            for j in range(GH):
                head(0, j, 0, behind=min(j, 2))
            with act.Fori(0, (GROUPS - 2) // 2) as i:
                for e in (1, 2):
                    for j in range(GH):
                        head(i * 2 + e, j, e % 2)
            for j in range(GH):
                head(GROUPS - 1, j, 1, feature_part=1)
            for j in range(GH):
                head(GROUPS, j, 0)
            with act.Fori(0, (GROUPS - 2) // 2) as i:
                for e in (1, 2):
                    for j in range(GH):
                        head(i * 2 + (GROUPS + e), j, e % 2)
            for j in range(GH):
                head(2 * GROUPS - 1, j, 1, feature_part=2, has_values=False)

            s0 = HALVES * F1

            def step3(f, sf, h, split_next=True):
                feed(f + (A30 + h * F3), (A30 + h * F3 + sf) % 2, f + (T30 + h * F3), (T30 + h * F3 + sf) % 2,
                     f + (s0 + h * F3), last_block=True, f=f, split_next=split_next)

            silu(A30, s0, True, 0)
            split_a(A30 + 1, (A30 + 1) % 2)
            copy_probs(HN)
            split_b(T30 - 1, (T30 - 1) % 2)
            act.wait_ge(pv_mm, HN)
            tile_from(T30 - 1, (T30 - 1) % 2, bank[3][:])
            split_b(T30, T30 % 2)
            act.wait_ge(hidden_ok, s0 + 1)
            tile_from(T30, T30 % 2, hidden[T30 % 2])
            step3(1, 1, 0)
            step3(2, 2, 0)
            for f in range(3, PEEL3):
                step3(f, f, 0)
            with act.Fori(0, LOOP3) as i:
                for j in range(2):
                    step3(i * 2 + (PEEL3 + j), PEEL3 + j, 0)
            a, m, f = A30 + F3 - 1, T30 + F3 - 1, F3 - 1
            chunk(3, 0, bank[2])
            chunk(3, 1, bank[3])
            split_a(a + 1, (a + 1) % 2)
            silu(a, s0 + f, True, f)
            chunk(3, 2, bank[2])
            chunk(3, 3, bank[3])
            split_b(m, m % 2)
            act.wait_ge(hidden_ok, s0 + f + 1)
            tile_from(m, m % 2, hidden[m % 2])
            step3(0, 0, 1)
            step3(1, 1, 1)
            for f in range(2, PEEL3):
                step3(f, f, 1)
            with act.Fori(0, LOOP3) as i:
                for j in range(2):
                    step3(i * 2 + (PEEL3 + j), PEEL3 + j, 1)
            step3(F3 - 1, F3 - 1, 1, split_next=False)
            for t in range(TT - 1):
                act.wait_ge(last_offset, t + 1)
                x = resid[:, TT + t, :]
                act.activation(x, x, ACT.Identity, scale=scale[:, t:t + 1], bias=neg_mean[:, t:t + 1]).then_inc(last_act_ok, 1)
            act.wait_ge(last_ok, 1)
            act.dma_start(out[1, TT - 1][P // 2:], resid[P // 2:, 2 * TT - 1, :]).then_inc(last_out_dma, 16)

        @block.vector
        def _(dve):
            def low(out_ap, whole, high):
                return dve.tensor_tensor(out_ap, whole, high, ALU.subtract)

            def split_a(n, par):
                dve.wait_ge(a_hi_ok, n + 2)
                low(a_lo[par][:].rearrange("p w c k -> p (w c k)"), a_raw[par][:],
                    a_hi[par][:].rearrange("p w c k -> p (w c k)").bitcast(F32)).then_inc(a_lo_ok, 1)

            def split_b(m, par):
                dve.wait_ge(b_hi_ok, m + 1)
                low(b_lo[par][:], b_raw[par][:], b_hi[par][:].bitcast(F32)).then_inc(b_lo_ok, 1)

            def split_stage(k, hi, lo):
                dve.wait_ge(stage_hi_ok, k + C)
                low(lo[:].rearrange("p c n -> p (c n)"), stage[:],
                    hi[:].rearrange("p c n -> p (c n)").bitcast(F32)).then_inc(stage_lo_ok, 1)

            def tile_rest(m, par, src):
                dve.wait_ge(tile_hi_ok, m + 1)
                low(tile_lo[par][:], src, tile_hi[par][:].bitcast(F32)).then_inc(tile_lo_ok, 1)

            def product(a, done, m, mpar, last_block, f):
                dve.wait_ge(silu_ok, done + 1)
                dve.wait_ge(a_used, a + 1)
                dve.wait_ge(tile_lo_ok, m - 1)
                if last_block:
                    dve.scalar_tensor_tensor(out=hidden[mpar], in0=bank[1][:], scalar=const[:, bass.ds(f + COL_AU, 1)],
                                             in1=gated[:], op0=ALU.mult, op1=ALU.mult).then_inc(hidden_ok, 1)
                else:
                    dve.tensor_tensor(hidden[mpar], bank[1][:], gated[:], ALU.mult).then_inc(hidden_ok, 1)

            def feed(a, apar, m, mpar, done, last_block=False, f=0, split_next=True, before=None, after=None):
                if split_next:
                    split_a(a + 1, 1 - apar)
                if before is not None:
                    before()
                product(a, done, m, mpar, last_block, f)
                if after is not None:
                    after()
                split_b(m, mpar)
                dve.wait_ge(hidden_ok, done + 1)
                tile_rest(m, mpar, hidden[mpar])

            def chunk(p, c, bank_):
                dve.wait_ge(feat_hi_ok, p * C + c + 1)
                high = feat_hi[p % 2][:, c, :].bitcast(F32)
                if p < 2:
                    dve.scalar_tensor_tensor(out=feat_lo[p % 2][:, c, :], in0=bank_[:], scalar=const[:, COL_LNW + c:COL_LNW + c + 1],
                                             in1=high, op0=ALU.mult, op1=ALU.subtract).then_inc(feat_lo_ok, 1)
                else:
                    low(feat_lo[p % 2][:, c, :], bank_[:], high).then_inc(feat_lo_ok, 1)

            steps = [0]

            def step(ins):
                steps[0] += 1
                ins.then_inc(ln_step, 1)

            def after_steps():
                dve.wait_ge(ln_step, steps[0])

            def residual(p):
                for t in range(TT):
                    if t < TT - 1:
                        dve.wait_ge(acc_full, p * (TT - 1) + t + 1)
                    else:
                        dve.wait_ge(b_used, PART_END[p] + 1)
                    x = resid[:, (p % 2) * TT + t, :]
                    if p < 2:
                        dve.tensor_tensor(x, acc[t][:], x, ALU.add).then_inc(acc_read, 1)
                    elif p < 4:
                        dve.scalar_tensor_tensor(out=x, in0=x, scalar=2.0, in1=acc[t][:], op0=ALU.mult, op1=ALU.add).then_inc(acc_read, 1)
                    else:
                        dve.tensor_tensor(normed[:, t, :], acc[t][:], ad_sb[:], ALU.mult).then_inc(acc_read, 1)

            def take_moments(p):
                for t in range(TT):
                    step(dve.bn_stats(stats[:, t, :], resid[:, (p % 2) * TT + t, :]))
                after_steps()
                for t in range(TT):
                    step(dve.bn_aggr(moments[:, t, :], stats[:, t, :]))
                after_steps()

            def variances(p):
                if p < 4:
                    dve.wait_ge(acc_read, (p + 1) * TT)
                else:
                    dve.wait_ge(acc_sum, TT)
                take_moments(p)
                dve.sem_inc(moments_ok, 1)

            dve.memset(table_in[:], 0.0).then_inc(table_in_ok, 1)

            def split_half_a(which):
                dve.wait_ge(a_hi_ok, which + 1)
                low(a_lo[0][:, which].rearrange("p c k -> p (c k)"), a_raw[0][:, which * C * P:(which + 1) * C * P],
                    a_hi[0][:, which].rearrange("p c k -> p (c k)").bitcast(F32)).then_inc(a_lo_ok, 1)

            split_half_a(0)
            for c in range(C):
                dve.wait_ge(stage_hi_ok, c + 1)
                low(feat_lo[0][:, c, :], stage[:, c * N:(c + 1) * N], feat_hi[0][:, c, :].bitcast(F32)).then_inc(stage_lo_ok, 1)
            split_half_a(1)
            dve.wait_ge(const_dma, 16)
            dve.tensor_scalar(ratio_log[:, 0:1], const[:, COL_DISC:COL_DISC + 1], -1.0, None, ALU.mult)
            dve.tensor_tensor(ratio_log[:, 1:ORDERS], const[:, COL_DISC:COL_DISC + ORDERS - 1],
                              const[:, COL_DISC + 1:COL_DISC + ORDERS], ALU.subtract).then_inc(ratio_in, 1)

            for h in range(HALVES):
                a0, t0, s0, p0 = h * A1, h * T1, h * F1, h * POLY_STEPS

                def step1(f, sf, before=None, after=None):
                    feed(f + (a0 + 1), (a0 + 1 + sf) % 2, f + (t0 + POLY), (t0 + POLY + sf) % 2, f + s0,
                         before=before, after=after)

                split_a(a0 + 1, (a0 + 1) % 2)
                dve.wait_ge(first_mm, a0 + 1)
                dve.tensor_scalar(delta, bank[0][:], const[:, COL_POINT:COL_POINT + 1], None, ALU.subtract).then_inc(poly_ok, 1)
                dve.wait_ge(poly_ok, p0 + 1)
                dve.tensor_tensor(delta_kept, delta, delta, ALU.mult).then_inc(poly_ok, 1)
                dve.wait_ge(poly_ok, p0 + 2)
                dve.scalar_tensor_tensor(out=delta_kept, in0=delta_kept, scalar=THD ** 2, in1=delta,
                                         op0=ALU.is_le, op1=ALU.mult).then_inc(poly_ok, 1)
                if h == 0:
                    dve.wait_ge(ratio_ok, 1)
                dve.wait_ge(a_used, a0 + 1)
                if h > 0:
                    dve.wait_ge(tile_lo_ok, t0)
                tile_rest(t0, t0 % 2, bank[1][:])
                dve.scalar_tensor_tensor(out=hidden[(t0 + 1) % 2], in0=bank[1][:], scalar=ratio[:, 0:1], in1=delta,
                                         op0=ALU.mult, op1=ALU.mult).then_inc(poly_ok, 1)
                split_b(t0, t0 % 2)
                if h > 0:
                    residual(0)
                for m in range(1, POLY):
                    if m + 1 < POLY:
                        dve.wait_ge(poly_ok, p0 + 3 + m)
                        dve.wait_ge(tile_lo_ok, t0 + m)
                        dve.scalar_tensor_tensor(out=hidden[(t0 + m + 1) % 2], in0=hidden[(t0 + m) % 2],
                                                 scalar=ratio[:, m:m + 1], in1=(delta if m < KEEP_ORDER else delta_kept),
                                                 op0=ALU.mult, op1=ALU.mult).then_inc(poly_ok, 1)
                    split_b(t0 + m, (t0 + m) % 2)
                    tile_rest(t0 + m, (t0 + m) % 2, hidden[(t0 + m) % 2])
                    if m == 1:
                        split_a(a0 + 2, a0 % 2)
                product(a0 + 1, s0, t0 + POLY, (t0 + POLY) % 2, False, 0)
                split_b(t0 + POLY, (t0 + POLY) % 2)
                dve.wait_ge(hidden_ok, s0 + 1)
                tile_rest(t0 + POLY, (t0 + POLY) % 2, hidden[(t0 + POLY) % 2])
                if h == 0:
                    step1(1, 1, after=lambda: split_stage(1, feat_hi[1], feat_lo[1]))
                    step1(2, 2, after=lambda: split_stage(2, ctx_hi[0], ctx_lo[0]))
                    dve.wait_ge(mask_dma, 32)
                    dve.tensor_scalar(mask_add[:], mask_u8, 1.0, MASKED, ALU.subtract, ALU.mult).then_inc(mask_ok, 1)
                    dve.tensor_reduce(row_valid[:], mask_u8, AX_X, ALU.max).then_inc(mask_ok, 1)
                    dve.tensor_reduce(many[:, 0:BATCH], mask_u8[:, :, 0:SEQ - FEW], AX_X, ALU.max).then_inc(many_ok, 1)
                    dve.wait_ge(many_ok, 1)
                    dve.tensor_reduce(many[:, BATCH:BATCH + 1], many[:, 0:BATCH], AX_X, ALU.max).then_inc(many_ok, 1)
                    dve.wait_ge(resid_dma, 32)
                else:
                    step1(1, 1, before=lambda: variances(0), after=lambda: split_stage(STAGE_V, wv_hi, wv_lo))
                    step1(2, 2)
                with dve.Fori(0, LOOP1) as i:
                    for j in range(2):
                        step1(i * 2 + (PEEL1 + j), PEEL1 + j)
                if h == 0:
                    dve.wait_ge(ident_ok, 1)
                    dve.tensor_reduce(value_rows[:], ident[:].rearrange("p (k b) -> p b k", b=HB), AX_X,
                                      ALU.max).then_inc(rows_in, 1)
                    dve.wait_ge(rows_in, 1)
                    dve.wait_ge(many_ok, 3)
                    dve.tensor_scalar(value_rows[:], value_rows[:], many[:, BATCH + 1:BATCH + 2], None,
                                      ALU.max).then_inc(value_rows_ok, 1)
                    step1(F1 - 1, F1 - 1, after=lambda: split_stage(3, ctx_hi[1], ctx_lo[1]))
            a, m, done = 2 * A1 - 1, TX0 - 1, HALVES * F1 - 1
            chunk(0, 0, bank[2])
            chunk(0, 1, bank[3])
            split_a(a + 1, (a + 1) % 2)
            product(a, done, m, m % 2, False, 0)
            chunk(0, 2, bank[2])
            split_b(m, m % 2)
            dve.wait_ge(hidden_ok, done + 1)
            tile_rest(m, m % 2, hidden[m % 2])
            chunk(0, 3, bank[3])

            def head(g, j, gpar, half, behind=2, feature_part=None, has_next=True, past_half=None, before=None):
                n = g * GH + j
                if behind >= 1:
                    divide(n, half if past_half is None else past_half)
                if j == 0 and has_next:
                    high, rest = wv_hi[:].rearrange("p c n -> p (c n)").bitcast(F32), wv_lo[:].rearrange("p c n -> p (c n)")
                    dve.wait_ge(wv_cut_ok, g + 1)
                    low(rest[:, 0:WV_CUT], stage[:, 0:WV_CUT], high[:, 0:WV_CUT])
                    dve.wait_ge(stage_hi_ok, g + staged(STAGE_V + 1))
                    low(rest[:, WV_CUT:], stage[:, WV_CUT:], high[:, WV_CUT:]).then_inc(stage_lo_ok, 1)
                split_a(n + (AX0 + 1), (AX0 + j + 1) % 2)
                if before is not None:
                    before()
                dve.wait_ge(score_mm, n + 1)
                dve.wait_ge(bias_dma[gpar], g * 8 + (16 - 8 * gpar))
                dve.tensor_tensor(score[:], bank[0][:].rearrange("p (b k) -> p b k", b=HB),
                                  bias_sb[gpar][:, j * SEQ:(j + 1) * SEQ].unsqueeze(1).broadcast_to([P, HB, SEQ]),
                                  ALU.add).then_inc(biased_ok, 1)
                dve.wait_ge(mask_ok, 2)
                dve.wait_ge(biased_ok, n + 1)
                for b in range(HB):
                    ins = dve.tensor_tensor_reduce(score[:, b, :], score[:, b, :], mask_add[:, half * HB + b, :], 1.0, -3e38,
                                                   ALU.add, ALU.max, row_max[:, b:b + 1])
                ins.then_inc(masked_ok, 1)
                dve.wait_ge(masked_ok, n + 1)
                dve.tensor_scalar(neg_max[:], row_max[:], -1.0, None, ALU.mult).then_inc(neg_max_ok, 1)
                if behind >= 1:
                    split_b(n + (TX0 - 1), (TX0 + j - 1) % 2)
                    tile_rest(n + (TX0 - 1), (TX0 + j - 1) % 2, bank[1][:])
                if feature_part is not None:
                    chunk(feature_part, j, bank[2])

            def look_at(k, par):
                dve.wait_ge(piece_dma[par], k * 8 + (16 - 8 * par))
                dve.tensor_scalar(piece[par], piece[par], LOW_BITS, None, ALU.bitwise_and).then_inc(piece_bits, 1)
                dve.wait_ge(piece_bits, k + 1)
                dve.tensor_reduce(piece_top[:, bass.ds(k, 1)], piece[par], AX_X, ALU.max).then_inc(piece_free, 1)

            def divide(n, half):
                dve.wait_ge(exp_ok, n)
                dve.reciprocal(row_inv[:], row_sum[:]).then_inc(inv_ok, 1)
                dve.wait_ge(inv_ok, n * 2 - 1)
                dve.tensor_tensor(row_inv[:], row_inv[:], row_valid[:, half * HB:(half + 1) * HB], ALU.mult).then_inc(inv_ok, 1)
                dve.wait_ge(inv_ok, n * 2)
                by_key = prob[:].rearrange("p (k b) -> p k b", b=HB)
                dve.tensor_tensor(by_key, by_key, row_inv[:].unsqueeze(1).broadcast_to([P, SEQ, HB]), ALU.mult).then_inc(prob_ok, 1)

            dve.wait_ge(tile_lo_ok, TX0)
            dve.sem_inc(piece_free, 2)
            ends = {1: lambda: residual(1), 2: lambda: variances(1)}
            for j in range(GH):
                head(0, j, 0, 0, behind=min(j, 2), before=ends.get(j))
            with dve.Fori(0, (GROUPS - 2) // 2) as i:
                for e in (1, 2):
                    for j in range(GH):
                        head(i * 2 + e, j, e % 2, 0,
                             before=lambda: look_at(i * (2 * GH) + ((e - 1) * GH + j), j % 2))
            dve.wait_ge(piece_free, SCANS + 2)
            dve.tensor_reduce(piece_all[:, 0:1], piece_top[:], AX_X, ALU.max).then_inc(top_ok, 1)
            for j in range(GH):
                head(GROUPS - 1, j, 1, 0, feature_part=1)

            ends = {2: lambda: residual(2), 3: lambda: variances(2)}
            for j in range(GH):
                head(GROUPS, j, 0, 1, past_half=(0 if j == 0 else 1), before=ends.get(j))
            with dve.Fori(0, (GROUPS - 2) // 2) as i:
                for e in (1, 2):
                    for j in range(GH):
                        head(i * 2 + (GROUPS + e), j, e % 2, 1)
            for j in range(GH):
                head(2 * GROUPS - 1, j, 1, 1, feature_part=2, has_next=False)

            s0 = HALVES * F1

            def step3(f, sf, h, split_next=True, after=None):
                feed(f + (A30 + h * F3), (A30 + h * F3 + sf) % 2, f + (T30 + h * F3), (T30 + h * F3 + sf) % 2,
                     f + (s0 + h * F3), last_block=True, f=f, split_next=split_next, after=after)

            divide(HN, 1)
            split_a(A30 + 1, (A30 + 1) % 2)
            product(A30, s0, T30, T30 % 2, True, 0)
            split_b(T30 - 1, (T30 - 1) % 2)
            tile_rest(T30 - 1, (T30 - 1) % 2, bank[3][:])
            split_b(T30, T30 % 2)
            dve.wait_ge(hidden_ok, s0 + 1)
            tile_rest(T30, T30 % 2, hidden[T30 % 2])
            step3(1, 1, 0, after=lambda: residual(3))
            step3(2, 2, 0, after=lambda: variances(3))
            step3(3, 3, 0)
            with dve.Fori(0, LOOP3) as i:
                for j in range(2):
                    step3(i * 2 + (PEEL3 + j), PEEL3 + j, 0)
            a, m, f = A30 + F3 - 1, T30 + F3 - 1, F3 - 1
            chunk(3, 0, bank[2])
            chunk(3, 1, bank[3])
            split_a(a + 1, (a + 1) % 2)
            chunk(3, 2, bank[2])
            chunk(3, 3, bank[3])
            product(a, s0 + f, m, m % 2, True, f)
            split_b(m, m % 2)
            dve.wait_ge(hidden_ok, s0 + f + 1)
            tile_rest(m, m % 2, hidden[m % 2])
            step3(0, 0, 1, after=lambda: residual(4))
            step3(1, 1, 1, after=lambda: variances(4))
            step3(2, 2, 1)
            step3(3, 3, 1)
            with dve.Fori(0, LOOP3) as i:
                for j in range(2):
                    step3(i * 2 + (PEEL3 + j), PEEL3 + j, 1)
            step3(F3 - 1, F3 - 1, 1, split_next=False)

            last = TT - 1
            for t in range(TT):
                if t < last:
                    dve.wait_ge(acc_full, 5 * (TT - 1) + t + 1)
                else:
                    dve.wait_ge(b_used, LAST_T + 1)
                dve.tensor_tensor(normed[:, t, :], acc[t][:], ad_sb[:], ALU.mult).then_inc(acc_read, 1)
            x = resid[:, TT + last, :]
            dve.wait_ge(acc_read, 6 * TT)
            dve.tensor_tensor(x, normed[:, last, :], x, ALU.add).then_inc(last_sum, 1)

            def measured(t):
                if t < last:
                    dve.wait_ge(acc_sum, TT + t + 1)
                else:
                    dve.wait_ge(last_sum, 1)
                dve.bn_stats(stats[:, t, :], resid[:, TT + t, :]).then_inc(last_stats, 1)
                dve.wait_ge(last_stats, t + 1)
                dve.bn_aggr(moments[:, t, :], stats[:, t, :]).then_inc(last_moments, 1)

            def offset(t):
                dve.wait_ge(last_scale, t + 1)
                dve.scalar_tensor_tensor(out=neg_mean[:, t:t + 1], in0=moments[:, t, 0:1], scalar=-1.0,
                                         in1=scale[:, t:t + 1], op0=ALU.mult, op1=ALU.mult).then_inc(last_offset, 1)

            measured(0)
            for t in range(1, TT):
                measured(t)
                offset(t - 1)
            dve.wait_ge(last_scale, TT)
            dve.tensor_scalar(x, x, moments[:, last, 0:1], scale[:, last:TT], ALU.subtract, ALU.mult).then_inc(last_ok, 1)


def build(nc, arrays):
    aps = {name: nc.dram_tensor(name, a.shape, mybir.dt.from_np(a.dtype), kind="ExternalInput").ap()
           for name, a in arrays.items()}
    out = nc.dram_tensor("out", (HALVES, TT, P, D), F32, kind="ExternalOutput").ap()
    decoder_kernel(nc, out=out, **aps)


def kernel(**inputs):
    import numpy as np
    import concourse.bacc as bacc
    from concourse.bass_utils import run_bass_kernel_spmd

    g = {k: np.asarray(v) for k, v in inputs.items()}

    def feature_major(x):
        return x.reshape(HALVES, N, C, P).transpose(0, 3, 2, 1).reshape(HALVES, P, C * N)

    def in_maps(w, tiles):
        w = np.concatenate([w, np.zeros((tiles * P - w.shape[0], D), w.dtype)])
        return w.reshape(tiles, P, C, P).transpose(0, 3, 2, 1).reshape(tiles, P, C * P)

    def out_maps(w, tiles):
        w = np.concatenate([w.T, np.zeros((tiles * P - w.shape[1], D), w.dtype)])
        return w.reshape(tiles, P, D)

    def columns(v, tiles):
        v = np.concatenate([v, np.zeros(tiles * P - v.shape[0], v.dtype)])
        return v.reshape(tiles, P).T

    def pair(w0, w1, tiles):
        return np.concatenate([in_maps(w0, tiles), in_maps(w1, tiles)], axis=2)

    wv = g["L0_xattn_w_v"].reshape(GROUPS, GH * P, C, P).transpose(0, 3, 2, 1).reshape(GROUPS, P, C * GH * P)
    arrays = {
        "xT": feature_major(g["x"]),
        "ctxT": feature_major(g["ctx_4096"].reshape(HALVES, HB, SEQ, D).transpose(0, 2, 1, 3)),
        "x_tok": g["x"].reshape(HALVES, TT, P, D).transpose(0, 2, 1, 3),
        "mask": np.ascontiguousarray(g["mask_BxSxS2_bk0"].transpose(1, 0, 2)).view(np.uint32),
        "consts": np.concatenate([
            columns(g["L0_attn_local_point"], 1), columns(g["L0_xattn_ln_weight"], C),
            np.broadcast_to(g["L0_attn_discount_factor"], (P, ORDERS)),
            columns(g["L0_ffn_ag"], F3), columns(g["L0_ffn_au"], F3)], axis=1),
        "ad": np.broadcast_to(g["L0_ffn_ad"], (P, D)),
        "a1": np.concatenate([pair(g["L0_attn_gate_w"], g["L0_attn_up_w"], 1),
                              pair(g["L0_attn_ffn_gate_w"], g["L0_attn_ffn_up_w"], F1)]),
        "b1": np.concatenate([out_maps(g["L0_attn_local_approx_output"], 1)]
                             + [out_maps(g["L0_attn_fuse_weight"][:, :, m], 1) for m in range(ORDERS)]
                             + [out_maps(g["L0_attn_ffn_down_w"], F1)]),
        "ax": pair(g["L0_xattn_w_q"], g["L0_xattn_w_k"], HEADS),
        "bx": out_maps(g["L0_xattn_w_out"], HEADS),
        "wv": np.concatenate([wv, wv[:1]]),
        "bias": g["L0_xattn_position_bias"].reshape(GROUPS, GH, SEQ, SEQ).transpose(0, 2, 1, 3).reshape(GROUPS, P, GH * SEQ),
        "w3": np.concatenate([pair(g["L0_ffn_Wg"], g["L0_ffn_Wu"], F3), out_maps(g["L0_ffn_Wd"], F3)], axis=2),
    }
    arrays = {k: np.ascontiguousarray(v) for k, v in arrays.items()}
    nc = bacc.Bacc("TRN2", target_bir_lowering=False, num_devices=1)
    build(nc, arrays)
    r = run_bass_kernel_spmd(nc, [arrays], core_ids=[0])
    return r.results[0]["out"].reshape(BATCH, SEQ, D)
```
